# Optimizing a Trainium2 kernel written in Bass

```python
import numpy as np
import jax
import jax.numpy as jnp

def _softmax(x, axis=-1):
    return jax.nn.softmax(x, axis=axis)
def _gelu(x):
    return jax.nn.gelu(x, approximate=True)
def _silu(x):
    return jax.nn.silu(x)
def _sigmoid(x):
    return jax.nn.sigmoid(x)
def _layernorm(x, axis=-1, eps=1e-5):
    m = jnp.mean(x, axis=axis, keepdims=True)
    v = jnp.var(x, axis=axis, keepdims=True)
    return (x - m) / jnp.sqrt(v + eps)
def _scatter_add(tgt, idx, src, axis=0):
    return tgt.at[idx].add(src)
def _segment_sum(src, seg, n):
    return jax.ops.segment_sum(src, seg, n)

kernel_name = 'mk_adj_preln_d2_adj_256_49bf0c'

def setup_inputs(seed: int = 0):
    np.random.seed(seed)
    _w = jnp.asarray
    def _rec_inputs():
        import jax
        import jax.numpy as jnp
        _gk = jax.random.key(seed)
        x = -0.0005146 + 1 * jax.random.normal(jax.random.fold_in(_gk, 1), (8, 2048, 256), jnp.float32)
        _a = jax.random.bernoulli(jax.random.fold_in(_gk, 2), 0.015625, (8, 2048, 2048))
        adj = _a.astype(jnp.int32)
        return x, adj
    x, adj = _rec_inputs()
    def _L0_gnn_setup():
        import jax, jax.numpy as jnp
        import numpy as np
        B, N, C, OUT, S = (4, 2048, 256, 256, 25)
        DENSITY = 0.008
        key = jax.random.key(seed)
        kA, kX, kW = jax.random.split(key, 3)
        A = jax.random.bernoulli(kA, DENSITY, (B, N, N)).astype(jnp.int32)
        X = jax.random.normal(kX, (B, N, C), dtype=jnp.float32)
        W = jax.random.normal(kW, (2 * C, OUT), dtype=jnp.float32) * np.float32(1.0 / np.sqrt(2 * C))
        b = jnp.zeros((OUT,), dtype=jnp.float32)
        return {'A': A, 'X': X, 'W': W, 'b': b}
    _L0_gnn_all = _L0_gnn_setup()
    _L0_gnn_in = {k: v for k, v in _L0_gnn_all.items() if k in ('W', 'b', )}
    del _L0_gnn_all

    def _L1_gnn_setup():
        import jax, jax.numpy as jnp
        import numpy as np
        B, N, D = (8, 1024, 256)
        H, HO = (4, 64)
        T = 5
        NEG = -1000000000.0
        EPS = 1e-06
        key = jax.random.key(seed)
        ks = jax.random.split(key, 6)
        nodes_embed = jax.random.normal(ks[0], (B, N, D), dtype=jnp.float32)
        node_adj = jax.random.randint(ks[1], (B, N, N), 0, T + 1)
        W = jax.random.normal(ks[2], (H, D, HO), dtype=jnp.float32) * (1.0 / np.sqrt(D))
        a_src = jax.random.normal(ks[3], (H, T, HO), dtype=jnp.float32) * 0.1
        a_dst = jax.random.normal(ks[4], (H, T, HO), dtype=jnp.float32) * 0.1
        bias = jnp.zeros((H, HO), dtype=jnp.float32)
        ln_gamma = jnp.ones((H, HO), dtype=jnp.float32)
        ln_beta = jnp.zeros((H, HO), dtype=jnp.float32)
        return {'nodes_embed': nodes_embed, 'node_adj': node_adj, 'W': W, 'a_src': a_src, 'a_dst': a_dst, 'bias': bias, 'ln_gamma': ln_gamma, 'ln_beta': ln_beta}
    _L1_gnn_all = _L1_gnn_setup()
    _L1_gnn_in = {k: v for k, v in _L1_gnn_all.items() if k in ('W', 'a_src', 'a_dst', 'bias', 'ln_gamma', 'ln_beta', )}
    del _L1_gnn_all

    return {
        "x": x,
        "adj": adj,
        "L0_gnn_W": _L0_gnn_in["W"],
        "L0_gnn_b": _L0_gnn_in["b"],
        "L1_gnn_W": _L1_gnn_in["W"],
        "L1_gnn_a_src": _L1_gnn_in["a_src"],
        "L1_gnn_a_dst": _L1_gnn_in["a_dst"],
        "L1_gnn_bias": _L1_gnn_in["bias"],
        "L1_gnn_ln_gamma": _L1_gnn_in["ln_gamma"],
        "L1_gnn_ln_beta": _L1_gnn_in["ln_beta"],
    }

def reference(x, adj, L0_gnn_W, L0_gnn_b, L1_gnn_W, L1_gnn_a_src, L1_gnn_a_dst, L1_gnn_bias, L1_gnn_ln_gamma, L1_gnn_ln_beta):
    import jax
    import jax.numpy as jnp
    def _L0_gnn_ref(A, X, W, b):
        import jax, jax.numpy as jnp
        import numpy as np
        B, N, C, OUT, S = (4, 2048, 256, 256, 25)
        DENSITY = 0.008
        mask = A != 0
        neg_inf = jnp.float32(-jnp.inf)
        pri = -jnp.arange(N, dtype=jnp.float32)
        scores = jnp.where(mask, pri, neg_inf)
        vals, idx = jax.lax.top_k(scores, S)
        valid = vals > neg_inf
        feats = jax.vmap(lambda x, i: x[i])(X, idx)
        feats = jnp.where(valid[..., None], feats, neg_inf)
        agg = feats.max(axis=2)
        degree = mask.sum(axis=-1)
        agg = jnp.where((degree <= S)[..., None], jnp.maximum(agg, 0.0), agg)
        h = jnp.concatenate([X, agg], axis=-1)
        out = jax.nn.relu(jnp.einsum('bnf,fo->bno', h, W) + b)
        return out

    def _L1_gnn_ref(nodes_embed, node_adj, W, a_src, a_dst, bias, ln_gamma, ln_beta):
        import jax, jax.numpy as jnp
        import numpy as np
        B, N, D = (8, 1024, 256)
        H, HO = (4, 64)
        T = 5
        NEG = -1000000000.0
        EPS = 1e-06
        h = jnp.einsum('bnd,hde->bhne', nodes_embed, W)
        e_src = jnp.einsum('bhne,hte->bhtn', h, a_src)
        e_dst = jnp.einsum('bhne,hte->bhtn', h, a_dst)
        n_types = a_src.shape[1]
        weight = jnp.zeros(h.shape[:2] + (h.shape[2], h.shape[2]), dtype=h.dtype)
        for t in range(n_types):
            mask = (node_adj == t + 1).astype(h.dtype)[:, None]
            weight = weight + mask * (e_src[:, :, t, :, None] + e_dst[:, :, t, None, :])
        weight = jax.nn.leaky_relu(weight, negative_slope=0.01)
        weight = jnp.where(node_adj[:, None] == 0, NEG, weight)
        attention = jax.nn.softmax(weight, axis=-1)
        dst = jnp.einsum('bhij,bhje->bhie', attention, h) + bias[None, :, None, :]
        out = jax.nn.relu(dst) + h
        mu = out.mean(axis=-1, keepdims=True)
        var = out.var(axis=-1, keepdims=True)
        out = (out - mu) / jnp.sqrt(var + EPS) * ln_gamma[None, :, None, :] + ln_beta[None, :, None, :]
        b, hh, n, e = out.shape
        return out.transpose(0, 2, 1, 3).reshape(b, n, hh * e)

    h = jnp.maximum(_layernorm(x, axis=-1), 0.0)
    x = x + _L0_gnn_ref(adj, h, L0_gnn_W, L0_gnn_b)
    h = jnp.maximum(_layernorm(x, axis=-1), 0.0)
    x = x + _L1_gnn_ref(h, adj, L1_gnn_W, L1_gnn_a_src, L1_gnn_a_dst, L1_gnn_bias, L1_gnn_ln_gamma, L1_gnn_ln_beta)
    return x


_drawn_inputs = setup_inputs


def setup_inputs(seed=0):
    import zlib

    import numpy as np

    out = dict(_drawn_inputs(seed))
    spreads = {'L0_gnn_b': (0.0, 0.1),
     'L1_gnn_bias': (0.0, 0.1),
     'L1_gnn_ln_gamma': (1.0, 0.2),
     'L1_gnn_ln_beta': (0.0, 0.1)}
    factors = {'L1_gnn_a_src': 7.615, 'L1_gnn_a_dst': 4.047}
    for name, (base, spread) in spreads.items():
        noise = np.random.default_rng([zlib.crc32(name.encode()), seed]).standard_normal(out[name].shape)
        drawn = base * np.exp(spread * noise) if base else spread * noise
        out[name] = jnp.asarray(drawn.astype(out[name].dtype))
    for name, factor in factors.items():
        out[name] = (out[name] * factor).astype(out[name].dtype)
    return out
```

```python
import concourse.bass as bass
from concourse import mybir
from contextlib import ExitStack

f32 = mybir.dt.float32
bf16 = mybir.dt.bfloat16
f8 = mybir.dt.float8e4
i32 = mybir.dt.int32
u32 = mybir.dt.uint32
u8 = mybir.dt.uint8
ALU = mybir.AluOpType
ACT = mybir.ActivationFunctionType
AX = mybir.AxisListType

P = 128
QT = 4
CREDIT = 4
S = 25
GROUPS = [9, 8, 8]
EPS0 = 1e-5
EPS1 = 1e-6
SLOPE = 0.01
BIG = 2.0 ** 100
EDMAX = 30.0
NEG = -1e9
TINY = 1e-37


def spread(ap, dim, n):
    shape = list(ap.shape)
    return ap.unsqueeze(dim).broadcast_to(shape[:dim] + [n] + shape[dim:])


class Chain:

    def __init__(self, eng, sem, hold):
        self.eng, self.sem, self.n, self.hold = eng, sem, 0, hold

    def start(self):
        self.hold(self.eng)
        self.eng.sem_clear(self.sem)
        self.n = 0

    def link(self, ins):
        self.n += 1
        ins.then_inc(self.sem, 1)
        self.eng.wait_ge(self.sem, self.n)


def gnn_two_layers(nc, x, adj, W0, b0, W1, a_src, a_dst, bias1, gamma1, beta1, out):
    B, N, C = x.shape
    H, D, HO = W1.shape
    T = a_src.shape[1]
    NT = N // P
    NQ = NT // QT
    TILES = B * NT
    IQ = QT * P
    KC = C // P
    PARTS = 3
    FW = PARTS * (HO + 1)
    GW = 8
    NG = N // GW
    ZROW = B * N
    ZEROS = 16 * B
    assert NQ == 4 and QT == H and H * HO == C and S == sum(GROUPS)

    x_t = x.rearrange("b (t p) c -> (b t) p c", p=P)
    adj_t = adj.rearrange("b (t p) j -> (b t) p j", p=P)
    out_q = out.rearrange("b (q i p) (h e) -> (b q) p i h e", i=QT, p=P, h=H)

    h0_dram = nc.dram_tensor("h0_rows", (B * N + 1, C), f32, kind="Internal").ap()
    at_dram = nc.dram_tensor("adjacency_transposed", (TILES, P, NT * P), u8, kind="Internal").ap()
    es_dram = nc.dram_tensor("e_src_rows", (B * NQ, H, IQ), f32, kind="Internal").ap()
    f_dram = nc.dram_tensor("weighted_features", (TILES, P, H, 2 * FW), bf16, kind="Internal").ap()
    xh_dram = nc.dram_tensor("x1_and_h", (B * NQ, QT, P, H, 2, HO), f32, kind="Internal").ap()
    h0_t = h0_dram[0:B * N, :].rearrange("(t p) c -> t p c", p=P)

    keep = ExitStack()
    ident = keep.enter_context(nc.sbuf_tensor("ident", [P, P], f32))
    ones = keep.enter_context(nc.sbuf_tensor("ones", [P, P], f32))
    eps = keep.enter_context(nc.sbuf_tensor("eps", [P, 2], f32))
    over_a = keep.enter_context(nc.sbuf_tensor("over_a", [P, TILES], f32))
    top_s = keep.enter_context(nc.sbuf_tensor("top_s", [P, TILES], f32))
    dtop = keep.enter_context(nc.sbuf_tensor("dtop", [P, B, 2, H], f32))
    flags = keep.enter_context(nc.sbuf_tensor("flags", [1, B], i32))

    ctx = ExitStack()
    with ctx:
        def sb(name, shape, dt=f32):
            return ctx.enter_context(nc.sbuf_tensor(name, shape, dt))

        def pb(name, shape, dt=f32):
            return ctx.enter_context(nc.psum_tensor(name, shape, dt))

        sems, dma_sems = [], []

        def sem(name):
            sems.append(ctx.enter_context(nc.semaphore(name)))
            return sems[-1]

        def pair(name):
            two = [ctx.enter_context(nc.semaphore(f"{name}{k}")) for k in range(2)]
            dma_sems.extend(two)
            return two

        ident_b = sb("ident_b", [P, P], bf16)
        group_desc = sb("group_desc", [P, NG])
        bit_mask = sb("bit_mask", [P, GW], i32)
        bit_pos = sb("bit_pos", [P, GW], i32)
        pack = sb("pack", [P, P // GW], bf16)
        rank8 = sb("rank8", [P, 1])
        row_end = sb("row_end", [P, TILES])
        row_zero = sb("row_zero", [P, TILES])
        W0_sb = sb("W0_sb", [P, 2 * KC, C])
        W1_sb = sb("W1_sb", [P, KC, C + 2 * H])
        b0_row = sb("b0_row", [1, C])
        a_sb = sb("a_sb", [P, 2, H, HO])
        a_prod = sb("a_prod", [P, 2, H, HO])
        bias_b = sb("bias_b", [P, H, HO])
        gamma_b = sb("gamma_b", [P, H, HO])
        beta_b = sb("beta_b", [P, H, HO])
        xp = sb("xp", [P, 2, C])
        h0s = sb("h0s", [P, 2, C])
        p_st = sb("p_st", [P, 6])
        p_mv = sb("p_mv", [P, 2])
        p_sd = sb("p_sd", [P, 1])
        p_rn = sb("p_rn", [P, 2, 2])
        adj_sb = sb("adj_sb", [P, N], i32)
        adj_b = sb("adj_b", [P, N], bf16)
        at_st = sb("at_st", [P, 2, NT * P], f8)
        code = sb("code", [P, 2, NG])
        code_top = sb("code_top", [P, 32])
        code_int = sb("code_int", [P, 32], i32)
        first8 = sb("first8", [P, 32], i32)
        bits = sb("bits", [P, 32, GW], i32)
        cand_v = sb("cand_v", [P, 32, GW])
        cand = sb("cand", [P, 2, 32 * GW])
        score = sb("score", [P, 32])
        zero_fix = sb("zero_fix", [P, 32])
        idx = sb("idx", [P, QT, 32], i32)
        g = sb("g", [P, 2, GROUPS[0], C])
        aggp = sb("aggp", [P, len(GROUPS), C])
        cat = sb("cat", [P, 2 * KC, P])
        xr = sb("xr", [P, 2, C])
        catT = sb("catT", [P, 2 * KC, P])
        xh = sb("xh", [P, 2, H, 2, HO])
        l_st = sb("l_st", [P, 6])
        l_mv = sb("l_mv", [P, 2])
        l_sd = sb("l_sd", [P, 1])
        l_rn = sb("l_rn", [P, 2])
        h1 = sb("h1", [P, C])
        h1T = sb("h1T", [P, KC, P])
        es_row = sb("es_row", [H, 2, P])
        esed = sb("esed", [P, NT, 2, H])
        uf = sb("uf", [P, 2, H, HO + 1])
        f_st = sb("f_st", [P, 2, H, 2, PARTS, HO + 1], bf16)
        at_q = sb("at_q", [P, QT, NT, P], u8)
        es_b = sb("es_b", [P, 2, IQ])
        ed_big = sb("ed_big", [P, NT, H])
        F = sb("F", [P, NT, H, 2 * FW], bf16)
        sign = sb("sign", [P, 2, 4, IQ], u8)
        BC = sb("BC", [P, 2, 2, NT, IQ], u8)
        dmx = sb("dmx", [P, 2, H])
        dmx_t = sb("dmx_t", [2 * H, 1])
        dmx_d = sb("dmx_d", [2 * H, 2 * H])
        srow = sb("srow", [P, NT, H])
        mrow = sb("mrow", [P, NT, H])
        ab_arg = sb("ab_arg", [P, 2, NT, H])
        ab = sb("ab", [P, 2, NT, H])
        vb = sb("vb", [P, 2, FW])
        wb = sb("wb", [P, FW])
        oraw = sb("oraw", [P, QT, HO + 1])
        xhr = sb("xhr", [P, 2, QT, 2, HO])
        rden = sb("rden", [P, QT])
        o1 = sb("o1", [P, QT, HO])
        o_st = sb("o_st", [P, QT, 6])
        o_mv = sb("o_mv", [P, QT, 2])
        o_sd = sb("o_sd", [P, QT])
        o_rs = sb("o_rs", [P, QT])
        o2 = sb("o2", [P, QT, HO])
        outs = sb("outs", [P, 2, QT, HO])
        sum_a = sb("sum_a", [P, 2])
        cnt_a = sb("cnt_a", [P, 2])

        ps_A = pb("ps_A", [P, N], bf16)
        ps_cat = pb("ps_cat", [P, 2 * KC, P])
        ps_x = pb("ps_x", [P, 2, C])
        ps_h = pb("ps_h", [P, 512])
        ps_k = pb("ps_k", [P, 512])
        ps_o = [pb(f"ps_o{k}", [P, 512]) for k in range(2)]

        consts_loaded = ctx.enter_context(nc.semaphore("consts_loaded"))
        consts_made = ctx.enter_context(nc.semaphore("consts_made"))
        weights_ready = ctx.enter_context(nc.semaphore("weights_ready"))
        zeros_written = ctx.enter_context(nc.semaphore("zeros_written"))
        held = ctx.enter_context(nc.semaphore("held"))
        credits_given = ctx.enter_context(nc.semaphore("credits_given"))
        xp_loaded = pair("xp_loaded")
        h0_written = pair("h0_written")
        adj_loaded = ctx.enter_context(nc.semaphore("adj_loaded"))
        at_written = pair("at_written")
        gathered = [ctx.enter_context(nc.semaphore(f"gathered{k}")) for k in range(2)]
        cat_loaded = ctx.enter_context(nc.semaphore("cat_loaded"))
        xr_loaded = pair("xr_loaded")
        xh_written = pair("xh_written")
        es_written = pair("es_written")
        f_written = pair("f_written")
        at_q_loaded = [ctx.enter_context(nc.semaphore(f"at_q_loaded{k}")) for k in range(4)]
        es_b_loaded = pair("es_b_loaded")
        F_loaded = [ctx.enter_context(nc.semaphore(f"F_loaded{h}")) for h in range(H)]
        xhr_loaded = pair("xhr_loaded")
        out_written = pair("out_written")
        p_var = sem("p_var")
        p_sqrt = sem("p_sqrt")
        p_norm = sem("p_norm")
        h0_ready = sem("h0_ready")
        adj_b_ready = sem("adj_b_ready")
        A_T_done = sem("A_T_done")
        at_ready = sem("at_ready")
        codes_done = sem("codes_done")
        codes_read = sem("codes_read")
        idx_ready = sem("idx_ready")
        group_reduced = sem("group_reduced")
        agg_ready = sem("agg_ready")
        cat_T_done = sem("cat_T_done")
        catT_ready = sem("catT_ready")
        x1_done = sem("x1_done")
        x1_ready = sem("x1_ready")
        l_var = sem("l_var")
        l_sqrt = sem("l_sqrt")
        l_norm = sem("l_norm")
        h1_ready = sem("h1_ready")
        h1_T_done = sem("h1_T_done")
        h1T_ready = sem("h1T_ready")
        wh_done = sem("wh_done")
        wh_ready = sem("wh_ready")
        es_row_ready = sem("es_row_ready")
        exps_ready = sem("exps_ready")
        esed_ready = sem("esed_ready")
        uf_ready = sem("uf_ready")
        hi_ready = sem("hi_ready")
        rest_ready = sem("rest_ready")
        mid_ready = sem("mid_ready")
        rest2_ready = sem("rest2_ready")
        f_ready = sem("f_ready")
        sign_ready = sem("sign_ready")
        bc_ready = sem("bc_ready")
        acc_done = sem("acc_done")
        half_ready = sem("half_ready")
        acc_read = sem("acc_read")
        o_var = sem("o_var")
        o_sqrt = sem("o_sqrt")
        out_ready = sem("out_ready")
        dmx_ready = sem("dmx_ready")
        dmx_T_done = sem("dmx_T_done")
        dmx_d_ready = sem("dmx_d_ready")
        dtop_done = sem("dtop_done")
        ed_big_ready = sem("ed_big_ready")
        ab_arg_ready = sem("ab_arg_ready")
        ab_ready = sem("ab_ready")
        dv_prep = ctx.enter_context(nc.semaphore("dv_prep"))
        dv_idx = ctx.enter_context(nc.semaphore("dv_idx"))
        dv_l0 = ctx.enter_context(nc.semaphore("dv_l0"))
        dv_l1 = ctx.enter_context(nc.semaphore("dv_l1"))
        dv_batch = ctx.enter_context(nc.semaphore("dv_batch"))
        dv_const = ctx.enter_context(nc.semaphore("dv_const"))

        fills, filled = [0, 0], {}
        for i in range(QT):
            for k, size in enumerate(GROUPS):
                slot = (len(GROUPS) * i + k) % 2
                fills[slot] += 16 * size
                filled[i, k] = (slot, fills[slot])
        assert QT * len(GROUPS) % 2 == 0

        def after(k):
            return k + CREDIT

        def landed(n, i, more):
            return 16 + 8 * (n + i - i % 2 + more)

        def hold(eng):
            eng.sem_inc(held, 1)

        def schedule(eng, body):
            spans = [(0, 1), (1, 2), (2, B), (B, B + 1), (B + 1, B + 2)]
            if B == 1:
                spans = [(0, 1), (1, 2), (2, 3)]
            for lo, hi in spans:
                if lo >= hi:
                    continue
                st = {"prep": lo < B, "l0": 1 <= lo <= B, "l1": lo >= 2, "idx": 1 <= lo <= B,
                      "idx_last": lo < B, "at": 2 <= lo, "at_last": 1 <= lo <= B}

                def run(tb):
                    first = {k for k in ("prep", "idx", "l0", "l1", "at") if st[k]}
                    final = {k for k in ("prep", "l0", "l1") if st[k]} | {k for k in ("idx", "at") if st[k + "_last"]}
                    with eng.Fori(0, NQ - 1) as q:
                        body(tb, q, first, False)
                    body(tb, NQ - 1, final, True)
                if hi - lo == 1:
                    run(lo)
                else:
                    with eng.Fori(lo, hi) as tb:
                        run(tb)

        def t_prep(tb, q):
            return tb * NT + q * QT

        def t_idx(tb, q):
            return tb * NT + q * QT - 3 * QT

        def t_l0(tb, q):
            return tb * NT + q * QT - NT

        def t_l1(tb, q):
            return tb * NT + q * QT - 2 * NT

        def q_of(tb, q, lag):
            return tb * NQ + q - lag

        block = ctx.enter_context(nc.Block())

        @block.sync
        def _(sp):
            for s in sems:
                sp.sem_inc(s, CREDIT)
            for s in dma_sems:
                sp.sem_inc(s, 16)
            sp.sem_inc(credits_given, 1)
            sp.wait_ge(consts_made, 1)
            sp.dma_start(h0_dram[B * N:B * N + 1, :], g[0:1, 0, 0, :]).then_inc(zeros_written, 16)
            if B > 1:
                later = h0_dram[N:B * N, :].rearrange("(p r) c -> p r c", p=P)
                for k in range(0, later.shape[1], NT):
                    sp.dma_start(later[:, k:k + NT, :],
                                 g[:, :, :, :].rearrange("p a s c -> p (a s) c")[:, 0:NT, :]).then_inc(zeros_written, 16)
            sp.dma_start(W0_sb[:, :, :], W0.rearrange("(k p) o -> p k o", p=P)).then_inc(consts_loaded, 16)
            for h in range(H):
                sp.dma_start(W1_sb[:, :, h * HO:(h + 1) * HO],
                             W1[h].rearrange("(k p) e -> p k e", p=P)).then_inc(consts_loaded, 16)
            sp.dma_start(b0_row[:, :], b0.rearrange("(a c) -> a c", a=1)).then_inc(consts_loaded, 16)
            for k, a in enumerate((a_src, a_dst)):
                sp.dma_start(a_sb[:, k, :, :], spread(a[:, 0, :], 0, P)
                             ).then_inc(consts_loaded, 16)
            for dst, src in ((bias_b, bias1), (gamma_b, gamma1), (beta_b, beta1)):
                sp.dma_start(dst[:, :, :], spread(src, 0, P)).then_inc(consts_loaded, 16)

            def prep_load(n, i):
                sp.wait_ge(h0_ready, after(n + i - 1))
                sp.dma_start(xp[:, i % 2, :], x_t[n + i]).then_inc(xp_loaded[i % 2], 16)

            def prep_store(n, i):
                sp.wait_ge(h0_ready, after(n + i + 1))
                sp.wait_ge(zeros_written, ZEROS)
                sp.dma_start(h0_t[n + i], h0s[:, i % 2, :]).then_inc(h0_written[i % 2], 16)

            def adj_load(n, i):
                sp.wait_ge(adj_b_ready, after(n + i))
                sp.dma_start(adj_sb[:, :], adj_t[n + i]).then_inc(adj_loaded, 16)

            def at_store(n, i):
                sp.wait_ge(at_ready, after(n + i + 1))
                sp.dma_start(at_dram[n + i], at_st[:, i % 2, :].bitcast(u8)).then_inc(at_written[i % 2], 16)

            def l0_load(n, i):
                sp.wait_ge(cat_T_done, after(n + i))
                sp.dma_start(cat[:, 0:KC, :].rearrange("p k c -> p (k c)"), h0_t[n + i]).then_inc(cat_loaded, 16)
                sp.wait_ge(x1_ready, after(n + i - 1))
                sp.dma_start(xr[:, i % 2, :], x_t[n + i]).then_inc(xr_loaded[i % 2], 16)

            def l0_store(n, Q, i):
                sp.wait_ge(es_row_ready, after(n + i + 1))
                sp.dma_start(es_dram[Q, :, i * P:(i + 1) * P], es_row[:, i % 2, :]).then_inc(es_written[i % 2], 16)
                sp.wait_ge(wh_ready, after(n + i + 1))
                sp.dma_start(xh_dram[Q, i].rearrange("p h a e -> p (h a e)"),
                             xh[:, i % 2].rearrange("p h a e -> p (h a e)")).then_inc(xh_written[i % 2], 16)
                sp.wait_ge(f_ready, after(n + i + 1))
                sp.dma_start(f_dram[n + i].rearrange("p h f -> p (h f)"),
                             f_st[:, i % 2].rearrange("p h a r e -> p (h a r e)")).then_inc(f_written[i % 2], 16)

            def at_load(n, k):
                sp.wait_ge(bc_ready, after((n - 1) * 4 + k + 1))
                hold(sp)
                for w in at_written:
                    sp.wait_ge(w, 16 + 8 * (n + QT))
                    hold(sp)
                sp.dma_start(at_q[:, :, 4 * k:4 * k + 4, :],
                             at_dram[bass.ds(n, QT), :, 4 * k * P:4 * (k + 1) * P].rearrange("t p (j i) -> p t j i", i=P)
                             if not isinstance(n, int) else
                             at_dram[n:n + QT, :, 4 * k * P:4 * (k + 1) * P].rearrange("t p (j i) -> p t j i", i=P)
                             ).then_inc(at_q_loaded[k], 16)

            def body(tb, q, stages, last):
                for i in range(QT):
                    if "idx" in stages:
                        n = t_idx(tb, q)
                        adj_load(n, i)
                    if "prep" in stages:
                        prep_load(t_prep(tb, q), i)
                    if "l0" in stages:
                        l0_load(t_l0(tb, q), i)
                    if "l1" in stages:
                        n = t_l1(tb, q)
                        Q = q_of(tb, q, 2 * NQ)
                        if i == 0:
                            for k in range(2):
                                for w in (es_written, xh_written):
                                    sp.wait_ge(w[k], 16 + 16 * (NT // 2) * (tb - 1))
                        sp.wait_ge(sign_ready, after((n + i - 1) * 4))
                        sp.dma_start(es_b[:, i % 2, :], spread(es_dram[Q, i], 0, P)
                                     ).then_inc(es_b_loaded[i % 2], 16)
                        sp.wait_ge(out_ready, after(n + i - 1))
                        sp.dma_start(xhr[:, i % 2].rearrange("p i a e -> p i (a e)"),
                                     xh_dram[Q, :, :, i].rearrange("i p a e -> p i (a e)")).then_inc(xhr_loaded[i % 2], 16)
                    if "prep" in stages:
                        prep_store(t_prep(tb, q), i)
                    if "idx" in stages:
                        at_store(t_idx(tb, q), i)
                    if "l0" in stages:
                        l0_store(t_l0(tb, q), q_of(tb, q, NQ), i)
                    if "l1" in stages:
                        n, Q = t_l1(tb, q), q_of(tb, q, 2 * NQ)
                        sp.wait_ge(out_ready, after(n + i + 1))
                        sp.dma_start(out_q[Q, :, :, i, :], outs[:, i % 2]).then_inc(out_written[i % 2], 16)
                    if i == QT - 1 and "at" in stages:
                        for k in range(4):
                            at_load(t_l1(tb, q) + QT, k)
                if last and "l0" in stages:
                    for k in range(2):
                        sp.wait_ge(f_written[k], 16 + 16 * (NT // 2) * tb)
                    for h in range(H):
                        if "l1" in stages:
                            sp.wait_ge(acc_done, after((t_l1(tb, q) + h + 1) * QT))
                        t0 = tb * NT - NT
                        sp.dma_start(F[:, :, h, :], f_dram[bass.ds(t0, NT), :, h, :].rearrange("t p f -> p t f")
                                     ).then_inc(F_loaded[h], 16)

            schedule(sp, body)
            for k in range(2):
                sp.wait_ge(out_written[k], 16 + 16 * TILES // 2)

        @block.gpsimd
        def _(pool):
            pool.memset(ident[:, :], 0.0)
            pool.memset(ident_b[:, :], 0.0)
            pool.memset(ones[:, :], 1.0)
            pool.memset(eps[:, 0:1], EPS0)
            pool.memset(eps[:, 1:2], EPS1)
            pool.memset(g[:, :, :, :], 0.0).then_inc(consts_made, 1)
            pool.wait_ge(consts_made, 1)
            pool.affine_select(out=ident[:, :], in_=ident[:, :], compare_op=ALU.not_equal, fill=1.0, base=0,
                               pattern=[[-1, P]], channel_multiplier=1)
            pool.affine_select(out=ident_b[:, :], in_=ident_b[:, :], compare_op=ALU.not_equal, fill=1.0, base=0,
                               pattern=[[-1, P]], channel_multiplier=1)
            pool.iota(group_desc[:, :], [[-256, NG]], base=256 * NG, channel_multiplier=0,
                      allow_small_or_imprecise_dtypes=True)
            pool.iota(bit_pos[:, :], [[1, GW]], base=0, channel_multiplier=0)
            for k in range(GW):
                pool.memset(bit_mask[:, k:k + 1], 2 ** (GW - 1 - k))
            pool.iota(row_end[:, :], [[N, B], [0, NT]], base=N, channel_multiplier=0,
                      allow_small_or_imprecise_dtypes=True)
            pool.iota(row_zero[:, :], [[-N, B], [0, NT]], base=ZROW - N, channel_multiplier=0,
                      allow_small_or_imprecise_dtypes=True)
            pool.memset(pack[:, :], 0.0).then_inc(consts_made, 1)
            pool.wait_ge(consts_made, 2)
            for k in range(GW):
                pool.affine_select(out=pack[:, :], in_=pack[:, :], compare_op=ALU.not_equal,
                                   fill=float(2 ** (GW - 1 - k)), base=-k, pattern=[[-GW, P // GW]],
                                   channel_multiplier=1).then_inc(consts_made, 1)
                pool.wait_ge(consts_made, 3 + k)
            pool.wait_ge(zeros_written, ZEROS)
            pool.wait_ge(consts_loaded, 16 * 11)
            pool.wait_ge(credits_given, 1)
            pool.nop().then_inc(consts_made, 1)

            def body(tb, q, stages, last):
                if "l0" not in stages:
                    return
                n, Q = t_l0(tb, q), q_of(tb, q, NQ)
                for k in range(2):
                    pool.wait_ge(h0_written[k], 16 + 16 * (NT // 2) * tb)
                for i in range(QT):
                    pool.wait_ge(idx_ready, after(n + i + 1))
                    for k, size in enumerate(GROUPS):
                        slot = filled[i, k][0]
                        pool.wait_ge(group_reduced, after((n + i) * len(GROUPS) + k - 1))
                        hold(pool)
                        for s in range(size):
                            at = sum(GROUPS[:k]) + s
                            pool.indirect_dma_start(
                                g[:, slot, s, :], None, h0_dram,
                                bass.IndirectOffsetOnAxis(ap=idx[:, i, at:at + 1], axis=0)).then_inc(gathered[slot], 16)

            schedule(pool, body)

        @block.scalar
        def _(act):
            act.wait_ge(consts_made, 3 + GW)

            def prep(n, i):
                act.wait_ge(p_var, after(n + i + 1))
                nc.scalar.activation(p_sd[:, :], p_mv[:, 1:2], ACT.Sqrt, bias=eps[:, 0:1]).then_inc(p_sqrt, 1)
                act.wait_ge(p_norm, after(n + i + 1))
                act.wait_ge(h0_written[i % 2], landed(n, i, 0))
                nc.scalar.activation(h0s[:, i % 2, :], xp[:, i % 2, :], ACT.Relu, bias=p_rn[:, i % 2, 1:2],
                                     scale=p_rn[:, i % 2, 0:1]).then_inc(h0_ready, 1)

            def adj_convert(n, i):
                act.wait_ge(adj_loaded, 16 * (n + i + 1))
                act.wait_ge(A_T_done, after(n + i))
                act.wait_ge(idx_ready, after(n + i - 1))
                nc.scalar.activation(adj_b[:, :], adj_sb[:, :].bitcast(u32), ACT.Copy,
                                     accum_out=sum_a[:, i % 2:i % 2 + 1]).then_inc(adj_b_ready, 1)

            def adj_transposed(n, i):
                act.wait_ge(A_T_done, after(n + i + 1))
                act.wait_ge(at_written[i % 2], landed(n, i, 0))
                act.wait_ge(codes_done, after(n + i - 1))
                hold(act)
                nc.scalar.activation(at_st[:, i % 2, :], ps_A[:, :], ACT.Sign,
                                     accum_out=cnt_a[:, i % 2:i % 2 + 1], saturate=False).then_inc(at_ready, 1)

            def l0_a(n, i):
                act.wait_ge(cat_T_done, after(n + i + 1))
                act.wait_ge(x1_done, after(n + i))
                nc.scalar.activation(catT[:, :, :], ps_cat[:, :, :], ACT.Copy).then_inc(catT_ready, 1)

            def l0_b(n, i):
                act.wait_ge(l_var, after(n + i + 1))
                nc.scalar.activation(l_sd[:, :], l_mv[:, 1:2], ACT.Sqrt, bias=eps[:, 0:1]).then_inc(l_sqrt, 1)
                act.wait_ge(l_norm, after(n + i + 1))
                act.wait_ge(h1_T_done, after(n + i))
                nc.scalar.activation(h1[:, :].rearrange("p (h e) -> p h e", h=H), xh[:, i % 2, :, 0, :], ACT.Relu,
                                     bias=l_rn[:, 1:2], scale=l_rn[:, 0:1]).then_inc(h1_ready, 1)
                act.wait_ge(h1_T_done, after(n + i + 1))
                act.wait_ge(wh_done, after(n + i))
                nc.scalar.activation(h1T[:, :, :].rearrange("p k c -> p (k c)"), ps_x[:, 1, :], ACT.Copy).then_inc(h1T_ready, 1)

            def l0_c(n, q, i):
                act.wait_ge(wh_done, after(n + i + 1))
                act.wait_ge(f_ready, after(n + i))
                nc.scalar.activation(uf[:, 0, :, HO], ps_h[:, C + H:C + 2 * H], ACT.Exp)
                nc.scalar.activation(uf[:, 1, :, HO], ps_h[:, C + H:C + 2 * H], ACT.Exp, scale=SLOPE).then_inc(exps_ready, 1)
                act.wait_ge(xh_written[i % 2], landed(n, i, 0))
                nc.scalar.activation(xh[:, i % 2, :, 1, :], ps_h[:, 0:C].rearrange("p (h e) -> p h e", h=H),
                                     ACT.Copy).then_inc(wh_ready, 1)
                nc.scalar.activation(esed[:, bass.ds(q * QT + i, 1), :, :] if not isinstance(q, int) else
                                     esed[:, q * QT + i:q * QT + i + 1, :, :],
                                     ps_h[:, C:C + 2 * H].rearrange("p (o a h) -> p o a h", o=1, a=2),
                                     ACT.Copy).then_inc(esed_ready, 1)
                act.wait_ge(es_written[i % 2], landed(n, i, 0))
                nc.scalar.activation(es_row[:, i % 2, :], ps_h[0:H, 384:512], ACT.Copy).then_inc(es_row_ready, 1)
                act.wait_ge(f_written[i % 2], landed(n, i, 0))
                act.wait_ge(uf_ready, after(n + i + 1))
                nc.scalar.activation(parts(i, 0), uf_v, ACT.Copy).then_inc(hi_ready, 1)
                act.wait_ge(rest_ready, after(n + i + 1))
                nc.scalar.activation(parts(i, 1), uf_v, ACT.Copy).then_inc(mid_ready, 1)
                act.wait_ge(rest2_ready, after(n + i + 1))
                nc.scalar.activation(parts(i, 2), uf_v, ACT.Copy).then_inc(f_ready, 1)

            def signs(n, i, k):
                if k == 0:
                    act.wait_ge(es_b_loaded[i % 2], landed(n, i, 2))
                act.wait_ge(bc_ready, after((n + i) * 4 + k - 1))
                for j in range(4):
                    jc = 4 * k + j
                    last = nc.scalar.activation(sign[:, k % 2, j, :], es_b[:, i % 2, :], ACT.Relu,
                                                bias=ed_big[:, jc, i:i + 1], scale=BIG)
                last.then_inc(sign_ready, 1)

            def scale_acc(n, Q, i, it):
                act.wait_ge(acc_done, after((n + i) * 4 + it + 1))
                act.wait_ge(acc_read, after((n + i) * 4 + it - 1))
                nc.scalar.activation(vb[:, it % 2, :], ps_o[it % 2][:, 0:FW], ACT.Copy,
                                     scale=ab[:, 0, bass.ds(Q_in(Q) + it, 1), i]).then_inc(half_ready, 1)

            def body(tb, q, stages, last):
                np_, ni, n0, n1 = t_prep(tb, q), t_idx(tb, q), t_l0(tb, q), t_l1(tb, q)
                for i in range(QT):
                    if "idx" in stages:
                        adj_convert(ni, i)
                    if "prep" in stages:
                        prep(np_, i)
                    if "l1" in stages:
                        signs(n1, i, 0)
                        signs(n1, i, 1)
                    if "idx" in stages:
                        adj_transposed(ni, i)
                    if "l1" in stages:
                        signs(n1, i, 2)
                        signs(n1, i, 3)
                    if "l0" in stages:
                        l0_a(n0, i)
                    if "l0" in stages:
                        l0_b(n0, i)
                    if "l1" in stages:
                        for it in range(QT):
                            act.wait_ge(acc_done, after((n1 + i) * 4 + it + 1))
                            act.wait_ge(acc_read, after((n1 + i) * 4 + it - 1))
                            nc.scalar.activation(vb[:, it % 2, :], ps_o[it % 2][:, 0:FW], ACT.Copy,
                                                 scale=ab_col(0, q, it, i)).then_inc(half_ready, 1)
                    if "l0" in stages:
                        l0_c(n0, q, i)
                    if "l1" in stages:
                        act.wait_ge(o_var, after(n1 + i + 1))
                        nc.scalar.activation(o_sd[:, :], o_mv[:, :, 1], ACT.Sqrt, bias=eps[:, 1:2]).then_inc(o_sqrt, 1)
                if last and "l0" in stages:
                    act.wait_ge(ab_arg_ready, after(tb))
                    nc.scalar.activation(ab[:, :, :, :], ab_arg[:, :, :, :], ACT.Exp).then_inc(ab_ready, 1)

            uf_v = uf[:, :, :, :]

            def parts(i, r):
                return f_st[:, i % 2, :, :, r, :].rearrange("p h a e -> p a h e")

            def ab_col(a, q, it, h):
                return ab[:, a, bass.ds(q * QT + it, 1), h] if not isinstance(q, int) else \
                    ab[:, a, q * QT + it:q * QT + it + 1, h]

            schedule(act, body)

        @block.vector
        def _(dve):
            V = nc.vector
            c0 = Chain(dve, dv_const, hold)
            c0.start()
            dve.wait_ge(consts_made, 3 + GW)
            for k in range(KC):
                for a in range(2):
                    c0.link(V.tensor_tensor(a_prod[:, a, :, :], W1_sb[:, k, 0:C].rearrange("p (h e) -> p h e", h=H),
                                            a_sb[:, a, :, :], ALU.mult))
                    c0.link(V.tensor_reduce(W1_sb[:, k, C + a * H:C + (a + 1) * H], a_prod[:, a, :, :], AX.X, ALU.add))
            V.memset(esed[:, 0, :, :], 0.0).then_inc(weights_ready, 1)

            ch_prep, ch_idx, ch_l0 = Chain(dve, dv_prep, hold), Chain(dve, dv_idx, hold), Chain(dve, dv_l0, hold)
            ch_l1, ch_b = Chain(dve, dv_l1, hold), Chain(dve, dv_batch, hold)

            def prep_a(n, i):
                dve.wait_ge(xp_loaded[i % 2], landed(n, i, 2))
                ch_prep.start()
                dve.wait_ge(p_sqrt, after(n + i))
                ch_prep.link(V.bn_stats(p_st[:, :], xp[:, i % 2, :]))
                V.bn_aggr(p_mv[:, :], p_st[:, :]).then_inc(p_var, 1)

            def prep_b(n, i):
                dve.wait_ge(p_sqrt, after(n + i + 1))
                dve.wait_ge(h0_ready, after(n + i - 1))
                ch_prep.link(V.reciprocal(p_rn[:, i % 2, 0:1], p_sd[:, :]))
                V.scalar_tensor_tensor(p_rn[:, i % 2, 1:2], p_mv[:, 0:1], -1.0, p_rn[:, i % 2, 0:1], ALU.mult,
                                       ALU.mult).then_inc(p_norm, 1)

            def top32(chain, dst, buf):
                for r in range(4):
                    chain.link(V.max(dst[:, 8 * r:8 * r + 8], buf[:, r % 2, :]))
                    if r < 3:
                        chain.link(V.match_replace(buf[:, 1 - r % 2, :], dst[:, 8 * r:8 * r + 8], buf[:, r % 2, :], 0.0))

            def find(n, i):
                ch_idx.start()
                dve.wait_ge(codes_done, after(n + i + 1))
                ch_idx.link(V.scalar_tensor_tensor(code[:, 1, :], ps_k[:, 0:NG], 0.0, group_desc[:, :], ALU.is_gt, ALU.mult))
                V.tensor_tensor(code[:, 0, :], code[:, 1, :], ps_k[:, 0:NG], ALU.add).then_inc(codes_read, 1)
                dve.wait_ge(codes_read, after(n + i + 1))
                hold(dve)
                top32(ch_idx, code_top, code)
                ch_idx.link(V.tensor_copy(code_int[:, :], code_top[:, :]))
                V.tensor_scalar(first8[:, :], code_int[:, :], 8, 3, ALU.logical_shift_right, ALU.logical_shift_left)
                ch_idx.link(V.tensor_tensor(bits[:, :, :], spread(code_int[:, :], 2, GW),
                                            spread(bit_mask[:, :], 1, 32), ALU.bitwise_and))
                ch_idx.link(V.tensor_tensor(cand_v[:, :, :], spread(first8[:, :], 2, GW),
                                            spread(bit_pos[:, :], 1, 32), ALU.subtract))
                ch_idx.link(V.scalar_tensor_tensor(cand[:, 0, :].rearrange("p (s k) -> p s k", k=GW), bits[:, :, :], 0.0,
                                                   cand_v[:, :, :], ALU.is_gt, ALU.mult))
                top32(ch_idx, score, cand)
                V.tensor_copy(top_s[:, bass.ds(n + i, 1)], score[:, 0:1])
                V.tensor_tensor(over_a[:, bass.ds(n + i, 1)], sum_a[:, i % 2:i % 2 + 1], cnt_a[:, i % 2:i % 2 + 1],
                                ALU.subtract)
                ch_idx.link(V.tensor_scalar(zero_fix[:, :], score[:, :], 0.0, row_zero[:, bass.ds(n + i, 1)],
                                            ALU.is_equal, ALU.mult))
                ch_idx.link(V.scalar_tensor_tensor(zero_fix[:, :], score[:, :], -1.0, zero_fix[:, :], ALU.mult, ALU.add))
                V.tensor_scalar(idx[:, i, :], zero_fix[:, :], row_end[:, bass.ds(n + i, 1)], None, ALU.add).then_inc(idx_ready, 1)

            def reduce_group(n, Q, i, k):
                slot, count = filled[i, k]
                dve.wait_ge(gathered[slot], Q * fills[slot] + count)
                if k == 0:
                    dve.wait_ge(agg_ready, after(n + i))
                V.tensor_reduce(aggp[:, k, :], g[:, slot, 0:GROUPS[k], :].rearrange("p s c -> p c s"), AX.X,
                                ALU.max).then_inc(group_reduced, 1)

            def aggregate(n, i):
                dve.wait_ge(group_reduced, after((n + i + 1) * len(GROUPS)))
                dve.wait_ge(cat_T_done, after(n + i))
                V.tensor_reduce(cat[:, KC:, :].rearrange("p k c -> p (k c)"), aggp[:, :, :].rearrange("p s c -> p c s"),
                                AX.X, ALU.max).then_inc(agg_ready, 1)

            def l0_x1(n, i):
                dve.wait_ge(x1_done, after(n + i + 1))
                dve.wait_ge(xr_loaded[i % 2], landed(n, i, 2))
                dve.wait_ge(xh_written[i % 2], landed(n, i, 0))
                V.scalar_tensor_tensor(xh[:, i % 2, :, 0, :], ps_x[:, 0, :].rearrange("p (h e) -> p h e", h=H), 0.0,
                                       xr[:, i % 2, :].rearrange("p (h e) -> p h e", h=H), ALU.max,
                                       ALU.add).then_inc(x1_ready, 1)
                dve.wait_ge(x1_ready, after(n + i + 1))
                ch_l0.start()
                ch_l0.link(V.bn_stats(l_st[:, :], xh[:, i % 2, :, 0, :]))
                V.bn_aggr(l_mv[:, :], l_st[:, :]).then_inc(l_var, 1)

            def l0_norm(n, i):
                dve.wait_ge(l_sqrt, after(n + i + 1))
                dve.wait_ge(h1_ready, after(n + i))
                ch_l0.link(V.reciprocal(l_rn[:, 0:1], l_sd[:, :]))
                V.scalar_tensor_tensor(l_rn[:, 1:2], l_mv[:, 0:1], -1.0, l_rn[:, 0:1], ALU.mult,
                                       ALU.mult).then_inc(l_norm, 1)

            def l0_features(n, q, i):
                dve.wait_ge(exps_ready, after(n + i + 1))
                dve.wait_ge(wh_ready, after(n + i + 1))
                for a in range(2):
                    last = V.tensor_tensor(uf[:, a, :, 0:HO], xh[:, i % 2, :, 1, :],
                                           spread(uf[:, a, :, HO], 2, HO), ALU.mult)
                last.then_inc(uf_ready, 1)
                dve.wait_ge(hi_ready, after(n + i + 1))
                V.tensor_tensor(uf[:, :, :, :], uf[:, :, :, :], part_v(i, 0), ALU.subtract).then_inc(rest_ready, 1)
                dve.wait_ge(mid_ready, after(n + i + 1))
                V.tensor_tensor(uf[:, :, :, :], uf[:, :, :, :], part_v(i, 1), ALU.subtract).then_inc(rest2_ready, 1)

            def part_v(i, r):
                return f_st[:, i % 2, :, :, r, :].rearrange("p h a e -> p a h e")

            def mask(n, Q, i, k):
                dve.wait_ge(sign_ready, after((n + i) * 4 + k + 1))
                if i == 0:
                    dve.wait_ge(at_q_loaded[k], 16 * (Q + 1))
                if k == 0:
                    dve.wait_ge(acc_done, after((n + i - 1) * 4))
                js = slice(4 * k, 4 * k + 4)
                a = at_q[:, :, js, :].bitcast(u32).rearrange("p t j w -> p j t w")
                b = BC[:, i % 2, 0, js, :].bitcast(u32).rearrange("p j (t w) -> p j t w", t=QT)
                c = BC[:, i % 2, 1, js, :].bitcast(u32).rearrange("p j (t w) -> p j t w", t=QT)
                s = sign[:, k % 2, :, :].bitcast(u32).rearrange("p j (t w) -> p j t w", t=QT)
                ch_l1.link(V.tensor_tensor(b, s, a, ALU.bitwise_and))
                V.tensor_tensor(c, a, b, ALU.bitwise_xor).then_inc(bc_ready, 1)

            def read_acc(n, q, i, it):
                dve.wait_ge(half_ready, after((n + i) * 4 + it + 1))
                beta_col = ab[:, 1, bass.ds(q * QT + it, 1), i] if not isinstance(q, int) else \
                    ab[:, 1, q * QT + it:q * QT + it + 1, i]
                V.scalar_tensor_tensor(wb[:, :], ps_o[it % 2][:, FW:2 * FW], beta_col, vb[:, it % 2, :], ALU.mult,
                                       ALU.add).then_inc(acc_read, 1)
                dve.wait_ge(acc_read, after((n + i) * 4 + it + 1))
                ch_l1.link(V.tensor_reduce(oraw[:, it, :], wb[:, :].rearrange("p (r e) -> p e r", r=PARTS), AX.X, ALU.add))

            def l1_norm(n, i):
                h = i
                ch_l1.link(V.tensor_scalar(rden[:, :], oraw[:, :, HO], TINY, None, ALU.max))
                ch_l1.link(V.reciprocal(rden[:, :], rden[:, :]))
                dve.wait_ge(xhr_loaded[i % 2], landed(n, i, 2))
                ch_l1.link(V.tensor_tensor(o1[:, :, :], oraw[:, :, 0:HO], spread(rden[:, :], 2, HO), ALU.mult))
                ch_l1.link(V.tensor_tensor(o1[:, :, :], o1[:, :, :], spread(bias_b[:, h, :], 1, QT), ALU.add))
                ch_l1.link(V.scalar_tensor_tensor(o1[:, :, :], o1[:, :, :], 0.0, xhr[:, i % 2, :, 1, :], ALU.max, ALU.add))
                for it in range(QT):
                    last = V.bn_stats(o_st[:, it, :], o1[:, it, :])
                ch_l1.link(last)
                for it in range(QT):
                    last = V.bn_aggr(o_mv[:, it, :], o_st[:, it, :])
                last.then_inc(o_var, 1)

            def l1_out(n, i):
                h = i
                dve.wait_ge(o_sqrt, after(n + i + 1))
                ch_l1.link(V.reciprocal(o_rs[:, :], o_sd[:, :]))
                for it in range(QT):
                    last = V.tensor_scalar(o2[:, it, :], o1[:, it, :], o_mv[:, it, 0:1], o_rs[:, it:it + 1],
                                           ALU.subtract, ALU.mult)
                ch_l1.link(last)
                ch_l1.link(V.tensor_tensor(o2[:, :, :], o2[:, :, :], spread(gamma_b[:, h, :], 1, QT), ALU.mult))
                ch_l1.link(V.tensor_tensor(o2[:, :, :], o2[:, :, :], spread(beta_b[:, h, :], 1, QT), ALU.add))
                dve.wait_ge(out_written[i % 2], landed(n, i, 0))
                V.tensor_tensor(outs[:, i % 2, :, :], o2[:, :, :], xhr[:, i % 2, :, 0, :], ALU.add).then_inc(out_ready, 1)

            def batch_end(tb, l1):
                b = tb - 1
                ch_b.start()
                dve.wait_ge(esed_ready, after(tb * NT))
                if l1:
                    dve.wait_ge(sign_ready, after(b * NT * 4))
                    dve.wait_ge(half_ready, after(b * NT * 4))
                ed = esed[:, :, 1, :]
                es = esed[:, :, 0, :]
                ch_b.link(V.tensor_scalar(ed_big[:, :, :], ed, BIG, None, ALU.mult))
                ch_b.link(V.tensor_reduce(dmx[:, 0, :], ed.rearrange("p t h -> p h t"), AX.X, ALU.max))
                ch_b.link(V.tensor_scalar(srow[:, :, :], ed, -1.0, None, ALU.mult))
                V.tensor_reduce(dmx[:, 1, :], srow[:, :, :].rearrange("p t h -> p h t"), AX.X, ALU.max).then_inc(dmx_ready, 1)
                dve.wait_ge(dmx_T_done, after(tb))
                ch_b.link(V.tensor_reduce(dmx_t[:, :], ps_k[0:2 * H, 256:256 + P], AX.X, ALU.max))
                V.tensor_scalar(dmx_d[:, :], ident[0:2 * H, 0:2 * H], dmx_t[:, :], None, ALU.mult).then_inc(dmx_d_ready, 1)
                dve.wait_ge(dtop_done, after(tb))
                dt = dtop[:, b, :, :] if isinstance(b, int) else dtop[:, bass.ds(b, 1), :, :].rearrange("p o a h -> p (o a) h")
                ch_b.link(V.tensor_copy(dt, ps_k[:, 384:384 + 2 * H].rearrange("p (a h) -> p a h", a=2)))
                ch_b.link(V.tensor_tensor(srow[:, :, :], es, spread(ps_k[:, 384:384 + H], 1, NT), ALU.add))
                ch_b.link(V.scalar_tensor_tensor(mrow[:, :, :], srow[:, :, :], SLOPE, srow[:, :, :], ALU.mult, ALU.max))
                ch_b.link(V.tensor_tensor(ab_arg[:, 0, :, :], es, mrow[:, :, :], ALU.subtract))
                V.scalar_tensor_tensor(ab_arg[:, 1, :, :], es, SLOPE, mrow[:, :, :], ALU.mult, ALU.subtract).then_inc(ab_arg_ready, 1)
                dve.wait_ge(ab_ready, after(tb))

            def body(tb, q, stages, last):
                np_, ni, n0, n1 = t_prep(tb, q), t_idx(tb, q), t_l0(tb, q), t_l1(tb, q)
                Q0, Q1 = q_of(tb, q, NQ), q_of(tb, q, 2 * NQ)
                for i in range(QT):
                    if "l1" in stages:
                        ch_l1.start()
                    if "prep" in stages:
                        prep_a(np_, i)
                    if "l0" in stages:
                        reduce_group(n0, Q0, i, 0)
                    if "prep" in stages:
                        prep_b(np_, i)
                    if "l1" in stages:
                        mask(n1, Q1, i, 0)
                        mask(n1, Q1, i, 1)
                    if "l0" in stages:
                        reduce_group(n0, Q0, i, 1)
                    if "l1" in stages:
                        mask(n1, Q1, i, 2)
                        mask(n1, Q1, i, 3)
                    if "l0" in stages:
                        reduce_group(n0, Q0, i, 2)
                        aggregate(n0, i)
                    if "idx" in stages:
                        find(ni, i)
                    if "l0" in stages:
                        l0_x1(n0, i)
                        l0_norm(n0, i)
                    if "l1" in stages:
                        for it in range(QT):
                            read_acc(n1, q, i, it)
                        l1_norm(n1, i)
                    if "l0" in stages:
                        l0_features(n0, q, i)
                    if "l1" in stages:
                        l1_out(n1, i)
                if last and "l0" in stages:
                    batch_end(tb, "l1" in stages)

            schedule(dve, body)

        @block.tensor
        def _(pe):
            M = nc.tensor
            pe.wait_ge(consts_made, 3 + GW)
            pe.wait_ge(weights_ready, 1)

            def adj_T(n, i):
                pe.wait_ge(adj_b_ready, after(n + i + 1))
                pe.wait_ge(at_ready, after(n + i))
                for j in range(NT):
                    last = M.transpose(ps_A[:, j * P:(j + 1) * P], adj_b[:, j * P:(j + 1) * P], ident_b[:, :])
                last.then_inc(A_T_done, 1)

            def codes(n, i):
                pe.wait_ge(at_ready, after(n + i + 1))
                pe.wait_ge(codes_read, after(n + i))
                hold(pe)
                w = P // GW
                for j in range(NT):
                    last = M.matmul(ps_k[:, j * w:(j + 1) * w], at_st[:, i % 2, j * P:(j + 1) * P], pack[:, :],
                                    start=True, stop=True)
                last.then_inc(codes_done, 1)

            def cat_T(n, i):
                pe.wait_ge(agg_ready, after(n + i + 1))
                pe.wait_ge(cat_loaded, 16 * (n + i + 1))
                pe.wait_ge(catT_ready, after(n + i))
                for k in range(2 * KC):
                    last = M.transpose(ps_cat[:, k, :], cat[:, k, :], ident[:, :])
                last.then_inc(cat_T_done, 1)

            def x1_mm(n, i):
                pe.wait_ge(catT_ready, after(n + i + 1))
                pe.wait_ge(x1_ready, after(n + i))
                for k in range(2 * KC):
                    M.matmul(ps_x[:, 0, :], catT[:, k, :], W0_sb[:, k, :], start=(k == 0), stop=False)
                M.matmul(ps_x[:, 0, :], ones[0:1, :], b0_row[:, :], start=False, stop=True).then_inc(x1_done, 1)

            def h1_T(n, i):
                pe.wait_ge(h1_ready, after(n + i + 1))
                pe.wait_ge(h1T_ready, after(n + i))
                for k in range(KC):
                    last = M.transpose(ps_x[:, 1, k * P:(k + 1) * P], h1[:, k * P:(k + 1) * P], ident[:, :])
                last.then_inc(h1_T_done, 1)

            def wh_mm(n, i):
                pe.wait_ge(h1T_ready, after(n + i + 1))
                pe.wait_ge(es_row_ready, after(n + i))
                pe.wait_ge(uf_ready, after(n + i))
                for k in range(KC):
                    M.matmul(ps_h[:, 0:C + 2 * H], h1T[:, k, :], W1_sb[:, k, :], start=(k == 0), stop=(k == KC - 1))
                for k in range(KC):
                    last = M.matmul(ps_h[0:H, 384:512], W1_sb[:, k, C:C + H], h1T[:, k, :], start=(k == 0),
                                    stop=(k == KC - 1))
                last.then_inc(wh_done, 1)

            def attend(tb, n, i, it, h):
                if it == 0:
                    pe.wait_ge(F_loaded[h], 16 * (tb - 1))
                    pe.wait_ge(bc_ready, after((n + i + 1) * 4))
                pe.wait_ge(acc_read, after((n + i) * 4 + it - 1))
                hold(pe)
                for a in range(2):
                    for j in range(NT):
                        last = M.matmul(ps_o[it % 2][:, a * FW:(a + 1) * FW],
                                        BC[:, i % 2, a, j, it * P:(it + 1) * P].bitcast(f8),
                                        F[:, j, h, a * FW:(a + 1) * FW], start=(j == 0), stop=(j == NT - 1))
                last.then_inc(acc_done, 1)

            def body(tb, q, stages, last):
                ni, n0, n1 = t_idx(tb, q), t_l0(tb, q), t_l1(tb, q)
                l0, l1, ix = "l0" in stages, "l1" in stages, "idx" in stages
                for i in range(QT):
                    if ix:
                        adj_T(ni, i)
                        codes(ni, i)
                    if l0:
                        cat_T(n0, i)
                        x1_mm(n0, i)
                        h1_T(n0, i)
                        wh_mm(n0, i)
                    if l1:
                        for it in range(QT):
                            attend(tb, n1, i, it, i)
                if last and l0:
                    pe.wait_ge(codes_read, after(ni + QT if ix else TILES))
                    pe.wait_ge(dmx_ready, after(tb))
                    M.transpose(ps_k[0:2 * H, 256:256 + P], dmx[:, :, :].rearrange("p a h -> p (a h)"), ident[:, :]).then_inc(dmx_T_done, 1)
                    pe.wait_ge(dmx_d_ready, after(tb))
                    M.matmul(ps_k[:, 384:384 + 2 * H], ones[0:2 * H, :], dmx_d[:, :], start=True, stop=True).then_inc(dtop_done, 1)
                    pe.wait_ge(ab_arg_ready, after(tb))

            schedule(pe, body)

    flag_batches(nc, ones, over_a, top_s, dtop, flags)
    general_layer1(nc, adj_t, xh_dram, a_src, a_dst, bias1, gamma1, beta1,
                   out.rearrange("b (t p) (h e) -> (b t) p h e", p=P, h=H), ident, eps, flags)
    keep.close()


def flag_batches(nc, ones, over_a, top_s, dtop, flags):
    TILES, B = over_a.shape[1], dtop.shape[1]
    with ExitStack() as ctx:
        empty = ctx.enter_context(nc.sbuf_tensor("empty", [P, TILES], f32))
        parts = ctx.enter_context(nc.sbuf_tensor("parts", [1, 3, B], f32))
        ps = ctx.enter_context(nc.psum_tensor("ps_flags", [P, 512], f32))
        empty_ready = ctx.enter_context(nc.semaphore("empty_ready"))
        sums_done = ctx.enter_context(nc.semaphore("sums_done"))
        dv_flags = ctx.enter_context(nc.semaphore("dv_flags"))
        block = ctx.enter_context(nc.Block())

        @block.vector
        def _(dve):
            V = nc.vector
            V.tensor_scalar(empty[:, :], top_s[:, :], 0.0, None, ALU.is_equal).then_inc(empty_ready, 1)
            dve.wait_ge(sums_done, 1)
            for k in range(2):
                V.tensor_reduce(parts[:, k, :], ps[0:1, k * TILES:(k + 1) * TILES].rearrange("p (b t) -> p b t", b=B),
                                AX.X, ALU.max)
            V.tensor_reduce(parts[:, 2, :], dtop[0:1, :, :, :].rearrange("p b a h -> p b (a h)"), AX.X,
                            ALU.max).then_inc(dv_flags, 1)
            dve.wait_ge(dv_flags, 1)
            V.tensor_scalar(parts[:, 0:2, :], parts[:, 0:2, :], 0.5, None, ALU.is_gt)
            V.tensor_scalar(parts[:, 2, :], parts[:, 2, :], EDMAX, None, ALU.is_gt).then_inc(dv_flags, 1)
            dve.wait_ge(dv_flags, 2)
            V.tensor_reduce(flags[:, :], parts[:, :, :].rearrange("p k b -> p b k"), AX.X, ALU.max)

        @block.tensor
        def _(pe):
            pe.wait_ge(empty_ready, 1)
            nc.tensor.matmul(ps[0:1, 0:TILES], ones[:, 0:1], over_a[:, :], start=True, stop=True)
            nc.tensor.matmul(ps[0:1, TILES:2 * TILES], ones[:, 0:1], empty[:, :], start=True,
                             stop=True).then_inc(sums_done, 1)


def general_layer1(nc, adj_t, xh_dram, a_src, a_dst, bias1, gamma1, beta1, out_t, ident, eps, flags):
    H, T, HO = a_src.shape
    N = adj_t.shape[2]
    B = flags.shape[1]
    NT = N // P
    NQ = NT // QT
    UNITS = H * NT
    xh_t = xh_dram.rearrange("q i p h a e -> (q i) p h a e")
    ed_dram = nc.dram_tensor("e_dst_rows", (T, N), f32, kind="Internal").ap()
    with ExitStack() as ctx:
        def sb(name, shape, dt=f32):
            return ctx.enter_context(nc.sbuf_tensor("g_" + name, shape, dt))

        def sem(name):
            return ctx.enter_context(nc.semaphore("g_" + name))

        a_sb = sb("a_sb", [P, 2, H, T, HO])
        bias_b, gamma_b, beta_b = (sb(n, [P, H, HO]) for n in ("bias", "gamma", "beta"))
        hh = sb("hh", [P, NT, HO])
        prod = sb("prod", [P, T, HO])
        es = sb("es", [P, NT, T])
        ed = sb("ed", [P, NT, T])
        edT = sb("edT", [T, N])
        ed_b = sb("ed_b", [P, T, N])
        adj_sb = sb("adj", [P, N], i32)
        s = sb("s", [P, 2, N])
        w = sb("w", [P, N])
        z = sb("z", [P, N])
        pr = sb("pr", [P, N])
        prT = sb("prT", [P, 4, P])
        nmx = sb("nmx", [P, 1])
        den = sb("den", [P, 1])
        rden = sb("rden", [P, 1])
        xh = sb("xh", [P, 2, HO])
        o = sb("o", [P, 6, HO])
        st, mv, sd, rs = sb("st", [P, 6]), sb("mv", [P, 2]), sb("sd", [P, 1]), sb("rs", [P, 1])
        ps_t = ctx.enter_context(nc.psum_tensor("g_ps_t", [P, 4, P], f32))
        ps_e = ctx.enter_context(nc.psum_tensor("g_ps_e", [P, 512], f32))
        ps_o = ctx.enter_context(nc.psum_tensor("g_ps_o", [P, 512], f32))

        consts_loaded = sem("consts_loaded")
        hh_loaded, ed_ready, ed_T_done, edT_ready = (sem(n) for n in ("hh_loaded", "ed_ready", "ed_T_done", "edT_ready"))
        ed_written, ed_b_loaded = sem("ed_written"), sem("ed_b_loaded")
        adj_loaded, xh_loaded, out_written = sem("adj_loaded"), sem("xh_loaded"), sem("out_written")
        s_ready, s_used = sem("s_ready"), sem("s_used")
        w_ready, exp_done = sem("w_ready"), sem("exp_done")
        T_done, prT_ready, mm_done = sem("T_done"), sem("prT_ready"), sem("mm_done")
        var_ready, sqrt_ready, out_ready = sem("var_ready"), sem("sqrt_ready"), sem("out_ready")
        held, chain = sem("held"), sem("chain")
        compute = [ed_ready, ed_T_done, edT_ready, s_ready, s_used, w_ready, exp_done, T_done, prT_ready, mm_done,
                   var_ready, sqrt_ready, out_ready]
        by_dma = [hh_loaded, ed_written, ed_b_loaded, adj_loaded, xh_loaded, out_written]
        arrived, reset_done, left = sem("arrived"), sem("reset_done"), sem("left")
        block = ctx.enter_context(nc.Block())

        def give_credits(sp):
            for x in compute:
                sp.sem_inc(x, 1)
            for x in by_dma:
                sp.sem_inc(x, 16)

        def hold(eng):
            eng.sem_inc(held, 1)

        def each_flagged(eng, head, unit):
            with eng.Fori(0, B) as b:
                flag = eng.value_load(flags[0:1, bass.ds(b, 1)], min_val=0, max_val=1)
                with eng.If(flag > 0):
                    for h in range(H):
                        head(b, h)
                        with eng.Fori(0, NT) as t:
                            unit(b, h, t, h * NT + t)
                    if eng is nc.sync:
                        eng.wait_ge(arrived, 3)
                        eng.sem_clear(arrived)
                        for x in compute + by_dma:
                            eng.sem_clear(x)
                        give_credits(eng)
                        eng.sem_inc(reset_done, 1)
                        eng.wait_ge(left, 3)
                        eng.sem_clear(reset_done)
                        eng.sem_clear(left)
                    else:
                        eng.sem_inc(arrived, 1)
                        eng.wait_ge(reset_done, 1)
                        eng.sem_inc(left, 1)

        @block.sync
        def _(sp):
            give_credits(sp)
            for k, a in enumerate((a_src, a_dst)):
                sp.dma_start(a_sb[:, k], spread(a, 0, P)).then_inc(consts_loaded, 16)
            for dst, src in ((bias_b, bias1), (gamma_b, gamma1), (beta_b, beta1)):
                sp.dma_start(dst[:, :, :], spread(src, 0, P)).then_inc(consts_loaded, 16)

            def head(b, h):
                sp.wait_ge(out_ready, 1 + h * NT)
                sp.dma_start(hh[:, :, :], xh_t[bass.ds(b * NT, NT), :, h, 1, :].rearrange("t p e -> p t e")
                             ).then_inc(hh_loaded, 16)
                sp.wait_ge(edT_ready, 1 + (h + 1) * NQ)
                sp.dma_start(ed_dram, edT[:, :]).then_inc(ed_written, 16)
                sp.wait_ge(ed_written, 16 + 16 * (h + 1))
                sp.dma_start(ed_b[:, :, :], spread(ed_dram, 0, P)).then_inc(ed_b_loaded, 16)
                sp.wait_ge(ed_b_loaded, 16 + 16 * (h + 1))
                hold(sp)

            def unit(b, h, t, u):
                sp.wait_ge(out_ready, 1 + u)
                sp.dma_start(adj_sb[:, :], adj_t[b * NT + t]).then_inc(adj_loaded, 16)
                sp.dma_start(xh[:, :, :], xh_t[b * NT + t, :, h]).then_inc(xh_loaded, 16)
                sp.wait_ge(out_ready, 1 + u + 1)
                sp.dma_start(out_t[b * NT + t, :, h, :], o[:, 5, :]).then_inc(out_written, 16)
                sp.wait_ge(out_written, 16 + 16 * (u + 1))
                hold(sp)

            each_flagged(sp, head, unit)

        @block.scalar
        def _(act):
            A = nc.scalar

            def head(b, h):
                for q in range(NQ):
                    act.wait_ge(ed_T_done, 1 + h * NQ + q + 1)
                    act.wait_ge(ed_b_loaded, 16 + 16 * h)
                    A.activation(edT[:, q * QT * P:(q + 1) * QT * P], ps_e[0:T, :], ACT.Copy).then_inc(edT_ready, 1)

            def unit(b, h, t, u):
                act.wait_ge(ed_b_loaded, 16 + 16 * (h + 1))
                for k in range(T):
                    if k >= 2:
                        act.wait_ge(s_used, 1 + u * T + k - 1)
                    else:
                        act.wait_ge(s_used, 1 + u * T)
                    A.activation(s[:, k % 2, :], ed_b[:, k, :], ACT.Identity, bias=es[:, bass.ds(t, 1), k]
                                 ).then_inc(s_ready, 1)
                act.wait_ge(w_ready, 1 + u + 1)
                act.wait_ge(T_done, 1 + 4 * u)
                A.activation(pr[:, :], w[:, :], ACT.Exp, bias=nmx[:, :], accum_out=den[:, :]).then_inc(exp_done, 1)
                for k in range(4):
                    act.wait_ge(T_done, 1 + 4 * u + k + 1)
                    act.wait_ge(mm_done, 1 + 4 * u + k)
                    A.activation(prT[:, :, :], ps_t[:, :, :], ACT.Copy).then_inc(prT_ready, 1)
                act.wait_ge(var_ready, 1 + u + 1)
                A.activation(sd[:, :], mv[:, 1:2], ACT.Sqrt, bias=eps[:, 1:2]).then_inc(sqrt_ready, 1)

            each_flagged(act, head, unit)

        @block.tensor
        def _(pe):
            M = nc.tensor

            def head(b, h):
                pe.wait_ge(ed_ready, 1 + h + 1)
                for q in range(NQ):
                    pe.wait_ge(edT_ready, 1 + h * NQ + q)
                    for k in range(QT):
                        last = M.transpose(ps_e[0:T, k * P:(k + 1) * P], ed[:, q * QT + k, :], ident[:, :])
                    last.then_inc(ed_T_done, 1)

            def unit(b, h, t, u):
                pe.wait_ge(exp_done, 1 + u + 1)
                pe.wait_ge(var_ready, 1 + u)
                for k in range(4):
                    pe.wait_ge(prT_ready, 1 + 4 * u + k)
                    for j in range(4):
                        last = M.transpose(ps_t[:, j, :], pr[:, (4 * k + j) * P:(4 * k + j + 1) * P], ident[:, :])
                    last.then_inc(T_done, 1)
                    pe.wait_ge(prT_ready, 1 + 4 * u + k + 1)
                    for j in range(4):
                        last = M.matmul(ps_o[:, 0:HO], prT[:, j, :], hh[:, 4 * k + j, :], start=(k + j == 0),
                                        stop=(k == 3 and j == 3))
                    last.then_inc(mm_done, 1)

            each_flagged(pe, head, unit)

        @block.vector
        def _(dve):
            V = nc.vector
            dve.wait_ge(consts_loaded, 16 * 5)

            c = Chain(dve, chain, hold)

            def head(b, h):
                dve.wait_ge(hh_loaded, 16 + 16 * (h + 1))
                c.start()
                for t in range(NT):
                    for k, dst in enumerate((es, ed)):
                        c.link(V.tensor_tensor(prod[:, :, :], a_sb[:, k, h], spread(hh[:, t, :], 1, T), ALU.mult))
                        if t == NT - 1 and k == 1:
                            V.tensor_reduce(dst[:, t, :], prod[:, :, :], AX.X, ALU.add).then_inc(ed_ready, 1)
                        else:
                            c.link(V.tensor_reduce(dst[:, t, :], prod[:, :, :], AX.X, ALU.add))

            def unit(b, h, t, u):
                dve.wait_ge(adj_loaded, 16 + 16 * (u + 1))
                c.start()
                for k in range(T):
                    dve.wait_ge(s_ready, 1 + u * T + k + 1)
                    V.scalar_tensor_tensor(z[:, :] if k else w[:, :], adj_sb[:, :], float(k + 1), s[:, k % 2, :],
                                           ALU.is_equal, ALU.mult).then_inc(s_used, 1)
                    if k:
                        dve.wait_ge(s_used, 1 + u * T + k + 1)
                        c.link(V.tensor_tensor(w[:, :], w[:, :], z[:, :], ALU.add))
                c.link(V.scalar_tensor_tensor(w[:, :], w[:, :], SLOPE, w[:, :], ALU.mult, ALU.max))
                c.link(V.tensor_scalar(z[:, :], adj_sb[:, :], 0.0, NEG, ALU.is_equal, ALU.mult))
                c.link(V.tensor_tensor(w[:, :], w[:, :], z[:, :], ALU.add))
                V.tensor_reduce(nmx[:, :], w[:, :], AX.X, ALU.max, negate=True).then_inc(w_ready, 1)
                dve.wait_ge(exp_done, 1 + u + 1)
                c.link(V.reciprocal(rden[:, :], den[:, :]))
                dve.wait_ge(mm_done, 1 + 4 * (u + 1))
                dve.wait_ge(xh_loaded, 16 + 16 * (u + 1))
                c.link(V.scalar_tensor_tensor(o[:, 0, :], ps_o[:, 0:HO], rden[:, :], bias_b[:, h, :], ALU.mult, ALU.add))
                c.link(V.scalar_tensor_tensor(o[:, 1, :], o[:, 0, :], 0.0, xh[:, 1, :], ALU.max, ALU.add))
                c.link(V.bn_stats(st[:, :], o[:, 1, :]))
                V.bn_aggr(mv[:, :], st[:, :]).then_inc(var_ready, 1)
                dve.wait_ge(sqrt_ready, 1 + u + 1)
                c.link(V.reciprocal(rs[:, :], sd[:, :]))
                c.link(V.tensor_scalar(o[:, 2, :], o[:, 1, :], mv[:, 0:1], rs[:, :], ALU.subtract, ALU.mult))
                c.link(V.tensor_tensor(o[:, 3, :], o[:, 2, :], gamma_b[:, h, :], ALU.mult))
                c.link(V.tensor_tensor(o[:, 4, :], o[:, 3, :], beta_b[:, h, :], ALU.add))
                dve.wait_ge(out_written, 16 + 16 * u)
                V.tensor_tensor(o[:, 5, :], o[:, 4, :], xh[:, 0, :], ALU.add).then_inc(out_ready, 1)

            each_flagged(dve, head, unit)


_INS = ["x", "adj", "L0_gnn_W", "L0_gnn_b", "L1_gnn_W", "L1_gnn_a_src", "L1_gnn_a_dst", "L1_gnn_bias",
        "L1_gnn_ln_gamma", "L1_gnn_ln_beta"]


def kernel(**inputs):
    import numpy as _np
    import concourse.bacc as _bacc
    from concourse import mybir as _mybir
    from concourse.bass_utils import run_bass_kernel_spmd as _run

    nc = _bacc.Bacc("TRN2", target_bir_lowering=False, num_devices=1)
    arrays, args = {}, []
    for name in _INS:
        a = _np.ascontiguousarray(inputs[name])
        arrays[f"in_{name}_dram"] = a
        args.append(nc.dram_tensor(f"in_{name}_dram", a.shape, _mybir.dt.from_np(a.dtype), kind="ExternalInput").ap())
    shape = inputs["x"].shape
    args.append(nc.dram_tensor("out_0_dram", shape, _mybir.dt.float32, kind="ExternalOutput").ap())
    gnn_two_layers(nc, *args)
    r = _run(nc, [arrays], core_ids=[0])
    return r.results[0]["out_0_dram"]
```

```python
import concourse.bass as bass
from concourse import mybir
from contextlib import ExitStack

f32 = mybir.dt.float32
bf16 = mybir.dt.bfloat16
f8 = mybir.dt.float8e4
i32 = mybir.dt.int32
u32 = mybir.dt.uint32
u8 = mybir.dt.uint8
ALU = mybir.AluOpType
ACT = mybir.ActivationFunctionType
AX = mybir.AxisListType

P = 128
QT = 4
CREDIT = 8
S = 25
GROUPS = [9, 8, 8]
EPS0 = 1e-5
EPS1 = 1e-6
SLOPE = 0.01
BIG = 2.0 ** 100
EDMAX = 30.0
NEG = -1e9
TINY = 1e-37


def spread(ap, dim, n):
    shape = list(ap.shape)
    return ap.unsqueeze(dim).broadcast_to(shape[:dim] + [n] + shape[dim:])


class Chain:

    def __init__(self, eng, sem, hold):
        self.eng, self.sem, self.n, self.hold = eng, sem, 0, hold

    def start(self):
        self.hold(self.eng)
        self.eng.sem_clear(self.sem)
        self.n = 0

    def link(self, ins):
        self.n += 1
        ins.then_inc(self.sem, 1)
        self.eng.wait_ge(self.sem, self.n)


def gnn_two_layers(nc, x, adj, W0, b0, W1, a_src, a_dst, bias1, gamma1, beta1, out):
    B, N, C = x.shape
    H, D, HO = W1.shape
    T = a_src.shape[1]
    NT = N // P
    NQ = NT // QT
    TILES = B * NT
    IQ = QT * P
    KC = C // P
    PARTS = 3
    FW = PARTS * (HO + 1)
    GW = 8
    NG = N // GW
    ZROW = B * N
    ZEROS = 16 * B
    assert NQ == 4 and QT == H and H * HO == C and S == sum(GROUPS)

    x_t = x.rearrange("b (t p) c -> (b t) p c", p=P)
    adj_t = adj.rearrange("b (t p) j -> (b t) p j", p=P)
    out_q = out.rearrange("b (q i p) (h e) -> (b q) p i h e", i=QT, p=P, h=H)

    h0_dram = nc.dram_tensor("h0_rows", (B * N + 1, C), f32, kind="Internal").ap()
    at_dram = nc.dram_tensor("adjacency_transposed", (TILES, P, NT * P), u8, kind="Internal").ap()
    es_dram = nc.dram_tensor("e_src_rows", (B * NQ, H, IQ), f32, kind="Internal").ap()
    f_dram = nc.dram_tensor("weighted_features", (TILES, P, H, 2 * FW), bf16, kind="Internal").ap()
    xh_dram = nc.dram_tensor("x1_and_h", (B * NQ, QT, P, H, 2, HO), f32, kind="Internal").ap()
    h0_t = h0_dram[0:B * N, :].rearrange("(t p) c -> t p c", p=P)

    keep = ExitStack()
    ident = keep.enter_context(nc.sbuf_tensor("ident", [P, P], f32))
    ones = keep.enter_context(nc.sbuf_tensor("ones", [P, P], f32))
    eps = keep.enter_context(nc.sbuf_tensor("eps", [P, 2], f32))
    over_a = keep.enter_context(nc.sbuf_tensor("over_a", [P, TILES], f32))
    top_s = keep.enter_context(nc.sbuf_tensor("top_s", [P, TILES], f32))
    dtop = keep.enter_context(nc.sbuf_tensor("dtop", [P, B, 2, H], f32))
    flags = keep.enter_context(nc.sbuf_tensor("flags", [1, B], i32))

    ctx = ExitStack()
    with ctx:
        def sb(name, shape, dt=f32):
            return ctx.enter_context(nc.sbuf_tensor(name, shape, dt))

        def pb(name, shape, dt=f32):
            return ctx.enter_context(nc.psum_tensor(name, shape, dt))

        sems, dma_sems = [], []

        def sem(name):
            sems.append(ctx.enter_context(nc.semaphore(name)))
            return sems[-1]

        def pair(name):
            two = [ctx.enter_context(nc.semaphore(f"{name}{k}")) for k in range(2)]
            dma_sems.extend(two)
            return two

        ident_b = sb("ident_b", [P, P], bf16)
        group_desc = sb("group_desc", [P, NG])
        bit_mask = sb("bit_mask", [P, GW], i32)
        bit_pos = sb("bit_pos", [P, GW], i32)
        pack = sb("pack", [P, P // GW], bf16)
        rank8 = sb("rank8", [P, 1])
        row_end = sb("row_end", [P, TILES])
        row_zero = sb("row_zero", [P, TILES])
        W0_sb = sb("W0_sb", [P, 2 * KC, C])
        W1_sb = sb("W1_sb", [P, KC, C + 2 * H])
        b0_row = sb("b0_row", [1, C])
        a_sb = sb("a_sb", [P, 2, H, HO])
        a_prod = sb("a_prod", [P, 2, H, HO])
        bias_b = sb("bias_b", [P, H, HO])
        gamma_b = sb("gamma_b", [P, H, HO])
        beta_b = sb("beta_b", [P, H, HO])
        xp = sb("xp", [P, 2, C])
        h0s = sb("h0s", [P, 2, C])
        p_st = sb("p_st", [P, 6])
        p_mv = sb("p_mv", [P, 2])
        p_sd = sb("p_sd", [P, 1])
        p_rn = sb("p_rn", [P, 2, 2])
        adj_sb = sb("adj_sb", [P, N], i32)
        adj_b = sb("adj_b", [P, N], bf16)
        at_st = sb("at_st", [P, 2, NT * P], f8)
        code = sb("code", [P, 2, NG])
        code_top = sb("code_top", [P, 32])
        code_int = sb("code_int", [P, 32], i32)
        first8 = sb("first8", [P, 32], i32)
        bits = sb("bits", [P, 32, GW], i32)
        cand_v = sb("cand_v", [P, 32, GW])
        cand = sb("cand", [P, 2, 32 * GW])
        score = sb("score", [P, 32])
        zero_fix = sb("zero_fix", [P, 32])
        idx = sb("idx", [P, QT, 32], i32)
        g = sb("g", [P, 2, GROUPS[0], C])
        aggp = sb("aggp", [P, len(GROUPS), C])
        cat = sb("cat", [P, 2 * KC, P])
        xr = sb("xr", [P, 2, C])
        catT = sb("catT", [P, 2 * KC, P])
        xh = sb("xh", [P, 2, H, 2, HO])
        l_st = sb("l_st", [P, 6])
        l_mv = sb("l_mv", [P, 2])
        l_sd = sb("l_sd", [P, 1])
        l_rn = sb("l_rn", [P, 2])
        h1 = sb("h1", [P, C])
        h1T = sb("h1T", [P, KC, P])
        es_row = sb("es_row", [H, 2, P])
        esed = sb("esed", [P, NT, 2, H])
        uf = sb("uf", [P, 2, H, HO + 1])
        f_st = sb("f_st", [P, 2, H, 2, PARTS, HO + 1], bf16)
        at_q = sb("at_q", [P, QT, NT, P], u8)
        es_b = sb("es_b", [P, 2, IQ])
        ed_big = sb("ed_big", [P, NT, H])
        F = sb("F", [P, NT, H, 2 * FW], bf16)
        sign = sb("sign", [P, 2, 4, IQ], u8)
        BC = sb("BC", [P, 2, 2, NT, IQ], u8)
        dmx = sb("dmx", [P, 2, H])
        dmx_t = sb("dmx_t", [2 * H, 1])
        dmx_d = sb("dmx_d", [2 * H, 2 * H])
        srow = sb("srow", [P, NT, H])
        mrow = sb("mrow", [P, NT, H])
        ab_arg = sb("ab_arg", [P, 2, NT, H])
        ab = sb("ab", [P, 2, NT, H])
        vb = sb("vb", [P, 2, FW])
        wb = sb("wb", [P, FW])
        oraw = sb("oraw", [P, QT, HO + 1])
        xhr = sb("xhr", [P, 2, QT, 2, HO])
        rden = sb("rden", [P, QT])
        o1 = sb("o1", [P, QT, HO])
        o_st = sb("o_st", [P, QT, 6])
        o_mv = sb("o_mv", [P, QT, 2])
        o_sd = sb("o_sd", [P, QT])
        o_rs = sb("o_rs", [P, QT])
        o2 = sb("o2", [P, QT, HO])
        outs = sb("outs", [P, 2, QT, HO])
        sum_a = sb("sum_a", [P, 2])
        cnt_a = sb("cnt_a", [P, 2])

        ps_A = pb("ps_A", [P, N], bf16)
        ps_cat = pb("ps_cat", [P, 2 * KC, P])
        ps_x = pb("ps_x", [P, 2, C])
        ps_h = pb("ps_h", [P, 512])
        ps_k = pb("ps_k", [P, 512])
        ps_o = [pb(f"ps_o{k}", [P, 512]) for k in range(2)]

        consts_loaded = ctx.enter_context(nc.semaphore("consts_loaded"))
        consts_made = ctx.enter_context(nc.semaphore("consts_made"))
        weights_ready = ctx.enter_context(nc.semaphore("weights_ready"))
        zeros_written = ctx.enter_context(nc.semaphore("zeros_written"))
        held = ctx.enter_context(nc.semaphore("held"))
        credits_given = ctx.enter_context(nc.semaphore("credits_given"))
        xp_loaded = pair("xp_loaded")
        h0_written = pair("h0_written")
        adj_loaded = ctx.enter_context(nc.semaphore("adj_loaded"))
        at_written = pair("at_written")
        gathered = [ctx.enter_context(nc.semaphore(f"gathered{k}")) for k in range(2)]
        cat_loaded = ctx.enter_context(nc.semaphore("cat_loaded"))
        xr_loaded = pair("xr_loaded")
        xh_written = pair("xh_written")
        es_written = pair("es_written")
        f_written = pair("f_written")
        at_q_loaded = [ctx.enter_context(nc.semaphore(f"at_q_loaded{k}")) for k in range(4)]
        es_b_loaded = pair("es_b_loaded")
        F_loaded = [ctx.enter_context(nc.semaphore(f"F_loaded{h}")) for h in range(H)]
        xhr_loaded = pair("xhr_loaded")
        out_written = pair("out_written")
        p_var = sem("p_var")
        p_sqrt = sem("p_sqrt")
        p_norm = sem("p_norm")
        h0_ready = sem("h0_ready")
        adj_b_ready = sem("adj_b_ready")
        A_T_done = sem("A_T_done")
        at_ready = sem("at_ready")
        codes_done = sem("codes_done")
        codes_read = sem("codes_read")
        idx_ready = sem("idx_ready")
        group_reduced = sem("group_reduced")
        agg_ready = sem("agg_ready")
        cat_T_done = sem("cat_T_done")
        catT_ready = sem("catT_ready")
        x1_done = sem("x1_done")
        x1_ready = sem("x1_ready")
        l_var = sem("l_var")
        l_sqrt = sem("l_sqrt")
        l_norm = sem("l_norm")
        h1_ready = sem("h1_ready")
        h1_T_done = sem("h1_T_done")
        h1T_ready = sem("h1T_ready")
        wh_done = sem("wh_done")
        wh_ready = sem("wh_ready")
        es_row_ready = sem("es_row_ready")
        exps_ready = sem("exps_ready")
        esed_ready = sem("esed_ready")
        uf_ready = sem("uf_ready")
        hi_ready = sem("hi_ready")
        rest_ready = sem("rest_ready")
        mid_ready = sem("mid_ready")
        rest2_ready = sem("rest2_ready")
        f_ready = sem("f_ready")
        sign_ready = sem("sign_ready")
        bc_ready = sem("bc_ready")
        acc_done = sem("acc_done")
        half_ready = sem("half_ready")
        acc_read = sem("acc_read")
        o_var = sem("o_var")
        o_sqrt = sem("o_sqrt")
        out_ready = sem("out_ready")
        dmx_ready = sem("dmx_ready")
        dmx_T_done = sem("dmx_T_done")
        dmx_d_ready = sem("dmx_d_ready")
        dtop_done = sem("dtop_done")
        ed_big_ready = sem("ed_big_ready")
        ab_arg_ready = sem("ab_arg_ready")
        ab_ready = sem("ab_ready")
        dv_prep = ctx.enter_context(nc.semaphore("dv_prep"))
        dv_idx = ctx.enter_context(nc.semaphore("dv_idx"))
        dv_l0 = ctx.enter_context(nc.semaphore("dv_l0"))
        dv_l1 = ctx.enter_context(nc.semaphore("dv_l1"))
        dv_batch = ctx.enter_context(nc.semaphore("dv_batch"))
        dv_const = ctx.enter_context(nc.semaphore("dv_const"))

        fills, filled = [0, 0], {}
        for i in range(QT):
            for k, size in enumerate(GROUPS):
                slot = (len(GROUPS) * i + k) % 2
                fills[slot] += 16 * size
                filled[i, k] = (slot, fills[slot])
        assert QT * len(GROUPS) % 2 == 0

        def after(k):
            return k + CREDIT

        def landed(n, i, more):
            return 16 + 8 * (n + i - i % 2 + more)

        def hold(eng):
            eng.sem_inc(held, 1)

        LAG = {"prep": 0, "prep_store": 1,
               "idx": 16, "at_store": 17,
               "gather": 17, "l0a": 18,
               "l0b": 19, "l0_store": 20,
               "mask": 35, "att": 36, "out_store": 37}

        class At:

            def __init__(self, stage, tb, q, i):
                lag = LAG[stage]
                self.i = (i - lag) % QT
                back = (i - lag - self.i) // QT
                self.n = tb * NT + q * QT + back * QT
                self.Q = tb * NQ + q + back
                shift = back % NQ - (NQ if back % NQ else 0)
                self.qb = (q + shift) % NQ if isinstance(q, int) else q + shift

        def active(stage, t0, t1):
            has = {0 <= t - LAG[stage] < TILES for t in (t0, t1)}
            assert len(has) == 1
            return has.pop()

        def schedule(eng, body):
            def stages(tb, qs):
                out = []
                for i in range(QT):
                    times = [tb * NT + q * QT + i for q in qs]
                    out.append(frozenset(x for x in LAG if active(x, times[0], times[-1])))
                return tuple(out)

            spans = []
            for tb in range(B + 3):
                what = (stages(tb, [0]), stages(tb, [1]), stages(tb, [2, 3]))
                if spans and spans[-1][2] == what:
                    spans[-1][1] = tb + 1
                else:
                    spans.append([tb, tb + 1, what])
            for lo, hi, (first, second, rest) in spans:
                def run(tb):
                    if any(first):
                        body(tb, 0, first)
                    if any(second):
                        body(tb, 1, second)
                    if any(rest):
                        with eng.Fori(2, NQ) as q:
                            body(tb, q, rest)
                if hi - lo == 1:
                    run(lo)
                else:
                    with eng.Fori(lo, hi) as tb:
                        run(tb)

        def tiles(lo, count=1):
            return slice(lo, lo + count) if isinstance(lo, int) else bass.ds(lo, count)

        def ends_batch(q, i, stages):
            return isinstance(q, int) and q == 0 and i == 2 and "l0b" in stages[2]

        block = ctx.enter_context(nc.Block())

        @block.sync
        def _(sp):
            for s in sems:
                sp.sem_inc(s, CREDIT)
            for s in dma_sems:
                sp.sem_inc(s, 16)
            sp.sem_inc(credits_given, 1)
            sp.wait_ge(consts_made, 1)
            sp.dma_start(h0_dram[B * N:B * N + 1, :], g[0:1, 0, 0, :]).then_inc(zeros_written, 16)
            if B > 1:
                later = h0_dram[N:B * N, :].rearrange("(p r) c -> p r c", p=P)
                for k in range(0, later.shape[1], NT):
                    sp.dma_start(later[:, k:k + NT, :],
                                 g[:, :, :, :].rearrange("p a s c -> p (a s) c")[:, 0:NT, :]).then_inc(zeros_written, 16)
            sp.dma_start(W0_sb[:, :, :], W0.rearrange("(k p) o -> p k o", p=P)).then_inc(consts_loaded, 16)
            for h in range(H):
                sp.dma_start(W1_sb[:, :, h * HO:(h + 1) * HO],
                             W1[h].rearrange("(k p) e -> p k e", p=P)).then_inc(consts_loaded, 16)
            sp.dma_start(b0_row[:, :], b0.rearrange("(a c) -> a c", a=1)).then_inc(consts_loaded, 16)
            for k, a in enumerate((a_src, a_dst)):
                sp.dma_start(a_sb[:, k, :, :], spread(a[:, 0, :], 0, P)
                             ).then_inc(consts_loaded, 16)
            for dst, src in ((bias_b, bias1), (gamma_b, gamma1), (beta_b, beta1)):
                sp.dma_start(dst[:, :, :], spread(src, 0, P)).then_inc(consts_loaded, 16)

            def prep_load(n, i):
                sp.wait_ge(h0_ready, after(n + i - 1))
                sp.dma_start(xp[:, i % 2, :], x_t[n + i]).then_inc(xp_loaded[i % 2], 16)

            def prep_store(n, i):
                sp.wait_ge(h0_ready, after(n + i + 1))
                sp.wait_ge(zeros_written, ZEROS)
                sp.dma_start(h0_t[n + i], h0s[:, i % 2, :]).then_inc(h0_written[i % 2], 16)

            def adj_load(n, i):
                sp.wait_ge(adj_b_ready, after(n + i))
                sp.dma_start(adj_sb[:, :], adj_t[n + i]).then_inc(adj_loaded, 16)

            def at_store(n, i):
                sp.wait_ge(at_ready, after(n + i + 1))
                sp.dma_start(at_dram[n + i], at_st[:, i % 2, :].bitcast(u8)).then_inc(at_written[i % 2], 16)

            def l0_load(n, i):
                sp.wait_ge(cat_T_done, after(n + i))
                sp.dma_start(cat[:, 0:KC, :].rearrange("p k c -> p (k c)"), h0_t[n + i]).then_inc(cat_loaded, 16)
                sp.wait_ge(x1_ready, after(n + i - 1))
                sp.dma_start(xr[:, i % 2, :], x_t[n + i]).then_inc(xr_loaded[i % 2], 16)

            def l0_store(n, Q, i):
                sp.wait_ge(es_row_ready, after(n + i + 1))
                sp.dma_start(es_dram[Q, :, i * P:(i + 1) * P], es_row[:, i % 2, :]).then_inc(es_written[i % 2], 16)
                sp.wait_ge(wh_ready, after(n + i + 1))
                sp.dma_start(xh_dram[Q, i].rearrange("p h a e -> p (h a e)"),
                             xh[:, i % 2].rearrange("p h a e -> p (h a e)")).then_inc(xh_written[i % 2], 16)

            def f_store(n, i):
                sp.wait_ge(f_ready, after(n + i + 1))
                sp.dma_start(f_dram[n + i].rearrange("p h f -> p (h f)"),
                             f_st[:, i % 2].rearrange("p h a r e -> p (h a r e)")).then_inc(f_written[i % 2], 16)

            def es_load(n, Q, i):
                sp.wait_ge(sign_ready, after((n + i - 1) * 4))
                if i == 0:
                    for w in es_written:
                        sp.wait_ge(w, 16 + 8 * (n + QT))
                sp.dma_start(es_b[:, i % 2, :], spread(es_dram[Q, i], 0, P)).then_inc(es_b_loaded[i % 2], 16)

            def xh_load(n, Q, i):
                sp.wait_ge(out_ready, after(n + i - 1))
                if i == 0:
                    for w in xh_written:
                        sp.wait_ge(w, 16 + 8 * (n + QT))
                sp.dma_start(xhr[:, i % 2].rearrange("p i a e -> p i (a e)"),
                             xh_dram[Q, :, :, i].rearrange("i p a e -> p i (a e)")).then_inc(xhr_loaded[i % 2], 16)

            def at_load(n, k):
                sp.wait_ge(bc_ready, after((n - 1) * 4 + k + 1))
                hold(sp)
                for w in at_written:
                    sp.wait_ge(w, 16 + 8 * (n + QT))
                    hold(sp)
                sp.dma_start(at_q[:, :, 4 * k:4 * k + 4, :],
                             at_dram[tiles(n, QT), :, 4 * k * P:4 * (k + 1) * P].rearrange("t p (j i) -> p t j i", i=P)
                             ).then_inc(at_q_loaded[k], 16)

            def F_load(tb, h):
                if not (isinstance(tb, int) and tb == 2):
                    sp.wait_ge(acc_done, after(((tb - 2) * NT - QT + h + 1) * QT))
                sp.dma_start(F[:, :, h, :], f_dram[tiles((tb - 2) * NT, NT), :, h, :].rearrange("t p f -> p t f")
                             ).then_inc(F_loaded[h], 16)

            def body(tb, q, stages):
                for i, on in enumerate(stages):
                    at = {x: At(x, tb, q, i) for x in on}
                    if "prep" in on:
                        prep_load(at["prep"].n, at["prep"].i)
                    if "idx" in on:
                        adj_load(at["idx"].n, at["idx"].i)
                    if "mask" in on:
                        es_load(at["mask"].n, at["mask"].Q, at["mask"].i)
                    if "att" in on:
                        xh_load(at["att"].n, at["att"].Q, at["att"].i)
                    if "prep_store" in on:
                        prep_store(at["prep_store"].n, at["prep_store"].i)
                    if "l0_store" in on:
                        l0_store(at["l0_store"].n, at["l0_store"].Q, at["l0_store"].i)
                    if "at_store" in on:
                        at_store(at["at_store"].n, at["at_store"].i)
                    if "gather" in on:
                        l0_load(at["gather"].n, at["gather"].i)
                    if "out_store" in on:
                        a = at["out_store"]
                        sp.wait_ge(out_ready, after(a.n + a.i + 1))
                        sp.dma_start(out_q[a.Q, :, :, a.i, :], outs[:, a.i % 2]).then_inc(out_written[a.i % 2], 16)
                    if "l0_store" in on:
                        f_store(at["l0_store"].n, at["l0_store"].i)
                    if i == 2 and "mask" in stages[3]:
                        for k in range(4):
                            at_load(tb * NT + q * QT - 2 * NT, k)
                    if ends_batch(q, i - 1, stages):
                        for w in f_written:
                            sp.wait_ge(w, 16 + 16 * (NT // 2) * (tb - 1))
                        for h in range(H - 1):
                            F_load(tb, h)
                    if isinstance(q, int) and q == 1 and i == 0 and "att" in on:
                        F_load(tb, H - 1)

            schedule(sp, body)
            for k in range(2):
                sp.wait_ge(out_written[k], 16 + 16 * TILES // 2)

        @block.gpsimd
        def _(pool):
            pool.memset(ident[:, :], 0.0)
            pool.memset(ident_b[:, :], 0.0)
            pool.memset(ones[:, :], 1.0)
            pool.memset(eps[:, 0:1], EPS0)
            pool.memset(eps[:, 1:2], EPS1)
            pool.memset(g[:, :, :, :], 0.0).then_inc(consts_made, 1)
            pool.wait_ge(consts_made, 1)
            pool.affine_select(out=ident[:, :], in_=ident[:, :], compare_op=ALU.not_equal, fill=1.0, base=0,
                               pattern=[[-1, P]], channel_multiplier=1)
            pool.affine_select(out=ident_b[:, :], in_=ident_b[:, :], compare_op=ALU.not_equal, fill=1.0, base=0,
                               pattern=[[-1, P]], channel_multiplier=1)
            pool.iota(group_desc[:, :], [[-256, NG]], base=256 * NG, channel_multiplier=0,
                      allow_small_or_imprecise_dtypes=True)
            pool.iota(bit_pos[:, :], [[1, GW]], base=0, channel_multiplier=0)
            for k in range(GW):
                pool.memset(bit_mask[:, k:k + 1], 2 ** (GW - 1 - k))
            pool.iota(row_end[:, :], [[N, B], [0, NT]], base=N, channel_multiplier=0,
                      allow_small_or_imprecise_dtypes=True)
            pool.iota(row_zero[:, :], [[-N, B], [0, NT]], base=ZROW - N, channel_multiplier=0,
                      allow_small_or_imprecise_dtypes=True)
            pool.memset(pack[:, :], 0.0).then_inc(consts_made, 1)
            pool.wait_ge(consts_made, 2)
            for k in range(GW):
                pool.affine_select(out=pack[:, :], in_=pack[:, :], compare_op=ALU.not_equal,
                                   fill=float(2 ** (GW - 1 - k)), base=-k, pattern=[[-GW, P // GW]],
                                   channel_multiplier=1).then_inc(consts_made, 1)
                pool.wait_ge(consts_made, 3 + k)
            pool.wait_ge(zeros_written, ZEROS)
            pool.wait_ge(consts_loaded, 16 * 11)
            pool.wait_ge(credits_given, 1)
            pool.nop().then_inc(consts_made, 1)

            def gather(n, i):
                pool.wait_ge(idx_ready, after(n + i + 1))
                for k, size in enumerate(GROUPS):
                    slot = filled[i, k][0]
                    pool.wait_ge(group_reduced, after((n + i) * len(GROUPS) + k - 1))
                    hold(pool)
                    for s in range(size):
                        nth = sum(GROUPS[:k]) + s
                        pool.indirect_dma_start(
                            g[:, slot, s, :], None, h0_dram,
                            bass.IndirectOffsetOnAxis(ap=idx[:, i, nth:nth + 1], axis=0)).then_inc(gathered[slot], 16)

            def body(tb, q, stages):
                for i, on in enumerate(stages):
                    if "gather" in on:
                        a = At("gather", tb, q, i)
                        if isinstance(q, int) and i < 2:
                            for w in h0_written:
                                pool.wait_ge(w, 16 + 16 * (NT // 2) * (tb - 1 if q == 0 and i == 0 else tb))
                        gather(a.n, a.i)

            schedule(pool, body)

        @block.scalar
        def _(act):
            act.wait_ge(consts_made, 3 + GW)

            def prep_sqrt(n, i):
                act.wait_ge(p_var, after(n + i + 1))
                nc.scalar.activation(p_sd[:, :], p_mv[:, 1:2], ACT.Sqrt, bias=eps[:, 0:1]).then_inc(p_sqrt, 1)

            def prep_relu(n, i):
                act.wait_ge(p_norm, after(n + i + 1))
                act.wait_ge(h0_written[i % 2], landed(n, i, 0))
                nc.scalar.activation(h0s[:, i % 2, :], xp[:, i % 2, :], ACT.Relu, bias=p_rn[:, i % 2, 1:2],
                                     scale=p_rn[:, i % 2, 0:1]).then_inc(h0_ready, 1)

            def adj_convert(n, i):
                act.wait_ge(adj_loaded, 16 * (n + i + 1))
                act.wait_ge(A_T_done, after(n + i))
                act.wait_ge(idx_ready, after(n + i - 1))
                nc.scalar.activation(adj_b[:, :], adj_sb[:, :].bitcast(u32), ACT.Copy,
                                     accum_out=sum_a[:, i % 2:i % 2 + 1]).then_inc(adj_b_ready, 1)

            def adj_transposed(n, i):
                act.wait_ge(A_T_done, after(n + i + 1))
                act.wait_ge(at_written[i % 2], landed(n, i, 0))
                act.wait_ge(codes_done, after(n + i - 1))
                hold(act)
                nc.scalar.activation(at_st[:, i % 2, :], ps_A[:, :], ACT.Sign,
                                     accum_out=cnt_a[:, i % 2:i % 2 + 1], saturate=False).then_inc(at_ready, 1)

            def cat_evacuate(n, i):
                act.wait_ge(cat_T_done, after(n + i + 1))
                act.wait_ge(x1_done, after(n + i))
                nc.scalar.activation(catT[:, :, :], ps_cat[:, :, :], ACT.Copy).then_inc(catT_ready, 1)

            def l0_sqrt(n, i):
                act.wait_ge(l_var, after(n + i + 1))
                nc.scalar.activation(l_sd[:, :], l_mv[:, 1:2], ACT.Sqrt, bias=eps[:, 0:1]).then_inc(l_sqrt, 1)

            def l0_relu(n, i):
                act.wait_ge(l_norm, after(n + i + 1))
                act.wait_ge(h1_T_done, after(n + i))
                nc.scalar.activation(h1[:, :].rearrange("p (h e) -> p h e", h=H), xh[:, i % 2, :, 0, :], ACT.Relu,
                                     bias=l_rn[:, 1:2], scale=l_rn[:, 0:1]).then_inc(h1_ready, 1)

            def h1_evacuate(n, i):
                act.wait_ge(h1_T_done, after(n + i + 1))
                act.wait_ge(wh_done, after(n + i))
                nc.scalar.activation(h1T[:, :, :].rearrange("p k c -> p (k c)"), ps_x[:, 1, :], ACT.Copy).then_inc(h1T_ready, 1)

            def wh_evacuate(n, qb, i):
                act.wait_ge(wh_done, after(n + i + 1))
                act.wait_ge(f_ready, after(n + i))
                nc.scalar.activation(uf[:, 0, :, HO], ps_h[:, C + H:C + 2 * H], ACT.Exp)
                nc.scalar.activation(uf[:, 1, :, HO], ps_h[:, C + H:C + 2 * H], ACT.Exp, scale=SLOPE).then_inc(exps_ready, 1)
                act.wait_ge(xh_written[i % 2], landed(n, i, 0))
                nc.scalar.activation(xh[:, i % 2, :, 1, :], ps_h[:, 0:C].rearrange("p (h e) -> p h e", h=H),
                                     ACT.Copy).then_inc(wh_ready, 1)
                nc.scalar.activation(esed[:, tiles(qb * QT + i), :, :],
                                     ps_h[:, C:C + 2 * H].rearrange("p (o a h) -> p o a h", o=1, a=2),
                                     ACT.Copy).then_inc(esed_ready, 1)
                act.wait_ge(es_written[i % 2], landed(n, i, 0))
                nc.scalar.activation(es_row[:, i % 2, :], ps_h[0:H, 384:512], ACT.Copy).then_inc(es_row_ready, 1)

            def part(n, i, r):
                if r == 0:
                    act.wait_ge(f_written[i % 2], landed(n, i, 0))
                act.wait_ge((uf_ready, rest_ready, rest2_ready)[r], after(n + i + 1))
                nc.scalar.activation(f_st[:, i % 2, :, :, r, :].rearrange("p h a e -> p a h e"), uf[:, :, :, :],
                                     ACT.Copy).then_inc((hi_ready, mid_ready, f_ready)[r], 1)

            def signs(n, i, k):
                if k == 0:
                    act.wait_ge(es_b_loaded[i % 2], landed(n, i, 2))
                act.wait_ge(bc_ready, after((n + i) * 4 + k - 1))
                for j in range(4):
                    jc = 4 * k + j
                    last = nc.scalar.activation(sign[:, k % 2, j, :], es_b[:, i % 2, :], ACT.Relu,
                                                bias=ed_big[:, jc, i:i + 1], scale=BIG)
                last.then_inc(sign_ready, 1)

            def scale_acc(n, qb, h, it):
                act.wait_ge(acc_done, after((n + h) * 4 + it + 1))
                act.wait_ge(acc_read, after((n + h) * 4 + it - 1))
                nc.scalar.activation(vb[:, it % 2, :], ps_o[it % 2][:, 0:FW], ACT.Copy,
                                     scale=ab[:, 0, tiles(qb * QT + it), h]).then_inc(half_ready, 1)

            def body(tb, q, stages):
                for i, on in enumerate(stages):
                    at = {x: At(x, tb, q, i) for x in on}
                    p, x, m, t = at.get("prep"), at.get("idx"), at.get("mask"), at.get("att")
                    a, b = at.get("l0a"), at.get("l0b")
                    if ends_batch(q, i - 1, stages):
                        act.wait_ge(ab_arg_ready, after(tb - 1))
                    if m:
                        signs(m.n, m.i, 0)
                    if a:
                        cat_evacuate(a.n, a.i)
                    if x:
                        adj_convert(x.n, x.i)
                    if t:
                        scale_acc(t.n, t.qb, t.i, 0)
                    if b:
                        h1_evacuate(b.n, b.i)
                    if m:
                        signs(m.n, m.i, 1)
                    if p:
                        prep_sqrt(p.n, p.i)
                    if a:
                        l0_sqrt(a.n, a.i)
                    if t:
                        scale_acc(t.n, t.qb, t.i, 1)
                    if p:
                        prep_relu(p.n, p.i)
                    if a:
                        l0_relu(a.n, a.i)
                    if x:
                        adj_transposed(x.n, x.i)
                    if m:
                        signs(m.n, m.i, 2)
                    if b:
                        wh_evacuate(b.n, b.qb, b.i)
                    if t:
                        scale_acc(t.n, t.qb, t.i, 2)
                    if m:
                        signs(m.n, m.i, 3)
                    if t:
                        scale_acc(t.n, t.qb, t.i, 3)
                    if b:
                        part(b.n, b.i, 0)
                    if t:
                        act.wait_ge(o_var, after(t.n + t.i + 1))
                        nc.scalar.activation(o_sd[:, :], o_mv[:, :, 1], ACT.Sqrt, bias=eps[:, 1:2]).then_inc(o_sqrt, 1)
                    if b:
                        part(b.n, b.i, 1)
                        part(b.n, b.i, 2)
                    if ends_batch(q, i - 1, stages):
                        act.wait_ge(acc_read, after((tb - 2) * NT * 4))
                        nc.scalar.activation(ab[:, :, :, :], ab_arg[:, :, :, :], ACT.Exp).then_inc(ab_ready, 1)
                        act.wait_ge(ab_ready, after(tb - 1))

            schedule(act, body)

        @block.vector
        def _(dve):
            V = nc.vector
            c0 = Chain(dve, dv_const, hold)
            c0.start()
            dve.wait_ge(consts_made, 3 + GW)
            for k in range(KC):
                for a in range(2):
                    c0.link(V.tensor_tensor(a_prod[:, a, :, :], W1_sb[:, k, 0:C].rearrange("p (h e) -> p h e", h=H),
                                            a_sb[:, a, :, :], ALU.mult))
                    c0.link(V.tensor_reduce(W1_sb[:, k, C + a * H:C + (a + 1) * H], a_prod[:, a, :, :], AX.X, ALU.add))
            V.memset(esed[:, 0, :, :], 0.0).then_inc(weights_ready, 1)

            ch_prep, ch_idx, ch_l0 = Chain(dve, dv_prep, hold), Chain(dve, dv_idx, hold), Chain(dve, dv_l0, hold)
            ch_l1, ch_b = Chain(dve, dv_l1, hold), Chain(dve, dv_batch, hold)

            def prep_a(n, i):
                dve.wait_ge(xp_loaded[i % 2], landed(n, i, 2))
                ch_prep.start()
                dve.wait_ge(p_sqrt, after(n + i))
                ch_prep.link(V.bn_stats(p_st[:, :], xp[:, i % 2, :]))
                V.bn_aggr(p_mv[:, :], p_st[:, :]).then_inc(p_var, 1)

            def prep_b(n, i):
                dve.wait_ge(p_sqrt, after(n + i + 1))
                dve.wait_ge(h0_ready, after(n + i - 1))
                ch_prep.link(V.reciprocal(p_rn[:, i % 2, 0:1], p_sd[:, :]))
                V.scalar_tensor_tensor(p_rn[:, i % 2, 1:2], p_mv[:, 0:1], -1.0, p_rn[:, i % 2, 0:1], ALU.mult,
                                       ALU.mult).then_inc(p_norm, 1)

            def top32(chain, dst, buf):
                for r in range(4):
                    chain.link(V.max(dst[:, 8 * r:8 * r + 8], buf[:, r % 2, :]))
                    if r < 3:
                        chain.link(V.match_replace(buf[:, 1 - r % 2, :], dst[:, 8 * r:8 * r + 8], buf[:, r % 2, :], 0.0))

            def find(n, i):
                ch_idx.start()
                dve.wait_ge(codes_done, after(n + i + 1))
                ch_idx.link(V.scalar_tensor_tensor(code[:, 1, :], ps_k[:, 0:NG], 0.0, group_desc[:, :], ALU.is_gt, ALU.mult))
                V.tensor_tensor(code[:, 0, :], code[:, 1, :], ps_k[:, 0:NG], ALU.add).then_inc(codes_read, 1)
                dve.wait_ge(codes_read, after(n + i + 1))
                hold(dve)
                top32(ch_idx, code_top, code)
                ch_idx.link(V.tensor_copy(code_int[:, :], code_top[:, :]))
                V.tensor_scalar(first8[:, :], code_int[:, :], 8, 3, ALU.logical_shift_right, ALU.logical_shift_left)
                ch_idx.link(V.tensor_tensor(bits[:, :, :], spread(code_int[:, :], 2, GW),
                                            spread(bit_mask[:, :], 1, 32), ALU.bitwise_and))
                ch_idx.link(V.tensor_tensor(cand_v[:, :, :], spread(first8[:, :], 2, GW),
                                            spread(bit_pos[:, :], 1, 32), ALU.subtract))
                ch_idx.link(V.scalar_tensor_tensor(cand[:, 0, :].rearrange("p (s k) -> p s k", k=GW), bits[:, :, :], 0.0,
                                                   cand_v[:, :, :], ALU.is_gt, ALU.mult))
                top32(ch_idx, score, cand)
                V.tensor_copy(top_s[:, tiles(n + i)], score[:, 0:1])
                V.tensor_tensor(over_a[:, tiles(n + i)], sum_a[:, i % 2:i % 2 + 1], cnt_a[:, i % 2:i % 2 + 1],
                                ALU.subtract)
                ch_idx.link(V.tensor_scalar(zero_fix[:, :], score[:, :], 0.0, row_zero[:, tiles(n + i)],
                                            ALU.is_equal, ALU.mult))
                ch_idx.link(V.scalar_tensor_tensor(zero_fix[:, :], score[:, :], -1.0, zero_fix[:, :], ALU.mult, ALU.add))
                V.tensor_scalar(idx[:, i, :], zero_fix[:, :], row_end[:, tiles(n + i)], None, ALU.add).then_inc(idx_ready, 1)

            def reduce_group(n, Q, i, k):
                slot, count = filled[i, k]
                dve.wait_ge(gathered[slot], Q * fills[slot] + count)
                if k == 0:
                    dve.wait_ge(agg_ready, after(n + i))
                V.tensor_reduce(aggp[:, k, :], g[:, slot, 0:GROUPS[k], :].rearrange("p s c -> p c s"), AX.X,
                                ALU.max).then_inc(group_reduced, 1)

            def aggregate(n, i):
                dve.wait_ge(group_reduced, after((n + i + 1) * len(GROUPS)))
                dve.wait_ge(cat_T_done, after(n + i))
                V.tensor_reduce(cat[:, KC:, :].rearrange("p k c -> p (k c)"), aggp[:, :, :].rearrange("p s c -> p c s"),
                                AX.X, ALU.max).then_inc(agg_ready, 1)

            def l0_x1(n, i):
                dve.wait_ge(x1_done, after(n + i + 1))
                dve.wait_ge(xr_loaded[i % 2], landed(n, i, 2))
                dve.wait_ge(xh_written[i % 2], landed(n, i, 0))
                V.scalar_tensor_tensor(xh[:, i % 2, :, 0, :], ps_x[:, 0, :].rearrange("p (h e) -> p h e", h=H), 0.0,
                                       xr[:, i % 2, :].rearrange("p (h e) -> p h e", h=H), ALU.max,
                                       ALU.add).then_inc(x1_ready, 1)
                dve.wait_ge(x1_ready, after(n + i + 1))
                ch_l0.start()
                ch_l0.link(V.bn_stats(l_st[:, :], xh[:, i % 2, :, 0, :]))
                V.bn_aggr(l_mv[:, :], l_st[:, :]).then_inc(l_var, 1)

            def l0_norm(n, i):
                dve.wait_ge(l_sqrt, after(n + i + 1))
                dve.wait_ge(h1_ready, after(n + i))
                ch_l0.link(V.reciprocal(l_rn[:, 0:1], l_sd[:, :]))
                V.scalar_tensor_tensor(l_rn[:, 1:2], l_mv[:, 0:1], -1.0, l_rn[:, 0:1], ALU.mult,
                                       ALU.mult).then_inc(l_norm, 1)

            def features(n, i):
                dve.wait_ge(exps_ready, after(n + i + 1))
                dve.wait_ge(wh_ready, after(n + i + 1))
                for a in range(2):
                    last = V.tensor_tensor(uf[:, a, :, 0:HO], xh[:, i % 2, :, 1, :],
                                           spread(uf[:, a, :, HO], 2, HO), ALU.mult)
                last.then_inc(uf_ready, 1)

            def rest(n, i, r):
                dve.wait_ge((hi_ready, mid_ready)[r], after(n + i + 1))
                V.tensor_tensor(uf[:, :, :, :], uf[:, :, :, :], part_v(i, r), ALU.subtract
                                ).then_inc((rest_ready, rest2_ready)[r], 1)

            def part_v(i, r):
                return f_st[:, i % 2, :, :, r, :].rearrange("p h a e -> p a h e")

            def mask(n, Q, i, k):
                dve.wait_ge(sign_ready, after((n + i) * 4 + k + 1))
                if i == 0:
                    dve.wait_ge(at_q_loaded[k], 16 * (Q + 1))
                if k == 0:
                    dve.wait_ge(acc_done, after((n + i - 1) * 4))
                js = slice(4 * k, 4 * k + 4)
                a = at_q[:, :, js, :].bitcast(u32).rearrange("p t j w -> p j t w")
                b = BC[:, i % 2, 0, js, :].bitcast(u32).rearrange("p j (t w) -> p j t w", t=QT)
                c = BC[:, i % 2, 1, js, :].bitcast(u32).rearrange("p j (t w) -> p j t w", t=QT)
                s = sign[:, k % 2, :, :].bitcast(u32).rearrange("p j (t w) -> p j t w", t=QT)
                ch_l1.link(V.tensor_tensor(b, s, a, ALU.bitwise_and))
                V.tensor_tensor(c, a, b, ALU.bitwise_xor).then_inc(bc_ready, 1)

            def read_acc(n, qb, i, it):
                dve.wait_ge(half_ready, after((n + i) * 4 + it + 1))
                V.scalar_tensor_tensor(wb[:, :], ps_o[it % 2][:, FW:2 * FW], ab[:, 1, tiles(qb * QT + it), i],
                                       vb[:, it % 2, :], ALU.mult, ALU.add).then_inc(acc_read, 1)
                dve.wait_ge(acc_read, after((n + i) * 4 + it + 1))
                ch_l1.link(V.tensor_reduce(oraw[:, it, :], wb[:, :].rearrange("p (r e) -> p e r", r=PARTS), AX.X, ALU.add))

            def l1_norm(n, i):
                h = i
                ch_l1.link(V.tensor_scalar(rden[:, :], oraw[:, :, HO], TINY, None, ALU.max))
                ch_l1.link(V.reciprocal(rden[:, :], rden[:, :]))
                dve.wait_ge(xhr_loaded[i % 2], landed(n, i, 2))
                ch_l1.link(V.tensor_tensor(o1[:, :, :], oraw[:, :, 0:HO], spread(rden[:, :], 2, HO), ALU.mult))
                ch_l1.link(V.tensor_tensor(o1[:, :, :], o1[:, :, :], spread(bias_b[:, h, :], 1, QT), ALU.add))
                ch_l1.link(V.scalar_tensor_tensor(o1[:, :, :], o1[:, :, :], 0.0, xhr[:, i % 2, :, 1, :], ALU.max, ALU.add))
                for it in range(QT):
                    last = V.bn_stats(o_st[:, it, :], o1[:, it, :])
                ch_l1.link(last)
                for it in range(QT):
                    last = V.bn_aggr(o_mv[:, it, :], o_st[:, it, :])
                last.then_inc(o_var, 1)

            def l1_out(n, i):
                h = i
                dve.wait_ge(o_sqrt, after(n + i + 1))
                ch_l1.link(V.reciprocal(o_rs[:, :], o_sd[:, :]))
                for it in range(QT):
                    last = V.tensor_scalar(o2[:, it, :], o1[:, it, :], o_mv[:, it, 0:1], o_rs[:, it:it + 1],
                                           ALU.subtract, ALU.mult)
                ch_l1.link(last)
                ch_l1.link(V.tensor_tensor(o2[:, :, :], o2[:, :, :], spread(gamma_b[:, h, :], 1, QT), ALU.mult))
                ch_l1.link(V.tensor_tensor(o2[:, :, :], o2[:, :, :], spread(beta_b[:, h, :], 1, QT), ALU.add))
                dve.wait_ge(out_written[i % 2], landed(n, i, 0))
                V.tensor_tensor(outs[:, i % 2, :, :], o2[:, :, :], xhr[:, i % 2, :, 0, :], ALU.add).then_inc(out_ready, 1)

            def batch_end(b):
                ch_b.start()
                dve.wait_ge(esed_ready, after((b + 1) * NT))
                dve.wait_ge(sign_ready, after(b * NT * 4))
                ed = esed[:, :, 1, :]
                es = esed[:, :, 0, :]
                ch_b.link(V.tensor_scalar(ed_big[:, :, :], ed, BIG, None, ALU.mult))
                ch_b.link(V.tensor_reduce(dmx[:, 0, :], ed.rearrange("p t h -> p h t"), AX.X, ALU.max))
                ch_b.link(V.tensor_scalar(srow[:, :, :], ed, -1.0, None, ALU.mult))
                V.tensor_reduce(dmx[:, 1, :], srow[:, :, :].rearrange("p t h -> p h t"), AX.X, ALU.max).then_inc(dmx_ready, 1)
                dve.wait_ge(dmx_T_done, after(b + 1))
                ch_b.link(V.tensor_reduce(dmx_t[:, :], ps_k[0:2 * H, 256:256 + P], AX.X, ALU.max))
                V.tensor_scalar(dmx_d[:, :], ident[0:2 * H, 0:2 * H], dmx_t[:, :], None, ALU.mult).then_inc(dmx_d_ready, 1)
                dve.wait_ge(dtop_done, after(b + 1))
                dt = dtop[:, b, :, :] if isinstance(b, int) else dtop[:, bass.ds(b, 1), :, :].rearrange("p o a h -> p (o a) h")
                ch_b.link(V.tensor_copy(dt, ps_k[:, 384:384 + 2 * H].rearrange("p (a h) -> p a h", a=2)))
                ch_b.link(V.tensor_tensor(srow[:, :, :], es, spread(ps_k[:, 384:384 + H], 1, NT), ALU.add))
                ch_b.link(V.scalar_tensor_tensor(mrow[:, :, :], srow[:, :, :], SLOPE, srow[:, :, :], ALU.mult, ALU.max))
                ch_b.link(V.tensor_tensor(ab_arg[:, 0, :, :], es, mrow[:, :, :], ALU.subtract))
                V.scalar_tensor_tensor(ab_arg[:, 1, :, :], es, SLOPE, mrow[:, :, :], ALU.mult, ALU.subtract).then_inc(ab_arg_ready, 1)

            def body(tb, q, stages):
                for i, on in enumerate(stages):
                    at = {x: At(x, tb, q, i) for x in on}
                    p, x, m, t = at.get("prep"), at.get("idx"), at.get("mask"), at.get("att")
                    g_, a, b = at.get("gather"), at.get("l0a"), at.get("l0b")
                    if m or t:
                        ch_l1.start()
                    if p:
                        prep_a(p.n, p.i)
                    if m:
                        mask(m.n, m.Q, m.i, 0)
                    if t:
                        read_acc(t.n, t.qb, t.i, 0)
                    if a:
                        l0_x1(a.n, a.i)
                    if g_:
                        reduce_group(g_.n, g_.Q, g_.i, 0)
                    if p:
                        prep_b(p.n, p.i)
                    if m:
                        mask(m.n, m.Q, m.i, 1)
                    if t:
                        read_acc(t.n, t.qb, t.i, 1)
                    if a:
                        l0_norm(a.n, a.i)
                    if g_:
                        reduce_group(g_.n, g_.Q, g_.i, 1)
                    if m:
                        mask(m.n, m.Q, m.i, 2)
                    if t:
                        read_acc(t.n, t.qb, t.i, 2)
                    if x:
                        find(x.n, x.i)
                    if m:
                        mask(m.n, m.Q, m.i, 3)
                    if t:
                        read_acc(t.n, t.qb, t.i, 3)
                    if b:
                        features(b.n, b.i)
                    if t:
                        l1_norm(t.n, t.i)
                    if g_:
                        reduce_group(g_.n, g_.Q, g_.i, 2)
                        aggregate(g_.n, g_.i)
                    if b:
                        rest(b.n, b.i, 0)
                    if t:
                        l1_out(t.n, t.i)
                    if b:
                        rest(b.n, b.i, 1)
                    if ends_batch(q, i, stages):
                        batch_end(tb - 2)

            schedule(dve, body)

        @block.tensor
        def _(pe):
            M = nc.tensor
            pe.wait_ge(consts_made, 3 + GW)
            pe.wait_ge(weights_ready, 1)

            def adj_T(n, i):
                pe.wait_ge(adj_b_ready, after(n + i + 1))
                pe.wait_ge(at_ready, after(n + i))
                for j in range(NT):
                    last = M.transpose(ps_A[:, j * P:(j + 1) * P], adj_b[:, j * P:(j + 1) * P], ident_b[:, :])
                last.then_inc(A_T_done, 1)

            def codes(n, i):
                pe.wait_ge(at_ready, after(n + i + 1))
                pe.wait_ge(codes_read, after(n + i))
                hold(pe)
                w = P // GW
                for j in range(NT):
                    last = M.matmul(ps_k[:, j * w:(j + 1) * w], at_st[:, i % 2, j * P:(j + 1) * P], pack[:, :],
                                    start=True, stop=True)
                last.then_inc(codes_done, 1)

            def cat_T(n, i):
                pe.wait_ge(agg_ready, after(n + i + 1))
                pe.wait_ge(cat_loaded, 16 * (n + i + 1))
                pe.wait_ge(catT_ready, after(n + i))
                for k in range(2 * KC):
                    last = M.transpose(ps_cat[:, k, :], cat[:, k, :], ident[:, :])
                last.then_inc(cat_T_done, 1)

            def x1_mm(n, i):
                pe.wait_ge(catT_ready, after(n + i + 1))
                pe.wait_ge(x1_ready, after(n + i))
                pe.wait_ge(h1T_ready, after(n + i))
                for k in range(2 * KC):
                    M.matmul(ps_x[:, 0, :], catT[:, k, :], W0_sb[:, k, :], start=(k == 0), stop=False)
                M.matmul(ps_x[:, 0, :], ones[0:1, :], b0_row[:, :], start=False, stop=True).then_inc(x1_done, 1)

            def h1_T(n, i):
                pe.wait_ge(h1_ready, after(n + i + 1))
                pe.wait_ge(h1T_ready, after(n + i))
                pe.wait_ge(x1_ready, after(n + i + 1))
                for k in range(KC):
                    last = M.transpose(ps_x[:, 1, k * P:(k + 1) * P], h1[:, k * P:(k + 1) * P], ident[:, :])
                last.then_inc(h1_T_done, 1)

            def wh_mm(n, i):
                pe.wait_ge(h1T_ready, after(n + i + 1))
                pe.wait_ge(es_row_ready, after(n + i))
                pe.wait_ge(uf_ready, after(n + i))
                for k in range(KC):
                    M.matmul(ps_h[:, 0:C + 2 * H], h1T[:, k, :], W1_sb[:, k, :], start=(k == 0), stop=(k == KC - 1))
                for k in range(KC):
                    last = M.matmul(ps_h[0:H, 384:512], W1_sb[:, k, C:C + H], h1T[:, k, :], start=(k == 0),
                                    stop=(k == KC - 1))
                last.then_inc(wh_done, 1)

            def attend(b, n, i, it):
                h = i
                if it == 0:
                    pe.wait_ge(F_loaded[h], 16 * (b + 1))
                    pe.wait_ge(bc_ready, after((n + i + 1) * 4))
                pe.wait_ge(acc_read, after((n + i) * 4 + it - 1))
                hold(pe)
                for a in range(2):
                    for j in range(NT):
                        last = M.matmul(ps_o[it % 2][:, a * FW:(a + 1) * FW],
                                        BC[:, i % 2, a, j, it * P:(it + 1) * P].bitcast(f8),
                                        F[:, j, h, a * FW:(a + 1) * FW], start=(j == 0), stop=(j == NT - 1))
                last.then_inc(acc_done, 1)

            def maxima(b, codes_so_far):
                pe.wait_ge(codes_read, after(codes_so_far))
                pe.wait_ge(dmx_ready, after(b + 1))
                M.transpose(ps_k[0:2 * H, 256:256 + P], dmx[:, :, :].rearrange("p a h -> p (a h)"),
                            ident[:, :]).then_inc(dmx_T_done, 1)
                pe.wait_ge(dmx_d_ready, after(b + 1))
                M.matmul(ps_k[:, 384:384 + 2 * H], ones[0:2 * H, :], dmx_d[:, :], start=True, stop=True
                         ).then_inc(dtop_done, 1)

            def body(tb, q, stages):
                for i, on in enumerate(stages):
                    at = {x: At(x, tb, q, i) for x in on}
                    x, t, a, b = at.get("idx"), at.get("att"), at.get("l0a"), at.get("l0b")
                    ab_ = tb - 3 if isinstance(q, int) and q == 0 else tb - 2
                    if a:
                        cat_T(a.n, a.i)
                    if t:
                        attend(ab_, t.n, t.i, 0)
                    if b:
                        h1_T(b.n, b.i)
                    if a:
                        x1_mm(a.n, a.i)
                    if t:
                        attend(ab_, t.n, t.i, 1)
                    if x:
                        adj_T(x.n, x.i)
                    if b:
                        wh_mm(b.n, b.i)
                    if t:
                        attend(ab_, t.n, t.i, 2)
                    if x:
                        if ends_batch(q, i - 1, stages):
                            pe.wait_ge(ab_arg_ready, after(tb - 1))
                        codes(x.n, x.i)
                    if t:
                        attend(ab_, t.n, t.i, 3)
                    if ends_batch(q, i, stages):
                        maxima(tb - 2, x.n + x.i + 1 if x else TILES)

            schedule(pe, body)

    flag_batches(nc, ones, over_a, top_s, dtop, flags)
    general_layer1(nc, adj_t, xh_dram, a_src, a_dst, bias1, gamma1, beta1,
                   out.rearrange("b (t p) (h e) -> (b t) p h e", p=P, h=H), ident, eps, flags)
    keep.close()


def flag_batches(nc, ones, over_a, top_s, dtop, flags):
    TILES, B = over_a.shape[1], dtop.shape[1]
    with ExitStack() as ctx:
        empty = ctx.enter_context(nc.sbuf_tensor("empty", [P, TILES], f32))
        parts = ctx.enter_context(nc.sbuf_tensor("parts", [1, 3, B], f32))
        ps = ctx.enter_context(nc.psum_tensor("ps_flags", [P, 512], f32))
        empty_ready = ctx.enter_context(nc.semaphore("empty_ready"))
        sums_done = ctx.enter_context(nc.semaphore("sums_done"))
        dv_flags = ctx.enter_context(nc.semaphore("dv_flags"))
        block = ctx.enter_context(nc.Block())

        @block.vector
        def _(dve):
            V = nc.vector
            V.tensor_scalar(empty[:, :], top_s[:, :], 0.0, None, ALU.is_equal).then_inc(empty_ready, 1)
            dve.wait_ge(sums_done, 1)
            for k in range(2):
                V.tensor_reduce(parts[:, k, :], ps[0:1, k * TILES:(k + 1) * TILES].rearrange("p (b t) -> p b t", b=B),
                                AX.X, ALU.max)
            V.tensor_reduce(parts[:, 2, :], dtop[0:1, :, :, :].rearrange("p b a h -> p b (a h)"), AX.X,
                            ALU.max).then_inc(dv_flags, 1)
            dve.wait_ge(dv_flags, 1)
            V.tensor_scalar(parts[:, 0:2, :], parts[:, 0:2, :], 0.5, None, ALU.is_gt)
            V.tensor_scalar(parts[:, 2, :], parts[:, 2, :], EDMAX, None, ALU.is_gt).then_inc(dv_flags, 1)
            dve.wait_ge(dv_flags, 2)
            V.tensor_reduce(flags[:, :], parts[:, :, :].rearrange("p k b -> p b k"), AX.X, ALU.max)

        @block.tensor
        def _(pe):
            pe.wait_ge(empty_ready, 1)
            nc.tensor.matmul(ps[0:1, 0:TILES], ones[:, 0:1], over_a[:, :], start=True, stop=True)
            nc.tensor.matmul(ps[0:1, TILES:2 * TILES], ones[:, 0:1], empty[:, :], start=True,
                             stop=True).then_inc(sums_done, 1)


def general_layer1(nc, adj_t, xh_dram, a_src, a_dst, bias1, gamma1, beta1, out_t, ident, eps, flags):
    H, T, HO = a_src.shape
    N = adj_t.shape[2]
    B = flags.shape[1]
    NT = N // P
    NQ = NT // QT
    UNITS = H * NT
    xh_t = xh_dram.rearrange("q i p h a e -> (q i) p h a e")
    ed_dram = nc.dram_tensor("e_dst_rows", (T, N), f32, kind="Internal").ap()
    with ExitStack() as ctx:
        def sb(name, shape, dt=f32):
            return ctx.enter_context(nc.sbuf_tensor("g_" + name, shape, dt))

        def sem(name):
            return ctx.enter_context(nc.semaphore("g_" + name))

        a_sb = sb("a_sb", [P, 2, H, T, HO])
        bias_b, gamma_b, beta_b = (sb(n, [P, H, HO]) for n in ("bias", "gamma", "beta"))
        hh = sb("hh", [P, NT, HO])
        prod = sb("prod", [P, T, HO])
        es = sb("es", [P, NT, T])
        ed = sb("ed", [P, NT, T])
        edT = sb("edT", [T, N])
        ed_b = sb("ed_b", [P, T, N])
        adj_sb = sb("adj", [P, N], i32)
        s = sb("s", [P, 2, N])
        w = sb("w", [P, N])
        z = sb("z", [P, N])
        pr = sb("pr", [P, N])
        prT = sb("prT", [P, 4, P])
        nmx = sb("nmx", [P, 1])
        den = sb("den", [P, 1])
        rden = sb("rden", [P, 1])
        xh = sb("xh", [P, 2, HO])
        o = sb("o", [P, 6, HO])
        st, mv, sd, rs = sb("st", [P, 6]), sb("mv", [P, 2]), sb("sd", [P, 1]), sb("rs", [P, 1])
        ps_t = ctx.enter_context(nc.psum_tensor("g_ps_t", [P, 4, P], f32))
        ps_e = ctx.enter_context(nc.psum_tensor("g_ps_e", [P, 512], f32))
        ps_o = ctx.enter_context(nc.psum_tensor("g_ps_o", [P, 512], f32))

        consts_loaded = sem("consts_loaded")
        hh_loaded, ed_ready, ed_T_done, edT_ready = (sem(n) for n in ("hh_loaded", "ed_ready", "ed_T_done", "edT_ready"))
        ed_written, ed_b_loaded = sem("ed_written"), sem("ed_b_loaded")
        adj_loaded, xh_loaded, out_written = sem("adj_loaded"), sem("xh_loaded"), sem("out_written")
        s_ready, s_used = sem("s_ready"), sem("s_used")
        w_ready, exp_done = sem("w_ready"), sem("exp_done")
        T_done, prT_ready, mm_done = sem("T_done"), sem("prT_ready"), sem("mm_done")
        var_ready, sqrt_ready, out_ready = sem("var_ready"), sem("sqrt_ready"), sem("out_ready")
        held, chain = sem("held"), sem("chain")
        compute = [ed_ready, ed_T_done, edT_ready, s_ready, s_used, w_ready, exp_done, T_done, prT_ready, mm_done,
                   var_ready, sqrt_ready, out_ready]
        by_dma = [hh_loaded, ed_written, ed_b_loaded, adj_loaded, xh_loaded, out_written]
        arrived, reset_done, left = sem("arrived"), sem("reset_done"), sem("left")
        block = ctx.enter_context(nc.Block())

        def give_credits(sp):
            for x in compute:
                sp.sem_inc(x, 1)
            for x in by_dma:
                sp.sem_inc(x, 16)

        def hold(eng):
            eng.sem_inc(held, 1)

        def each_flagged(eng, head, unit):
            with eng.Fori(0, B) as b:
                flag = eng.value_load(flags[0:1, bass.ds(b, 1)], min_val=0, max_val=1)
                with eng.If(flag > 0):
                    for h in range(H):
                        head(b, h)
                        with eng.Fori(0, NT) as t:
                            unit(b, h, t, h * NT + t)
                    if eng is nc.sync:
                        eng.wait_ge(arrived, 3)
                        eng.sem_clear(arrived)
                        for x in compute + by_dma:
                            eng.sem_clear(x)
                        give_credits(eng)
                        eng.sem_inc(reset_done, 1)
                        eng.wait_ge(left, 3)
                        eng.sem_clear(reset_done)
                        eng.sem_clear(left)
                    else:
                        eng.sem_inc(arrived, 1)
                        eng.wait_ge(reset_done, 1)
                        eng.sem_inc(left, 1)

        @block.sync
        def _(sp):
            give_credits(sp)
            for k, a in enumerate((a_src, a_dst)):
                sp.dma_start(a_sb[:, k], spread(a, 0, P)).then_inc(consts_loaded, 16)
            for dst, src in ((bias_b, bias1), (gamma_b, gamma1), (beta_b, beta1)):
                sp.dma_start(dst[:, :, :], spread(src, 0, P)).then_inc(consts_loaded, 16)

            def head(b, h):
                sp.wait_ge(out_ready, 1 + h * NT)
                sp.dma_start(hh[:, :, :], xh_t[bass.ds(b * NT, NT), :, h, 1, :].rearrange("t p e -> p t e")
                             ).then_inc(hh_loaded, 16)
                sp.wait_ge(edT_ready, 1 + (h + 1) * NQ)
                sp.dma_start(ed_dram, edT[:, :]).then_inc(ed_written, 16)
                sp.wait_ge(ed_written, 16 + 16 * (h + 1))
                sp.dma_start(ed_b[:, :, :], spread(ed_dram, 0, P)).then_inc(ed_b_loaded, 16)
                sp.wait_ge(ed_b_loaded, 16 + 16 * (h + 1))
                hold(sp)

            def unit(b, h, t, u):
                sp.wait_ge(out_ready, 1 + u)
                sp.dma_start(adj_sb[:, :], adj_t[b * NT + t]).then_inc(adj_loaded, 16)
                sp.dma_start(xh[:, :, :], xh_t[b * NT + t, :, h]).then_inc(xh_loaded, 16)
                sp.wait_ge(out_ready, 1 + u + 1)
                sp.dma_start(out_t[b * NT + t, :, h, :], o[:, 5, :]).then_inc(out_written, 16)
                sp.wait_ge(out_written, 16 + 16 * (u + 1))
                hold(sp)

            each_flagged(sp, head, unit)

        @block.scalar
        def _(act):
            A = nc.scalar

            def head(b, h):
                for q in range(NQ):
                    act.wait_ge(ed_T_done, 1 + h * NQ + q + 1)
                    act.wait_ge(ed_b_loaded, 16 + 16 * h)
                    A.activation(edT[:, q * QT * P:(q + 1) * QT * P], ps_e[0:T, :], ACT.Copy).then_inc(edT_ready, 1)

            def unit(b, h, t, u):
                act.wait_ge(ed_b_loaded, 16 + 16 * (h + 1))
                for k in range(T):
                    if k >= 2:
                        act.wait_ge(s_used, 1 + u * T + k - 1)
                    else:
                        act.wait_ge(s_used, 1 + u * T)
                    A.activation(s[:, k % 2, :], ed_b[:, k, :], ACT.Identity, bias=es[:, bass.ds(t, 1), k]
                                 ).then_inc(s_ready, 1)
                act.wait_ge(w_ready, 1 + u + 1)
                act.wait_ge(T_done, 1 + 4 * u)
                A.activation(pr[:, :], w[:, :], ACT.Exp, bias=nmx[:, :], accum_out=den[:, :]).then_inc(exp_done, 1)
                for k in range(4):
                    act.wait_ge(T_done, 1 + 4 * u + k + 1)
                    act.wait_ge(mm_done, 1 + 4 * u + k)
                    A.activation(prT[:, :, :], ps_t[:, :, :], ACT.Copy).then_inc(prT_ready, 1)
                act.wait_ge(var_ready, 1 + u + 1)
                A.activation(sd[:, :], mv[:, 1:2], ACT.Sqrt, bias=eps[:, 1:2]).then_inc(sqrt_ready, 1)

            each_flagged(act, head, unit)

        @block.tensor
        def _(pe):
            M = nc.tensor

            def head(b, h):
                pe.wait_ge(ed_ready, 1 + h + 1)
                for q in range(NQ):
                    pe.wait_ge(edT_ready, 1 + h * NQ + q)
                    for k in range(QT):
                        last = M.transpose(ps_e[0:T, k * P:(k + 1) * P], ed[:, q * QT + k, :], ident[:, :])
                    last.then_inc(ed_T_done, 1)

            def unit(b, h, t, u):
                pe.wait_ge(exp_done, 1 + u + 1)
                pe.wait_ge(var_ready, 1 + u)
                for k in range(4):
                    pe.wait_ge(prT_ready, 1 + 4 * u + k)
                    for j in range(4):
                        last = M.transpose(ps_t[:, j, :], pr[:, (4 * k + j) * P:(4 * k + j + 1) * P], ident[:, :])
                    last.then_inc(T_done, 1)
                    pe.wait_ge(prT_ready, 1 + 4 * u + k + 1)
                    for j in range(4):
                        last = M.matmul(ps_o[:, 0:HO], prT[:, j, :], hh[:, 4 * k + j, :], start=(k + j == 0),
                                        stop=(k == 3 and j == 3))
                    last.then_inc(mm_done, 1)

            each_flagged(pe, head, unit)

        @block.vector
        def _(dve):
            V = nc.vector
            dve.wait_ge(consts_loaded, 16 * 5)

            c = Chain(dve, chain, hold)

            def head(b, h):
                dve.wait_ge(hh_loaded, 16 + 16 * (h + 1))
                c.start()
                for t in range(NT):
                    for k, dst in enumerate((es, ed)):
                        c.link(V.tensor_tensor(prod[:, :, :], a_sb[:, k, h], spread(hh[:, t, :], 1, T), ALU.mult))
                        if t == NT - 1 and k == 1:
                            V.tensor_reduce(dst[:, t, :], prod[:, :, :], AX.X, ALU.add).then_inc(ed_ready, 1)
                        else:
                            c.link(V.tensor_reduce(dst[:, t, :], prod[:, :, :], AX.X, ALU.add))

            def unit(b, h, t, u):
                dve.wait_ge(adj_loaded, 16 + 16 * (u + 1))
                c.start()
                for k in range(T):
                    dve.wait_ge(s_ready, 1 + u * T + k + 1)
                    V.scalar_tensor_tensor(z[:, :] if k else w[:, :], adj_sb[:, :], float(k + 1), s[:, k % 2, :],
                                           ALU.is_equal, ALU.mult).then_inc(s_used, 1)
                    if k:
                        dve.wait_ge(s_used, 1 + u * T + k + 1)
                        c.link(V.tensor_tensor(w[:, :], w[:, :], z[:, :], ALU.add))
                c.link(V.scalar_tensor_tensor(w[:, :], w[:, :], SLOPE, w[:, :], ALU.mult, ALU.max))
                c.link(V.tensor_scalar(z[:, :], adj_sb[:, :], 0.0, NEG, ALU.is_equal, ALU.mult))
                c.link(V.tensor_tensor(w[:, :], w[:, :], z[:, :], ALU.add))
                V.tensor_reduce(nmx[:, :], w[:, :], AX.X, ALU.max, negate=True).then_inc(w_ready, 1)
                dve.wait_ge(exp_done, 1 + u + 1)
                c.link(V.reciprocal(rden[:, :], den[:, :]))
                dve.wait_ge(mm_done, 1 + 4 * (u + 1))
                dve.wait_ge(xh_loaded, 16 + 16 * (u + 1))
                c.link(V.scalar_tensor_tensor(o[:, 0, :], ps_o[:, 0:HO], rden[:, :], bias_b[:, h, :], ALU.mult, ALU.add))
                c.link(V.scalar_tensor_tensor(o[:, 1, :], o[:, 0, :], 0.0, xh[:, 1, :], ALU.max, ALU.add))
                c.link(V.bn_stats(st[:, :], o[:, 1, :]))
                V.bn_aggr(mv[:, :], st[:, :]).then_inc(var_ready, 1)
                dve.wait_ge(sqrt_ready, 1 + u + 1)
                c.link(V.reciprocal(rs[:, :], sd[:, :]))
                c.link(V.tensor_scalar(o[:, 2, :], o[:, 1, :], mv[:, 0:1], rs[:, :], ALU.subtract, ALU.mult))
                c.link(V.tensor_tensor(o[:, 3, :], o[:, 2, :], gamma_b[:, h, :], ALU.mult))
                c.link(V.tensor_tensor(o[:, 4, :], o[:, 3, :], beta_b[:, h, :], ALU.add))
                dve.wait_ge(out_written, 16 + 16 * u)
                V.tensor_tensor(o[:, 5, :], o[:, 4, :], xh[:, 0, :], ALU.add).then_inc(out_ready, 1)

            each_flagged(dve, head, unit)


_INS = ["x", "adj", "L0_gnn_W", "L0_gnn_b", "L1_gnn_W", "L1_gnn_a_src", "L1_gnn_a_dst", "L1_gnn_bias",
        "L1_gnn_ln_gamma", "L1_gnn_ln_beta"]


def kernel(**inputs):
    import numpy as _np
    import concourse.bacc as _bacc
    from concourse import mybir as _mybir
    from concourse.bass_utils import run_bass_kernel_spmd as _run

    nc = _bacc.Bacc("TRN2", target_bir_lowering=False, num_devices=1)
    arrays, args = {}, []
    for name in _INS:
        a = _np.ascontiguousarray(inputs[name])
        arrays[f"in_{name}_dram"] = a
        args.append(nc.dram_tensor(f"in_{name}_dram", a.shape, _mybir.dt.from_np(a.dtype), kind="ExternalInput").ap())
    shape = inputs["x"].shape
    args.append(nc.dram_tensor("out_0_dram", shape, _mybir.dt.float32, kind="ExternalOutput").ap())
    gnn_two_layers(nc, *args)
    r = _run(nc, [arrays], core_ids=[0])
    return r.results[0]["out_0_dram"]
```

```python
import concourse.bass as bass
from concourse import mybir
from contextlib import ExitStack

f32 = mybir.dt.float32
bf16 = mybir.dt.bfloat16
f8 = mybir.dt.float8e4
i32 = mybir.dt.int32
u32 = mybir.dt.uint32
u8 = mybir.dt.uint8
ALU = mybir.AluOpType
ACT = mybir.ActivationFunctionType
AX = mybir.AxisListType

P = 128
QT = 4
CREDIT = 8
S = 25
GROUPS = [9, 8, 8]
EPS0 = 1e-5
EPS1 = 1e-6
SLOPE = 0.01
BIG = 2.0 ** 100
EDMAX = 30.0
NEG = -1e9
TINY = 1e-37


def spread(ap, dim, n):
    shape = list(ap.shape)
    return ap.unsqueeze(dim).broadcast_to(shape[:dim] + [n] + shape[dim:])


class Chain:

    def __init__(self, eng, sem, hold):
        self.eng, self.sem, self.n, self.hold = eng, sem, 0, hold

    def start(self):
        self.hold(self.eng)
        self.eng.sem_clear(self.sem)
        self.n = 0

    def step(self, ins):
        self.n += 1
        ins.then_inc(self.sem, 1)

    def ready(self):
        self.eng.wait_ge(self.sem, self.n)

    def link(self, ins):
        self.step(ins)
        self.ready()


def gnn_two_layers(nc, x, adj, W0, b0, W1, a_src, a_dst, bias1, gamma1, beta1, out):
    B, N, C = x.shape
    H, D, HO = W1.shape
    T = a_src.shape[1]
    NT = N // P
    NQ = NT // QT
    TILES = B * NT
    IQ = QT * P
    KC = C // P
    PARTS = 3
    FW = PARTS * (HO + 1)
    GW = 8
    NG = N // GW
    ZROW = B * N
    ZEROS = 16 * B
    assert NQ == 4 and QT == H and H * HO == C and S == sum(GROUPS)

    x_t = x.rearrange("b (t p) c -> (b t) p c", p=P)
    adj_t = adj.rearrange("b (t p) j -> (b t) p j", p=P)
    out_q = out.rearrange("b (q i p) (h e) -> (b q) p i h e", i=QT, p=P, h=H)

    h0_dram = nc.dram_tensor("h0_rows", (B * N + 1, C), f32, kind="Internal").ap()
    at_dram = nc.dram_tensor("adjacency_transposed", (TILES, P, NT * P), u8, kind="Internal").ap()
    es_dram = nc.dram_tensor("e_src_rows", (B * NQ, H, IQ), f32, kind="Internal").ap()
    f_dram = nc.dram_tensor("weighted_features", (TILES, P, H, 2 * FW), bf16, kind="Internal").ap()
    xh_dram = nc.dram_tensor("x1_and_h", (B * NQ, QT, P, H, 2, HO), f32, kind="Internal").ap()
    h0_t = h0_dram[0:B * N, :].rearrange("(t p) c -> t p c", p=P)

    keep = ExitStack()
    ident = keep.enter_context(nc.sbuf_tensor("ident", [P, P], f32))
    ones = keep.enter_context(nc.sbuf_tensor("ones", [P, P], f32))
    eps = keep.enter_context(nc.sbuf_tensor("eps", [P, 2], f32))
    over_a = keep.enter_context(nc.sbuf_tensor("over_a", [P, TILES], f32))
    top_s = keep.enter_context(nc.sbuf_tensor("top_s", [P, TILES], f32))
    dtop = keep.enter_context(nc.sbuf_tensor("dtop", [P, B, 2, H], f32))
    flags = keep.enter_context(nc.sbuf_tensor("flags", [1, B], i32))

    ctx = ExitStack()
    with ctx:
        def sb(name, shape, dt=f32):
            return ctx.enter_context(nc.sbuf_tensor(name, shape, dt))

        def pb(name, shape, dt=f32):
            return ctx.enter_context(nc.psum_tensor(name, shape, dt))

        sems, dma_sems = [], []

        def sem(name):
            sems.append(ctx.enter_context(nc.semaphore(name)))
            return sems[-1]

        def pair(name):
            two = [ctx.enter_context(nc.semaphore(f"{name}{k}")) for k in range(2)]
            dma_sems.extend(two)
            return two

        ident_b = sb("ident_b", [P, P], bf16)
        group_desc = sb("group_desc", [1, NG], bf16)
        ones_b = sb("ones_b", [1, P], bf16)
        bit_mask = sb("bit_mask", [P, GW], i32)
        bit_pos = sb("bit_pos", [P, GW], i32)
        pack = sb("pack", [P, P // GW], bf16)
        row_end = sb("row_end", [P, TILES])
        row_zero = sb("row_zero", [P, TILES])
        W0_sb = sb("W0_sb", [P, 2 * KC, C])
        W1_sb = sb("W1_sb", [P, KC, C + 2 * H])
        b0_row = sb("b0_row", [1, C])
        a_sb = sb("a_sb", [P, 2, H, HO])
        a_prod = sb("a_prod", [P, 2, H, HO])
        bias_b = sb("bias_b", [P, H, HO])
        gamma_b = sb("gamma_b", [P, H, HO])
        beta_b = sb("beta_b", [P, H, HO])
        xp = sb("xp", [P, 2, C])
        h0s = sb("h0s", [P, 2, C])
        p_st = sb("p_st", [P, 6])
        p_mv = sb("p_mv", [P, 2])
        p_sd = sb("p_sd", [P, 1])
        p_rn = sb("p_rn", [P, 2, 2])
        adj_sb = sb("adj_sb", [P, N], i32)
        adj_b = sb("adj_b", [P, N], bf16)
        at_st = sb("at_st", [P, 2, NT * P], f8)
        code = sb("code", [P, 2, NG])
        code_top = sb("code_top", [P, 32])
        code_int = sb("code_int", [P, 32], i32)
        first8 = sb("first8", [P, 32], i32)
        bits = sb("bits", [P, 32, GW], i32)
        cand_v = sb("cand_v", [P, 32, GW])
        cand = sb("cand", [P, 32 * GW])
        score = sb("score", [P, 32])
        zero_fix = sb("zero_fix", [P, 32])
        idx = sb("idx", [P, QT, 32], i32)
        g = sb("g", [P, 2, GROUPS[0], C])
        cat = sb("cat", [P, 2 * KC, P])
        xr = sb("xr", [P, 2, C])
        catT = sb("catT", [P, 2 * KC, P])
        xh = sb("xh", [P, 2, H, 2, HO])
        l_st = sb("l_st", [P, 6])
        l_mv = sb("l_mv", [P, 2])
        l_sd = sb("l_sd", [P, 1])
        l_rn = sb("l_rn", [P, 2])
        h1 = sb("h1", [P, C])
        h1T = sb("h1T", [P, KC, P])
        es_row = sb("es_row", [H, 2, P])
        esed = sb("esed", [P, NT, 2, H])
        uf = sb("uf", [P, 2, H, HO + 1])
        f_st = sb("f_st", [P, 2, H, 2, PARTS, HO + 1], bf16)
        at_q = sb("at_q", [P, QT, NT, P], u8)
        es_b = sb("es_b", [P, 2, IQ])
        ed_big = sb("ed_big", [P, NT, H])
        F = sb("F", [P, NT, H, 2 * FW], bf16)
        sign = sb("sign", [P, 2, 4, IQ], u8)
        BC = sb("BC", [P, 2, 2, NT, IQ], u8)
        dmx = sb("dmx", [P, 2, H])
        dmx_t = sb("dmx_t", [2 * H, 1])
        dmx_d = sb("dmx_d", [2 * H, 2 * H])
        srow = sb("srow", [P, NT, H])
        mrow = sb("mrow", [P, NT, H])
        ab_arg = sb("ab_arg", [P, 2, NT, H])
        ab = sb("ab", [P, 2, NT, H])
        vb = sb("vb", [P, 2, FW])
        wb = sb("wb", [P, QT, FW])
        oraw = sb("oraw", [P, QT, HO + 1])
        xhr = sb("xhr", [P, 2, QT, 2, HO])
        rden = sb("rden", [P, QT])
        o1 = sb("o1", [P, QT, HO])
        o_st = sb("o_st", [P, QT, 6])
        o_mv = sb("o_mv", [P, QT, 2])
        o_sd = sb("o_sd", [P, QT])
        o_rn = sb("o_rn", [P, 2, QT])
        o2 = sb("o2", [P, QT, HO])
        outs = sb("outs", [P, 2, QT, HO])
        sum_a = sb("sum_a", [P, 2])
        cnt_a = sb("cnt_a", [P, 2])

        ps_A = pb("ps_A", [P, N], bf16)
        ps_cat = pb("ps_cat", [P, 2 * KC, P])
        ps_x = pb("ps_x", [P, 2, C])
        ps_h = pb("ps_h", [P, 512])
        ps_k = pb("ps_k", [P, 2, NG])
        ps_o = [pb(f"ps_o{k}", [P, 512]) for k in range(2)]

        consts_loaded = ctx.enter_context(nc.semaphore("consts_loaded"))
        consts_made = ctx.enter_context(nc.semaphore("consts_made"))
        weights_ready = ctx.enter_context(nc.semaphore("weights_ready"))
        zeros_written = ctx.enter_context(nc.semaphore("zeros_written"))
        held = ctx.enter_context(nc.semaphore("held"))
        credits_given = ctx.enter_context(nc.semaphore("credits_given"))
        xp_loaded = pair("xp_loaded")
        h0_written = pair("h0_written")
        adj_loaded = ctx.enter_context(nc.semaphore("adj_loaded"))
        at_written = pair("at_written")
        gathered = [ctx.enter_context(nc.semaphore(f"gathered{k}")) for k in range(2)]
        cat_loaded = ctx.enter_context(nc.semaphore("cat_loaded"))
        xr_loaded = pair("xr_loaded")
        xh_written = pair("xh_written")
        es_written = pair("es_written")
        f_written = pair("f_written")
        at_q_loaded = [ctx.enter_context(nc.semaphore(f"at_q_loaded{k}")) for k in range(4)]
        es_b_loaded = pair("es_b_loaded")
        F_loaded = [ctx.enter_context(nc.semaphore(f"F_loaded{h}")) for h in range(H)]
        xhr_loaded = pair("xhr_loaded")
        out_written = pair("out_written")
        p_var = sem("p_var")
        p_sqrt = sem("p_sqrt")
        p_norm = sem("p_norm")
        h0_ready = sem("h0_ready")
        adj_b_ready = sem("adj_b_ready")
        A_T_done = sem("A_T_done")
        at_ready = sem("at_ready")
        codes_done = sem("codes_done")
        placed_ready = sem("placed_ready")
        codes_read = sem("codes_read")
        idx_ready = sem("idx_ready")
        group_reduced = sem("group_reduced")
        cat_T_done = sem("cat_T_done")
        catT_ready = sem("catT_ready")
        x1_done = sem("x1_done")
        x1_ready = sem("x1_ready")
        l_var = sem("l_var")
        l_sqrt = sem("l_sqrt")
        l_norm = sem("l_norm")
        h1_ready = sem("h1_ready")
        h1_T_done = sem("h1_T_done")
        h1T_ready = sem("h1T_ready")
        wh_done = sem("wh_done")
        wh_ready = sem("wh_ready")
        es_row_ready = sem("es_row_ready")
        exps_ready = sem("exps_ready")
        esed_ready = sem("esed_ready")
        uf_ready = sem("uf_ready")
        hi_ready = sem("hi_ready")
        rest_ready = sem("rest_ready")
        mid_ready = sem("mid_ready")
        rest2_ready = sem("rest2_ready")
        f_ready = sem("f_ready")
        sign_ready = sem("sign_ready")
        bc_ready = sem("bc_ready")
        acc_done = sem("acc_done")
        half_ready = sem("half_ready")
        acc_read = sem("acc_read")
        o_var = sem("o_var")
        o_sqrt = sem("o_sqrt")
        o_scale_ready = sem("o_scale_ready")
        o_norm = sem("o_norm")
        out_ready = sem("out_ready")
        dmx_ready = sem("dmx_ready")
        dmx_T_done = sem("dmx_T_done")
        dmx_d_ready = sem("dmx_d_ready")
        dtop_done = sem("dtop_done")
        ab_arg_ready = sem("ab_arg_ready")
        ab_ready = sem("ab_ready")
        dv_prep = ctx.enter_context(nc.semaphore("dv_prep"))
        dv_idx = ctx.enter_context(nc.semaphore("dv_idx"))
        dv_l0 = ctx.enter_context(nc.semaphore("dv_l0"))
        dv_mask = ctx.enter_context(nc.semaphore("dv_mask"))
        dv_l1 = ctx.enter_context(nc.semaphore("dv_l1"))
        dv_out = ctx.enter_context(nc.semaphore("dv_out"))
        dv_batch = ctx.enter_context(nc.semaphore("dv_batch"))
        dv_const = ctx.enter_context(nc.semaphore("dv_const"))

        fills, filled = [0, 0], {}
        for i in range(QT):
            for k, size in enumerate(GROUPS):
                slot = (len(GROUPS) * i + k) % 2
                fills[slot] += 16 * size
                filled[i, k] = (slot, fills[slot])
        assert QT * len(GROUPS) % 2 == 0

        def after(k):
            return k + CREDIT

        def landed(n, i, more):
            return 16 + 8 * (n + i - i % 2 + more)

        def hold(eng):
            eng.sem_inc(held, 1)

        LAG = {"prep": 0, "prep_store": 1,
               "idx": 16, "at_store": 17,
               "find": 17,
               "gather": 18, "l0a": 19,
               "l0b": 20, "l0_store": 21, "lo": 21,
               "sign": 35, "mask": 36,
               "att": 37, "out": 38, "out_store": 39}

        class At:

            def __init__(self, stage, tb, q, i):
                lag = LAG[stage]
                self.i = (i - lag) % QT
                back = (i - lag - self.i) // QT
                self.n = tb * NT + q * QT + back * QT
                self.Q = tb * NQ + q + back
                shift = back % NQ - (NQ if back % NQ else 0)
                self.qb = (q + shift) % NQ if isinstance(q, int) else q + shift

        def active(stage, t0, t1):
            has = {0 <= t - LAG[stage] < TILES for t in (t0, t1)}
            assert len(has) == 1
            return has.pop()

        def schedule(eng, body):
            def stages(tb, qs):
                out = []
                for i in range(QT):
                    times = [tb * NT + q * QT + i for q in qs]
                    out.append(frozenset(x for x in LAG if active(x, times[0], times[-1])))
                return tuple(out)

            spans = []
            for tb in range(B + 3):
                what = (stages(tb, [0]), stages(tb, [1]), stages(tb, [2, 3]))
                if spans and spans[-1][2] == what:
                    spans[-1][1] = tb + 1
                else:
                    spans.append([tb, tb + 1, what])
            for lo, hi, (first, second, rest) in spans:
                def run(tb):
                    if any(first):
                        body(tb, 0, first)
                    if any(second):
                        body(tb, 1, second)
                    if any(rest):
                        with eng.Fori(2, NQ) as q:
                            body(tb, q, rest)
                if hi - lo == 1:
                    run(lo)
                else:
                    with eng.Fori(lo, hi) as tb:
                        run(tb)

        def tiles(lo, count=1):
            return slice(lo, lo + count) if isinstance(lo, int) else bass.ds(lo, count)

        def ends_batch(q, i, stages):
            return isinstance(q, int) and (q, i) == (0, 3) and "l0b" in stages[3]

        def begins_batch(q, i, stages):
            return isinstance(q, int) and (q, i) == (1, 0) and "mask" in stages[0]

        block = ctx.enter_context(nc.Block())

        @block.sync
        def _(sp):
            for s in sems:
                sp.sem_inc(s, CREDIT)
            for s in dma_sems:
                sp.sem_inc(s, 16)
            sp.sem_inc(credits_given, 1)
            sp.wait_ge(consts_made, 1)
            sp.dma_start(h0_dram[B * N:B * N + 1, :], g[0:1, 0, 0, :]).then_inc(zeros_written, 16)
            sp.dma_start(W0_sb[:, :, :], W0.rearrange("(k p) o -> p k o", p=P)).then_inc(consts_loaded, 16)
            for h in range(H):
                sp.dma_start(W1_sb[:, :, h * HO:(h + 1) * HO],
                             W1[h].rearrange("(k p) e -> p k e", p=P)).then_inc(consts_loaded, 16)
            sp.dma_start(b0_row[:, :], b0.rearrange("(a c) -> a c", a=1)).then_inc(consts_loaded, 16)
            for k, a in enumerate((a_src, a_dst)):
                sp.dma_start(a_sb[:, k, :, :], spread(a[:, 0, :], 0, P)
                             ).then_inc(consts_loaded, 16)
            for dst, src in ((bias_b, bias1), (gamma_b, gamma1), (beta_b, beta1)):
                sp.dma_start(dst[:, :, :], spread(src, 0, P)).then_inc(consts_loaded, 16)

            def prep_load(n, i):
                sp.wait_ge(h0_ready, after(n + i - 1))
                sp.dma_start(xp[:, i % 2, :], x_t[n + i]).then_inc(xp_loaded[i % 2], 16)

            def prep_store(n, i):
                sp.wait_ge(h0_ready, after(n + i + 1))
                if not (isinstance(n, int) and n < NT):
                    sp.wait_ge(zeros_written, ZEROS)
                sp.dma_start(h0_t[n + i], h0s[:, i % 2, :]).then_inc(h0_written[i % 2], 16)

            def adj_load(n, i):
                sp.wait_ge(adj_b_ready, after(n + i))
                sp.dma_start(adj_sb[:, :], adj_t[n + i]).then_inc(adj_loaded, 16)

            def at_store(n, i):
                sp.wait_ge(at_ready, after(n + i + 1))
                sp.dma_start(at_dram[n + i], at_st[:, i % 2, :].bitcast(u8)).then_inc(at_written[i % 2], 16)

            def l0_load(n, i):
                sp.wait_ge(cat_T_done, after(n + i))
                sp.dma_start(cat[:, 0:KC, :].rearrange("p k c -> p (k c)"), h0_t[n + i]).then_inc(cat_loaded, 16)
                sp.wait_ge(x1_ready, after(n + i - 1))
                sp.dma_start(xr[:, i % 2, :], x_t[n + i]).then_inc(xr_loaded[i % 2], 16)

            def l0_store(n, Q, i):
                sp.wait_ge(es_row_ready, after(n + i + 1))
                sp.dma_start(es_dram[Q, :, i * P:(i + 1) * P], es_row[:, i % 2, :]).then_inc(es_written[i % 2], 16)
                sp.wait_ge(wh_ready, after(n + i + 1))
                sp.dma_start(xh_dram[Q, i].rearrange("p h a e -> p (h a e)"),
                             xh[:, i % 2].rearrange("p h a e -> p (h a e)")).then_inc(xh_written[i % 2], 16)

            def f_store(n, i):
                sp.wait_ge(f_ready, after(n + i + 1))
                sp.dma_start(f_dram[n + i].rearrange("p h f -> p (h f)"),
                             f_st[:, i % 2].rearrange("p h a r e -> p (h a r e)")).then_inc(f_written[i % 2], 16)

            def es_load(n, Q, i):
                sp.wait_ge(sign_ready, after((n + i - 1) * 4))
                if i == 0:
                    for w in es_written:
                        sp.wait_ge(w, 16 + 8 * (n + QT))
                sp.dma_start(es_b[:, i % 2, :], spread(es_dram[Q, i], 0, P)).then_inc(es_b_loaded[i % 2], 16)

            def xh_load(n, Q, i):
                sp.wait_ge(out_ready, after(n + i - 1))
                if i == 0:
                    for w in xh_written:
                        sp.wait_ge(w, 16 + 8 * (n + QT))
                sp.dma_start(xhr[:, i % 2].rearrange("p i a e -> p i (a e)"),
                             xh_dram[Q, :, :, i].rearrange("i p a e -> p i (a e)")).then_inc(xhr_loaded[i % 2], 16)

            def at_load(n, k):
                sp.wait_ge(bc_ready, after((n - 1) * 4 + k + 1))
                hold(sp)
                for w in at_written:
                    sp.wait_ge(w, 16 + 8 * (n + QT))
                    hold(sp)
                sp.dma_start(at_q[:, :, 4 * k:4 * k + 4, :],
                             at_dram[tiles(n, QT), :, 4 * k * P:4 * (k + 1) * P].rearrange("t p (j i) -> p t j i", i=P)
                             ).then_inc(at_q_loaded[k], 16)

            def F_load(tb, h):
                if not (isinstance(tb, int) and tb == 2):
                    sp.wait_ge(acc_done, after(((tb - 2) * NT - QT + h + 1) * QT))
                sp.dma_start(F[:, :, h, :], f_dram[tiles((tb - 2) * NT, NT), :, h, :].rearrange("t p f -> p t f")
                             ).then_inc(F_loaded[h], 16)

            def body(tb, q, stages):
                for i, on in enumerate(stages):
                    at = {x: At(x, tb, q, i) for x in on}
                    if "prep" in on:
                        prep_load(at["prep"].n, at["prep"].i)
                    if "idx" in on:
                        adj_load(at["idx"].n, at["idx"].i)
                    if "sign" in on:
                        es_load(at["sign"].n, at["sign"].Q, at["sign"].i)
                    if "att" in on:
                        xh_load(at["att"].n, at["att"].Q, at["att"].i)
                    if "prep_store" in on:
                        prep_store(at["prep_store"].n, at["prep_store"].i)
                    if "l0_store" in on:
                        l0_store(at["l0_store"].n, at["l0_store"].Q, at["l0_store"].i)
                    if "at_store" in on:
                        at_store(at["at_store"].n, at["at_store"].i)
                    if "gather" in on:
                        l0_load(at["gather"].n, at["gather"].i)
                    if "out_store" in on:
                        a = at["out_store"]
                        sp.wait_ge(out_ready, after(a.n + a.i + 1))
                        sp.dma_start(out_q[a.Q, :, :, a.i, :], outs[:, a.i % 2]).then_inc(out_written[a.i % 2], 16)
                    if "l0_store" in on:
                        f_store(at["l0_store"].n, at["l0_store"].i)
                    if i == 3 and "sign" in on:
                        for k in range(4):
                            at_load(tb * NT + q * QT - 2 * NT, k)
                    if begins_batch(q, i, stages):
                        for w in f_written:
                            sp.wait_ge(w, 16 + 16 * (NT // 2) * (tb - 1))
                    if begins_batch(q, 0, stages):
                        F_load(tb, i)

            schedule(sp, body)
            for k in range(2):
                sp.wait_ge(out_written[k], 16 + 16 * TILES // 2)

        @block.gpsimd
        def _(pool):
            pool.memset(ident[:, :], 0.0)
            pool.memset(ident_b[:, :], 0.0)
            pool.memset(ones[:, :], 1.0)
            pool.memset(ones_b[:, :], 1.0)
            pool.memset(eps[:, 0:1], EPS0)
            pool.memset(eps[:, 1:2], EPS1)
            pool.memset(g[:, :, :, :], 0.0).then_inc(consts_made, 1)
            pool.wait_ge(consts_made, 1)
            pool.affine_select(out=ident[:, :], in_=ident[:, :], compare_op=ALU.not_equal, fill=1.0, base=0,
                               pattern=[[-1, P]], channel_multiplier=1)
            pool.affine_select(out=ident_b[:, :], in_=ident_b[:, :], compare_op=ALU.not_equal, fill=1.0, base=0,
                               pattern=[[-1, P]], channel_multiplier=1)
            pool.iota(group_desc[:, :], [[-256, NG]], base=256 * NG, channel_multiplier=0,
                      allow_small_or_imprecise_dtypes=True)
            pool.iota(bit_pos[:, :], [[1, GW]], base=0, channel_multiplier=0)
            for k in range(GW):
                pool.memset(bit_mask[:, k:k + 1], 2 ** (GW - 1 - k))
            pool.iota(row_end[:, :], [[N, B], [0, NT]], base=N, channel_multiplier=0,
                      allow_small_or_imprecise_dtypes=True)
            pool.iota(row_zero[:, :], [[-N, B], [0, NT]], base=ZROW - N, channel_multiplier=0,
                      allow_small_or_imprecise_dtypes=True)
            pool.memset(pack[:, :], 0.0).then_inc(consts_made, 1)
            pool.wait_ge(consts_made, 2)
            for k in range(GW):
                pool.affine_select(out=pack[:, :], in_=pack[:, :], compare_op=ALU.not_equal,
                                   fill=float(2 ** (GW - 1 - k)), base=-k, pattern=[[-GW, P // GW]],
                                   channel_multiplier=1).then_inc(consts_made, 1)
                pool.wait_ge(consts_made, 3 + k)
            pool.wait_ge(zeros_written, ZEROS)
            pool.wait_ge(consts_loaded, 16 * 11)
            pool.wait_ge(credits_given, 1)
            pool.nop().then_inc(consts_made, 1)

            def gather(n, i):
                pool.wait_ge(idx_ready, after(n + i + 1))
                for k, size in enumerate(GROUPS):
                    slot = filled[i, k][0]
                    pool.wait_ge(group_reduced, after((n + i) * len(GROUPS) + k - 1))
                    hold(pool)
                    for s in range(size):
                        nth = sum(GROUPS[:k]) + s
                        pool.indirect_dma_start(
                            g[:, slot, s, :], None, h0_dram,
                            bass.IndirectOffsetOnAxis(ap=idx[:, i, nth:nth + 1], axis=0)).then_inc(gathered[slot], 16)

            def body(tb, q, stages):
                for i, on in enumerate(stages):
                    if "gather" in on:
                        a = At("gather", tb, q, i)
                        if isinstance(q, int) and i % 2 == 0:
                            for w in h0_written:
                                pool.wait_ge(w, 16 + 16 * (NT // 2) * (tb - 1 if (q, i) == (0, 0) else tb))
                        gather(a.n, a.i)

            schedule(pool, body)

        @block.scalar
        def _(act):
            act.wait_ge(consts_made, 1)
            if B > 1:
                later = h0_dram[N:B * N, :].rearrange("(p r) c -> p r c", p=P)
                for k in range(0, later.shape[1], NT):
                    act.dma_start(later[:, k:k + NT, :],
                                  g[:, :, :, :].rearrange("p a s c -> p (a s) c")[:, 0:NT, :]).then_inc(zeros_written, 16)
            act.wait_ge(consts_made, 3 + GW)

            def prep_sqrt(n, i):
                act.wait_ge(p_var, after(n + i + 1))
                nc.scalar.activation(p_sd[:, :], p_mv[:, 1:2], ACT.Sqrt, bias=eps[:, 0:1]).then_inc(p_sqrt, 1)

            def l0_sqrt(n, i):
                act.wait_ge(l_var, after(n + i + 1))
                nc.scalar.activation(l_sd[:, :], l_mv[:, 1:2], ACT.Sqrt, bias=eps[:, 0:1]).then_inc(l_sqrt, 1)

            def l1_sqrt(n, i):
                act.wait_ge(o_var, after(n + i + 1))
                nc.scalar.activation(o_sd[:, :], o_mv[:, :, 1], ACT.Sqrt, bias=eps[:, 1:2]).then_inc(o_sqrt, 1)

            def l1_normalise(n, h):
                act.wait_ge(o_scale_ready, after(n + h + 1))
                act.wait_ge(out_ready, after(n + h))
                for it in range(QT):
                    last = nc.scalar.activation(o2[:, it, :], o1[:, it, :], ACT.Identity, bias=o_rn[:, 1, it:it + 1],
                                                scale=o_rn[:, 0, it:it + 1])
                last.then_inc(o_norm, 1)

            def prep_relu(n, i):
                act.wait_ge(p_norm, after(n + i + 1))
                act.wait_ge(h0_written[i % 2], landed(n, i, 0))
                nc.scalar.activation(h0s[:, i % 2, :], xp[:, i % 2, :], ACT.Relu, bias=p_rn[:, i % 2, 1:2],
                                     scale=p_rn[:, i % 2, 0:1]).then_inc(h0_ready, 1)

            def adj_convert(n, i):
                act.wait_ge(adj_loaded, 16 * (n + i + 1))
                act.wait_ge(A_T_done, after(n + i))
                act.wait_ge(idx_ready, after(n + i - 1))
                nc.scalar.activation(adj_b[:, :], adj_sb[:, :].bitcast(u32), ACT.Copy,
                                     accum_out=sum_a[:, i % 2:i % 2 + 1]).then_inc(adj_b_ready, 1)

            def adj_transposed(n, i):
                act.wait_ge(A_T_done, after(n + i + 1))
                act.wait_ge(at_written[i % 2], landed(n, i, 0))
                act.wait_ge(codes_done, after(n + i - 1))
                hold(act)
                nc.scalar.activation(at_st[:, i % 2, :], ps_A[:, :], ACT.Sign,
                                     accum_out=cnt_a[:, i % 2:i % 2 + 1], saturate=False).then_inc(at_ready, 1)

            def place_codes(n, i):
                act.wait_ge(codes_done, after(n + i + 1))
                act.wait_ge(idx_ready, after(n + i))
                nc.scalar.activation(code[:, 1, :], ps_k[:, 1, :], ACT.Copy).then_inc(placed_ready, 1)

            def cat_evacuate(n, i):
                act.wait_ge(cat_T_done, after(n + i + 1))
                act.wait_ge(x1_done, after(n + i))
                nc.scalar.activation(catT[:, :, :], ps_cat[:, :, :], ACT.Copy).then_inc(catT_ready, 1)

            def l0_relu(n, i):
                act.wait_ge(l_norm, after(n + i + 1))
                act.wait_ge(h1_T_done, after(n + i))
                nc.scalar.activation(h1[:, :].rearrange("p (h e) -> p h e", h=H), xh[:, i % 2, :, 0, :], ACT.Relu,
                                     bias=l_rn[:, 1:2], scale=l_rn[:, 0:1]).then_inc(h1_ready, 1)

            def h1_evacuate(n, i):
                act.wait_ge(h1_T_done, after(n + i + 1))
                act.wait_ge(wh_done, after(n + i))
                nc.scalar.activation(h1T[:, :, :].rearrange("p k c -> p (k c)"), ps_x[:, 1, :], ACT.Copy).then_inc(h1T_ready, 1)

            def wh_evacuate(n, qb, i):
                act.wait_ge(wh_done, after(n + i + 1))
                act.wait_ge(f_ready, after(n + i))
                nc.scalar.activation(uf[:, 0, :, HO], ps_h[:, C + H:C + 2 * H], ACT.Exp)
                nc.scalar.activation(uf[:, 1, :, HO], ps_h[:, C + H:C + 2 * H], ACT.Exp, scale=SLOPE).then_inc(exps_ready, 1)
                act.wait_ge(xh_written[i % 2], landed(n, i, 0))
                nc.scalar.activation(xh[:, i % 2, :, 1, :], ps_h[:, 0:C].rearrange("p (h e) -> p h e", h=H),
                                     ACT.Copy).then_inc(wh_ready, 1)
                nc.scalar.activation(esed[:, tiles(qb * QT + i), :, :],
                                     ps_h[:, C:C + 2 * H].rearrange("p (o a h) -> p o a h", o=1, a=2),
                                     ACT.Copy).then_inc(esed_ready, 1)
                act.wait_ge(es_written[i % 2], landed(n, i, 0))
                nc.scalar.activation(es_row[:, i % 2, :], ps_h[0:H, 384:512], ACT.Copy).then_inc(es_row_ready, 1)

            def part(n, i, r):
                if r == 0:
                    act.wait_ge(f_written[i % 2], landed(n, i, 0))
                act.wait_ge((uf_ready, rest_ready, rest2_ready)[r], after(n + i + 1))
                nc.scalar.activation(f_st[:, i % 2, :, :, r, :].rearrange("p h a e -> p a h e"), uf[:, :, :, :],
                                     ACT.Copy).then_inc((hi_ready, mid_ready, f_ready)[r], 1)

            def signs(n, i, k):
                if k == 0:
                    act.wait_ge(es_b_loaded[i % 2], landed(n, i, 2))
                act.wait_ge(bc_ready, after((n + i) * 4 + k - 1))
                for j in range(4):
                    jc = 4 * k + j
                    last = nc.scalar.activation(sign[:, k % 2, j, :], es_b[:, i % 2, :], ACT.Relu,
                                                bias=ed_big[:, jc, i:i + 1], scale=BIG)
                last.then_inc(sign_ready, 1)

            def scale_acc(n, qb, h, it):
                act.wait_ge(acc_done, after((n + h) * 4 + it + 1))
                act.wait_ge(acc_read, after((n + h) * 4 + it - 1))
                nc.scalar.activation(vb[:, it % 2, :], ps_o[it % 2][:, 0:FW], ACT.Copy,
                                     scale=ab[:, 0, tiles(qb * QT + it), h]).then_inc(half_ready, 1)

            def body(tb, q, stages):
                for i, on in enumerate(stages):
                    at = {x: At(x, tb, q, i) for x in on}
                    p, x, t = at.get("prep"), at.get("idx"), at.get("att")
                    a, b, lo = at.get("l0a"), at.get("l0b"), at.get("lo")
                    m, nx, o = at.get("mask"), at.get("sign"), at.get("out")
                    if t:
                        scale_acc(t.n, t.qb, t.i, 0)
                    if m and not a:
                        signs(m.n, m.i, 2)
                    if t:
                        scale_acc(t.n, t.qb, t.i, 1)
                    if a:
                        cat_evacuate(a.n, a.i)
                    if b:
                        h1_evacuate(b.n, b.i)
                    if o:
                        l1_normalise(o.n, o.i)
                    if p:
                        prep_sqrt(p.n, p.i)
                    if x:
                        adj_convert(x.n, x.i)
                    if m and a:
                        signs(m.n, m.i, 2)
                    if lo:
                        part(lo.n, lo.i, 2)
                    if p:
                        prep_relu(p.n, p.i)
                    if m:
                        signs(m.n, m.i, 3)
                    if x:
                        adj_transposed(x.n, x.i)
                    if a:
                        l0_sqrt(a.n, a.i)
                    if t:
                        scale_acc(t.n, t.qb, t.i, 2)
                    if a:
                        l0_relu(a.n, a.i)
                    if t:
                        scale_acc(t.n, t.qb, t.i, 3)
                    if b:
                        wh_evacuate(b.n, b.qb, b.i)
                    if nx and not ends_batch(q, i, stages):
                        signs(nx.n, nx.i, 0)
                    if nx and not ends_batch(q, i, stages):
                        signs(nx.n, nx.i, 1)
                    if b:
                        part(b.n, b.i, 0)
                        part(b.n, b.i, 1)
                    if x:
                        place_codes(x.n, x.i)
                    if t:
                        l1_sqrt(t.n, t.i)
                    if ends_batch(q, i, stages):
                        act.wait_ge(ab_arg_ready, after(tb - 1))
                        signs(nx.n, nx.i, 0)
                        signs(nx.n, nx.i, 1)
                    if begins_batch(q, i, stages):
                        act.wait_ge(acc_read, after((tb - 2) * NT * 4))
                        nc.scalar.activation(ab[:, :, :, :], ab_arg[:, :, :, :], ACT.Exp).then_inc(ab_ready, 1)
                        act.wait_ge(ab_ready, after(tb - 1))

            schedule(act, body)

        @block.vector
        def _(dve):
            V = nc.vector
            c0 = Chain(dve, dv_const, hold)
            c0.start()
            dve.wait_ge(consts_made, 3 + GW)
            for k in range(KC):
                for a in range(2):
                    c0.link(V.tensor_tensor(a_prod[:, a, :, :], W1_sb[:, k, 0:C].rearrange("p (h e) -> p h e", h=H),
                                            a_sb[:, a, :, :], ALU.mult))
                    c0.link(V.tensor_reduce(W1_sb[:, k, C + a * H:C + (a + 1) * H], a_prod[:, a, :, :], AX.X, ALU.add))
            V.memset(esed[:, 0, :, :], 0.0).then_inc(weights_ready, 1)

            ch_prep, ch_idx, ch_l0 = Chain(dve, dv_prep, hold), Chain(dve, dv_idx, hold), Chain(dve, dv_l0, hold)
            ch_m, ch_l1, ch_out = Chain(dve, dv_mask, hold), Chain(dve, dv_l1, hold), Chain(dve, dv_out, hold)
            ch_b = Chain(dve, dv_batch, hold)


            def prep(n, i, step):
                if step == 0:
                    dve.wait_ge(xp_loaded[i % 2], landed(n, i, 2))
                    ch_prep.start()
                    ch_prep.step(V.bn_stats(p_st[:, :], xp[:, i % 2, :]))
                elif step == 1:
                    dve.wait_ge(p_sqrt, after(n + i))
                    hold(dve)
                    ch_prep.ready()
                    V.bn_aggr(p_mv[:, :], p_st[:, :]).then_inc(p_var, 1)
                elif step == 2:
                    dve.wait_ge(p_sqrt, after(n + i + 1))
                    dve.wait_ge(h0_ready, after(n + i - 1))
                    ch_prep.step(V.reciprocal(p_rn[:, i % 2, 0:1], p_sd[:, :]))
                else:
                    ch_prep.ready()
                    V.scalar_tensor_tensor(p_rn[:, i % 2, 1:2], p_mv[:, 0:1], -1.0, p_rn[:, i % 2, 0:1], ALU.mult,
                                           ALU.mult).then_inc(p_norm, 1)

            def top_codes(r):
                ch_idx.ready()
                ch_idx.step(V.max(code_top[:, 8 * r:8 * r + 8], code[:, r % 2, :]))

            def strike_codes(r):
                ch_idx.ready()
                ch_idx.step(V.match_replace(code[:, 1 - r % 2, :], code_top[:, 8 * r:8 * r + 8], code[:, r % 2, :], 0.0))

            def top_rows(r):
                ch_idx.ready()
                ch_idx.step(V.max(score[:, 8 * r:8 * r + 8], cand[:, 0:8 * (r + 1) * GW]))

            def strike_rows(r):
                ch_idx.ready()
                first = cand[:, 0:8 * (r + 1) * GW]
                ch_idx.step(V.match_replace(first, score[:, 8 * r:8 * r + 8], first, 0.0))

            def find_codes(n, i):
                ch_idx.start()
                dve.wait_ge(placed_ready, after(n + i + 1))
                V.scalar_tensor_tensor(code[:, 0, :], ps_k[:, 0, :], 0.0, code[:, 1, :], ALU.is_gt, ALU.mult
                                       ).then_inc(codes_read, 1)
                dve.wait_ge(codes_read, after(n + i + 1))
                hold(dve)

            def find_bits(step):
                if step == 0:
                    ch_idx.ready()
                    ch_idx.step(V.tensor_copy(code_int[:, :], code_top[:, :]))
                elif step == 1:
                    ch_idx.ready()
                    ch_idx.step(V.tensor_scalar(first8[:, :], code_int[:, :], 8, 3, ALU.logical_shift_right,
                                                ALU.logical_shift_left))
                    ch_idx.step(V.tensor_tensor(bits[:, :, :], spread(code_int[:, :], 2, GW),
                                                spread(bit_mask[:, :], 1, 32), ALU.bitwise_and))
                elif step == 2:
                    ch_idx.ready()
                    ch_idx.step(V.tensor_tensor(cand_v[:, :, :], spread(first8[:, :], 2, GW),
                                                spread(bit_pos[:, :], 1, 32), ALU.subtract))
                else:
                    ch_idx.ready()
                    ch_idx.step(V.scalar_tensor_tensor(cand[:, :].rearrange("p (s k) -> p s k", k=GW), bits[:, :, :],
                                                       0.0, cand_v[:, :, :], ALU.is_gt, ALU.mult))

            def find_rows(n, i, step):
                if step == 0:
                    ch_idx.ready()
                    V.tensor_copy(top_s[:, tiles(n + i)], score[:, 0:1])
                    V.tensor_tensor(over_a[:, tiles(n + i)], sum_a[:, i % 2:i % 2 + 1], cnt_a[:, i % 2:i % 2 + 1],
                                    ALU.subtract)
                    ch_idx.step(V.tensor_scalar(zero_fix[:, :], score[:, :], 0.0, row_zero[:, tiles(n + i)],
                                                ALU.is_equal, ALU.mult))
                elif step == 1:
                    ch_idx.ready()
                    ch_idx.step(V.scalar_tensor_tensor(zero_fix[:, :], score[:, :], -1.0, zero_fix[:, :], ALU.mult,
                                                       ALU.add))
                else:
                    ch_idx.ready()
                    V.tensor_scalar(idx[:, i, :], zero_fix[:, :], row_end[:, tiles(n + i)], None, ALU.add
                                    ).then_inc(idx_ready, 1)

            def reduce_group(n, Q, i, k):
                slot, count = filled[i, k]
                dve.wait_ge(gathered[slot], Q * fills[slot] + count)
                dve.wait_ge(group_reduced, after((n + i) * len(GROUPS) + k))
                if k == len(GROUPS) - 1:
                    dve.wait_ge(cat_T_done, after(n + i))
                    most = cat[:, KC:, :].rearrange("p k c -> p (k c)")
                else:
                    most = g[:, 1 - slot, GROUPS[0] - 1, :]
                V.tensor_reduce(most, g[:, slot, :, :].rearrange("p s c -> p c s"), AX.X, ALU.max
                                ).then_inc(group_reduced, 1)

            def l0_x1(n, i, step):
                if step == 0:
                    dve.wait_ge(x1_done, after(n + i + 1))
                    dve.wait_ge(xr_loaded[i % 2], landed(n, i, 2))
                    dve.wait_ge(xh_written[i % 2], landed(n, i, 0))
                    V.scalar_tensor_tensor(xh[:, i % 2, :, 0, :], ps_x[:, 0, :].rearrange("p (h e) -> p h e", h=H), 0.0,
                                           xr[:, i % 2, :].rearrange("p (h e) -> p h e", h=H), ALU.max,
                                           ALU.add).then_inc(x1_ready, 1)
                elif step == 1:
                    dve.wait_ge(x1_ready, after(n + i + 1))
                    ch_l0.start()
                    ch_l0.step(V.bn_stats(l_st[:, :], xh[:, i % 2, :, 0, :]))
                elif step == 2:
                    ch_l0.ready()
                    V.bn_aggr(l_mv[:, :], l_st[:, :]).then_inc(l_var, 1)
                elif step == 3:
                    dve.wait_ge(l_sqrt, after(n + i + 1))
                    dve.wait_ge(h1_ready, after(n + i))
                    ch_l0.step(V.reciprocal(l_rn[:, 0:1], l_sd[:, :]))
                else:
                    ch_l0.ready()
                    V.scalar_tensor_tensor(l_rn[:, 1:2], l_mv[:, 0:1], -1.0, l_rn[:, 0:1], ALU.mult,
                                           ALU.mult).then_inc(l_norm, 1)

            def features(n, i):
                dve.wait_ge(exps_ready, after(n + i + 1))
                dve.wait_ge(wh_ready, after(n + i + 1))
                for a in range(2):
                    last = V.tensor_tensor(uf[:, a, :, 0:HO], xh[:, i % 2, :, 1, :],
                                           spread(uf[:, a, :, HO], 2, HO), ALU.mult)
                last.then_inc(uf_ready, 1)

            def rest(n, i, r):
                dve.wait_ge((hi_ready, mid_ready)[r], after(n + i + 1))
                V.tensor_tensor(uf[:, :, :, :], uf[:, :, :, :], part_v(i, r), ALU.subtract
                                ).then_inc((rest_ready, rest2_ready)[r], 1)

            def part_v(i, r):
                return f_st[:, i % 2, :, :, r, :].rearrange("p h a e -> p a h e")

            def mask_views(i, k):
                js = slice(4 * k, 4 * k + 4)
                a = at_q[:, :, js, :].bitcast(u32).rearrange("p t j w -> p j t w")
                b = BC[:, i % 2, 0, js, :].bitcast(u32).rearrange("p j (t w) -> p j t w", t=QT)
                c = BC[:, i % 2, 1, js, :].bitcast(u32).rearrange("p j (t w) -> p j t w", t=QT)
                s = sign[:, k % 2, :, :].bitcast(u32).rearrange("p j (t w) -> p j t w", t=QT)
                return a, b, c, s

            def mask_above(n, Q, i, k):
                dve.wait_ge(sign_ready, after((n + i) * 4 + k + 1))
                if i == 0:
                    dve.wait_ge(at_q_loaded[k], 16 * (Q + 1))
                if k == 0:
                    dve.wait_ge(acc_done, after((n + i - 1) * 4))
                a, b, c, s = mask_views(i, k)
                ch_m.step(V.tensor_tensor(b, s, a, ALU.bitwise_and))

            def mask_rest(n, i, k):
                a, b, c, s = mask_views(i, k)
                ch_m.ready()
                V.tensor_tensor(c, a, b, ALU.bitwise_xor).then_inc(bc_ready, 1)

            def add_acc(n, qb, i, it):
                dve.wait_ge(half_ready, after((n + i) * 4 + it + 1))
                V.scalar_tensor_tensor(wb[:, it, :], ps_o[it % 2][:, FW:2 * FW], ab[:, 1, tiles(qb * QT + it), i],
                                       vb[:, it % 2, :], ALU.mult, ALU.add).then_inc(acc_read, 1)

            def sum_parts(n, i):
                dve.wait_ge(acc_read, after((n + i + 1) * 4))
                ch_l1.step(V.tensor_reduce(oraw[:, :, :], wb[:, :, :].rearrange("p i (r e) -> p i e r", r=PARTS), AX.X,
                                           ALU.add))

            def l1_dst(n, h, step):
                ch_l1.ready()
                if step == 0:
                    ch_l1.step(V.tensor_scalar(rden[:, :], oraw[:, :, HO], TINY, None, ALU.max))
                elif step == 1:
                    ch_l1.step(V.reciprocal(rden[:, :], rden[:, :]))
                elif step == 2:
                    ch_l1.step(V.tensor_tensor(o1[:, :, :], oraw[:, :, 0:HO], spread(rden[:, :], 2, HO), ALU.mult))
                elif step == 3:
                    ch_l1.step(V.tensor_tensor(o1[:, :, :], o1[:, :, :], spread(bias_b[:, h, :], 1, QT), ALU.add))
                else:
                    dve.wait_ge(xhr_loaded[h % 2], landed(n, h, 2))
                    ch_l1.step(V.scalar_tensor_tensor(o1[:, :, :], o1[:, :, :], 0.0, xhr[:, h % 2, :, 1, :], ALU.max,
                                                      ALU.add))

            def l1_stats(n, h, step):
                ch_l1.ready()
                if step == 0:
                    for it in range(QT):
                        last = V.bn_stats(o_st[:, it, :], o1[:, it, :])
                    ch_l1.step(last)
                else:
                    for it in range(QT):
                        last = V.bn_aggr(o_mv[:, it, :], o_st[:, it, :])
                    last.then_inc(o_var, 1)

            def l1_out(n, h, step):
                if step == 0:
                    ch_out.start()
                    dve.wait_ge(o_sqrt, after(n + h + 1))
                    ch_out.step(V.reciprocal(o_rn[:, 0, :], o_sd[:, :]))
                elif step == 1:
                    ch_out.ready()
                    V.scalar_tensor_tensor(o_rn[:, 1, :], o_mv[:, :, 0], -1.0, o_rn[:, 0, :], ALU.mult, ALU.mult
                                           ).then_inc(o_scale_ready, 1)
                elif step == 2:
                    dve.wait_ge(o_norm, after(n + h + 1))
                    ch_out.step(V.tensor_tensor(o2[:, :, :], o2[:, :, :], spread(gamma_b[:, h, :], 1, QT), ALU.mult))
                elif step == 3:
                    ch_out.ready()
                    ch_out.step(V.tensor_tensor(o2[:, :, :], o2[:, :, :], spread(beta_b[:, h, :], 1, QT), ALU.add))
                else:
                    ch_out.ready()
                    dve.wait_ge(out_written[h % 2], landed(n, h, 0))
                    V.tensor_tensor(outs[:, h % 2, :, :], o2[:, :, :], xhr[:, h % 2, :, 0, :], ALU.add
                                    ).then_inc(out_ready, 1)

            def batch_end(b):
                ch_b.start()
                dve.wait_ge(esed_ready, after((b + 1) * NT))
                dve.wait_ge(sign_ready, after(b * NT * 4))
                ed = esed[:, :, 1, :]
                es = esed[:, :, 0, :]
                ch_b.link(V.tensor_scalar(ed_big[:, :, :], ed, BIG, None, ALU.mult))
                ch_b.link(V.tensor_reduce(dmx[:, 0, :], ed.rearrange("p t h -> p h t"), AX.X, ALU.max))
                ch_b.link(V.tensor_scalar(srow[:, :, :], ed, -1.0, None, ALU.mult))
                V.tensor_reduce(dmx[:, 1, :], srow[:, :, :].rearrange("p t h -> p h t"), AX.X, ALU.max).then_inc(dmx_ready, 1)
                dve.wait_ge(dmx_T_done, after(b + 1))
                ch_b.link(V.tensor_reduce(dmx_t[:, :], ps_cat[0:2 * H, 0, :], AX.X, ALU.max))
                V.tensor_scalar(dmx_d[:, :], ident[0:2 * H, 0:2 * H], dmx_t[:, :], None, ALU.mult).then_inc(dmx_d_ready, 1)
                dve.wait_ge(dtop_done, after(b + 1))
                dt = dtop[:, b, :, :] if isinstance(b, int) else dtop[:, bass.ds(b, 1), :, :].rearrange("p o a h -> p (o a) h")
                ch_b.link(V.tensor_copy(dt, ps_cat[:, 1, 0:2 * H].rearrange("p (a h) -> p a h", a=2)))
                ch_b.link(V.tensor_tensor(srow[:, :, :], es, spread(ps_cat[:, 1, 0:H], 1, NT), ALU.add))
                ch_b.link(V.scalar_tensor_tensor(mrow[:, :, :], srow[:, :, :], SLOPE, srow[:, :, :], ALU.mult, ALU.max))
                ch_b.link(V.tensor_tensor(ab_arg[:, 0, :, :], es, mrow[:, :, :], ALU.subtract))
                V.scalar_tensor_tensor(ab_arg[:, 1, :, :], es, SLOPE, mrow[:, :, :], ALU.mult, ALU.subtract).then_inc(ab_arg_ready, 1)

            def body(tb, q, stages):
                for i, on in enumerate(stages):
                    at = {x: At(x, tb, q, i) for x in on}
                    p, x, m, t = at.get("prep"), at.get("find"), at.get("mask"), at.get("att")
                    g_, a, b, lo = at.get("gather"), at.get("l0a"), at.get("l0b"), at.get("lo")
                    o = at.get("out")
                    if m:
                        ch_m.start()
                    if t:
                        ch_l1.start()
                    if p:
                        prep(p.n, p.i, 0)
                    if m:
                        mask_above(m.n, m.Q, m.i, 0)
                    if p:
                        prep(p.n, p.i, 1)
                    if m:
                        mask_rest(m.n, m.i, 0)
                    if t:
                        add_acc(t.n, t.qb, t.i, 0)
                    if o:
                        l1_out(o.n, o.i, 0)
                    if x:
                        find_codes(x.n, x.i)
                    if o:
                        l1_out(o.n, o.i, 1)
                    if lo:
                        rest(lo.n, lo.i, 1)
                    if m:
                        mask_above(m.n, m.Q, m.i, 1)
                    if x:
                        top_codes(0)
                    if m:
                        mask_rest(m.n, m.i, 1)
                    if t:
                        add_acc(t.n, t.qb, t.i, 1)
                    if x:
                        strike_codes(0)
                    if o:
                        l1_out(o.n, o.i, 2)
                    if x:
                        top_codes(1)
                    if o:
                        l1_out(o.n, o.i, 3)
                    if x:
                        strike_codes(1)
                    if o:
                        l1_out(o.n, o.i, 4)
                    if g_:
                        reduce_group(g_.n, g_.Q, g_.i, 0)
                    if x:
                        top_codes(2)
                    if m:
                        mask_above(m.n, m.Q, m.i, 2)
                    if p:
                        prep(p.n, p.i, 2)
                    if x:
                        strike_codes(2)
                    if m:
                        mask_rest(m.n, m.i, 2)
                    if p:
                        prep(p.n, p.i, 3)
                    if x:
                        top_codes(3)
                    if x:
                        find_bits(0)
                    if x:
                        find_bits(1)
                    if a:
                        l0_x1(a.n, a.i, 0)
                    if x:
                        find_bits(2)
                    if a:
                        l0_x1(a.n, a.i, 1)
                    if x:
                        find_bits(3)
                    if a:
                        l0_x1(a.n, a.i, 2)
                    if m:
                        mask_above(m.n, m.Q, m.i, 3)
                    if x:
                        top_rows(0)
                    if m:
                        mask_rest(m.n, m.i, 3)
                    if x:
                        strike_rows(0)
                    if a:
                        l0_x1(a.n, a.i, 3)
                    if t:
                        add_acc(t.n, t.qb, t.i, 2)
                    if x:
                        top_rows(1)
                    if a:
                        l0_x1(a.n, a.i, 4)
                    if x:
                        strike_rows(1)
                    if g_:
                        reduce_group(g_.n, g_.Q, g_.i, 1)
                    if x:
                        top_rows(2)
                    if x:
                        strike_rows(2)
                    if x:
                        top_rows(3)
                    if t:
                        add_acc(t.n, t.qb, t.i, 3)
                        sum_parts(t.n, t.i)
                    if b:
                        features(b.n, b.i)
                    if t:
                        l1_dst(t.n, t.i, 0)
                    if x:
                        find_rows(x.n, x.i, 0)
                    if t:
                        l1_dst(t.n, t.i, 1)
                    if x:
                        find_rows(x.n, x.i, 1)
                    if t:
                        l1_dst(t.n, t.i, 2)
                    if x:
                        find_rows(x.n, x.i, 2)
                    if t:
                        l1_dst(t.n, t.i, 3)
                    if t:
                        l1_dst(t.n, t.i, 4)
                    if b:
                        rest(b.n, b.i, 0)
                    if g_:
                        reduce_group(g_.n, g_.Q, g_.i, 2)
                    if t:
                        l1_stats(t.n, t.i, 0)
                        l1_stats(t.n, t.i, 1)
                    if ends_batch(q, i, stages):
                        batch_end(tb - 2)

            schedule(dve, body)

        @block.tensor
        def _(pe):
            M = nc.tensor
            pe.wait_ge(consts_made, 3 + GW)
            pe.wait_ge(weights_ready, 1)

            def adj_T(n, i):
                pe.wait_ge(adj_b_ready, after(n + i + 1))
                pe.wait_ge(at_ready, after(n + i))
                for j in range(NT):
                    last = M.transpose(ps_A[:, j * P:(j + 1) * P], adj_b[:, j * P:(j + 1) * P], ident_b[:, :])
                last.then_inc(A_T_done, 1)

            def codes(n, i):
                pe.wait_ge(at_ready, after(n + i + 1))
                pe.wait_ge(codes_read, after(n + i))
                hold(pe)
                w = P // GW
                for j in range(NT):
                    M.matmul(ps_k[:, 0, j * w:(j + 1) * w], at_st[:, i % 2, j * P:(j + 1) * P], pack[:, :],
                             start=True, stop=True)
                    M.matmul(ps_k[:, 1, j * w:(j + 1) * w], at_st[:, i % 2, j * P:(j + 1) * P], pack[:, :],
                             start=True, stop=False)
                    last = M.matmul(ps_k[:, 1, j * w:(j + 1) * w], ones_b[:, :], group_desc[:, j * w:(j + 1) * w],
                                    start=False, stop=True)
                last.then_inc(codes_done, 1)

            def cat_T(n, i):
                pe.wait_ge(group_reduced, after((n + i + 1) * len(GROUPS)))
                pe.wait_ge(cat_loaded, 16 * (n + i + 1))
                pe.wait_ge(catT_ready, after(n + i))
                for k in range(2 * KC):
                    last = M.transpose(ps_cat[:, k, :], cat[:, k, :], ident[:, :])
                last.then_inc(cat_T_done, 1)

            def x1_mm(n, i):
                pe.wait_ge(catT_ready, after(n + i + 1))
                pe.wait_ge(x1_ready, after(n + i))
                pe.wait_ge(h1T_ready, after(n + i))
                for k in range(2 * KC):
                    M.matmul(ps_x[:, 0, :], catT[:, k, :], W0_sb[:, k, :], start=(k == 0), stop=False)
                M.matmul(ps_x[:, 0, :], ones[0:1, :], b0_row[:, :], start=False, stop=True).then_inc(x1_done, 1)

            def h1_T(n, i):
                pe.wait_ge(h1_ready, after(n + i + 1))
                pe.wait_ge(h1T_ready, after(n + i))
                pe.wait_ge(x1_ready, after(n + i + 1))
                for k in range(KC):
                    last = M.transpose(ps_x[:, 1, k * P:(k + 1) * P], h1[:, k * P:(k + 1) * P], ident[:, :])
                last.then_inc(h1_T_done, 1)

            def wh_mm(n, i):
                pe.wait_ge(h1T_ready, after(n + i + 1))
                pe.wait_ge(es_row_ready, after(n + i))
                pe.wait_ge(uf_ready, after(n + i))
                for k in range(KC):
                    M.matmul(ps_h[:, 0:C + 2 * H], h1T[:, k, :], W1_sb[:, k, :], start=(k == 0), stop=(k == KC - 1))
                for k in range(KC):
                    last = M.matmul(ps_h[0:H, 384:512], W1_sb[:, k, C:C + H], h1T[:, k, :], start=(k == 0),
                                    stop=(k == KC - 1))
                last.then_inc(wh_done, 1)

            def attend(b, n, i, it):
                h = i
                if it == 0:
                    pe.wait_ge(F_loaded[h], 16 * (b + 1))
                    pe.wait_ge(bc_ready, after((n + i + 1) * 4))
                pe.wait_ge(acc_read, after((n + i) * 4 + it - 1))
                hold(pe)
                for a in range(2):
                    for j in range(NT):
                        last = M.matmul(ps_o[it % 2][:, a * FW:(a + 1) * FW],
                                        BC[:, i % 2, a, j, it * P:(it + 1) * P].bitcast(f8),
                                        F[:, j, h, a * FW:(a + 1) * FW], start=(j == 0), stop=(j == NT - 1))
                last.then_inc(acc_done, 1)

            def maxima(b, so_far):
                pe.wait_ge(catT_ready, after(so_far))
                pe.wait_ge(dmx_ready, after(b + 1))
                M.transpose(ps_cat[0:2 * H, 0, :], dmx[:, :, :].rearrange("p a h -> p (a h)"),
                            ident[:, :]).then_inc(dmx_T_done, 1)
                pe.wait_ge(dmx_d_ready, after(b + 1))
                M.matmul(ps_cat[:, 1, 0:2 * H], ones[0:2 * H, :], dmx_d[:, :], start=True, stop=True
                         ).then_inc(dtop_done, 1)
                pe.wait_ge(ab_arg_ready, after(b + 1))

            def body(tb, q, stages):
                for i, on in enumerate(stages):
                    at = {x: At(x, tb, q, i) for x in on}
                    x, t, a, b = at.get("idx"), at.get("att"), at.get("l0a"), at.get("l0b")
                    bt = tb - 3 if isinstance(q, int) and (q, i) <= (1, 0) else tb - 2
                    if t:
                        attend(bt, t.n, t.i, 0)
                        attend(bt, t.n, t.i, 1)
                    if a:
                        cat_T(a.n, a.i)
                    if b:
                        h1_T(b.n, b.i)
                    if a:
                        x1_mm(a.n, a.i)
                    if t:
                        attend(bt, t.n, t.i, 2)
                    if x:
                        adj_T(x.n, x.i)
                    if b:
                        wh_mm(b.n, b.i)
                    if t:
                        attend(bt, t.n, t.i, 3)
                    if x:
                        codes(x.n, x.i)
                    if ends_batch(q, i, stages):
                        maxima(tb - 2, a.n + a.i + 1 if a else TILES)

            schedule(pe, body)

    flag_batches(nc, ones, over_a, top_s, dtop, flags)
    general_layer1(nc, adj_t, xh_dram, a_src, a_dst, bias1, gamma1, beta1,
                   out.rearrange("b (t p) (h e) -> (b t) p h e", p=P, h=H), ident, eps, flags)
    keep.close()


def flag_batches(nc, ones, over_a, top_s, dtop, flags):
    TILES, B = over_a.shape[1], dtop.shape[1]
    with ExitStack() as ctx:
        empty = ctx.enter_context(nc.sbuf_tensor("empty", [P, TILES], f32))
        parts = ctx.enter_context(nc.sbuf_tensor("parts", [1, 3, B], f32))
        ps = ctx.enter_context(nc.psum_tensor("ps_flags", [P, 512], f32))
        empty_ready = ctx.enter_context(nc.semaphore("empty_ready"))
        sums_done = ctx.enter_context(nc.semaphore("sums_done"))
        dv_flags = ctx.enter_context(nc.semaphore("dv_flags"))
        block = ctx.enter_context(nc.Block())

        @block.vector
        def _(dve):
            V = nc.vector
            V.tensor_scalar(empty[:, :], top_s[:, :], 0.0, None, ALU.is_equal).then_inc(empty_ready, 1)
            dve.wait_ge(sums_done, 1)
            for k in range(2):
                V.tensor_reduce(parts[:, k, :], ps[0:1, k * TILES:(k + 1) * TILES].rearrange("p (b t) -> p b t", b=B),
                                AX.X, ALU.max)
            V.tensor_reduce(parts[:, 2, :], dtop[0:1, :, :, :].rearrange("p b a h -> p b (a h)"), AX.X,
                            ALU.max).then_inc(dv_flags, 1)
            dve.wait_ge(dv_flags, 1)
            V.tensor_scalar(parts[:, 0:2, :], parts[:, 0:2, :], 0.5, None, ALU.is_gt)
            V.tensor_scalar(parts[:, 2, :], parts[:, 2, :], EDMAX, None, ALU.is_gt).then_inc(dv_flags, 1)
            dve.wait_ge(dv_flags, 2)
            V.tensor_reduce(flags[:, :], parts[:, :, :].rearrange("p k b -> p b k"), AX.X, ALU.max)

        @block.tensor
        def _(pe):
            pe.wait_ge(empty_ready, 1)
            nc.tensor.matmul(ps[0:1, 0:TILES], ones[:, 0:1], over_a[:, :], start=True, stop=True)
            nc.tensor.matmul(ps[0:1, TILES:2 * TILES], ones[:, 0:1], empty[:, :], start=True,
                             stop=True).then_inc(sums_done, 1)


def general_layer1(nc, adj_t, xh_dram, a_src, a_dst, bias1, gamma1, beta1, out_t, ident, eps, flags):
    H, T, HO = a_src.shape
    N = adj_t.shape[2]
    B = flags.shape[1]
    NT = N // P
    NQ = NT // QT
    UNITS = H * NT
    xh_t = xh_dram.rearrange("q i p h a e -> (q i) p h a e")
    ed_dram = nc.dram_tensor("e_dst_rows", (T, N), f32, kind="Internal").ap()
    with ExitStack() as ctx:
        def sb(name, shape, dt=f32):
            return ctx.enter_context(nc.sbuf_tensor("g_" + name, shape, dt))

        def sem(name):
            return ctx.enter_context(nc.semaphore("g_" + name))

        a_sb = sb("a_sb", [P, 2, H, T, HO])
        bias_b, gamma_b, beta_b = (sb(n, [P, H, HO]) for n in ("bias", "gamma", "beta"))
        hh = sb("hh", [P, NT, HO])
        prod = sb("prod", [P, T, HO])
        es = sb("es", [P, NT, T])
        ed = sb("ed", [P, NT, T])
        edT = sb("edT", [T, N])
        ed_b = sb("ed_b", [P, T, N])
        adj_sb = sb("adj", [P, N], i32)
        s = sb("s", [P, 2, N])
        w = sb("w", [P, N])
        z = sb("z", [P, N])
        pr = sb("pr", [P, N])
        prT = sb("prT", [P, 4, P])
        nmx = sb("nmx", [P, 1])
        den = sb("den", [P, 1])
        rden = sb("rden", [P, 1])
        xh = sb("xh", [P, 2, HO])
        o = sb("o", [P, 6, HO])
        st, mv, sd, rs = sb("st", [P, 6]), sb("mv", [P, 2]), sb("sd", [P, 1]), sb("rs", [P, 1])
        ps_t = ctx.enter_context(nc.psum_tensor("g_ps_t", [P, 4, P], f32))
        ps_e = ctx.enter_context(nc.psum_tensor("g_ps_e", [P, 512], f32))
        ps_o = ctx.enter_context(nc.psum_tensor("g_ps_o", [P, 512], f32))

        consts_loaded = sem("consts_loaded")
        hh_loaded, ed_ready, ed_T_done, edT_ready = (sem(n) for n in ("hh_loaded", "ed_ready", "ed_T_done", "edT_ready"))
        ed_written, ed_b_loaded = sem("ed_written"), sem("ed_b_loaded")
        adj_loaded, xh_loaded, out_written = sem("adj_loaded"), sem("xh_loaded"), sem("out_written")
        s_ready, s_used = sem("s_ready"), sem("s_used")
        w_ready, exp_done = sem("w_ready"), sem("exp_done")
        T_done, prT_ready, mm_done = sem("T_done"), sem("prT_ready"), sem("mm_done")
        var_ready, sqrt_ready, out_ready = sem("var_ready"), sem("sqrt_ready"), sem("out_ready")
        held, chain = sem("held"), sem("chain")
        compute = [ed_ready, ed_T_done, edT_ready, s_ready, s_used, w_ready, exp_done, T_done, prT_ready, mm_done,
                   var_ready, sqrt_ready, out_ready]
        by_dma = [hh_loaded, ed_written, ed_b_loaded, adj_loaded, xh_loaded, out_written]
        arrived, reset_done, left = sem("arrived"), sem("reset_done"), sem("left")
        block = ctx.enter_context(nc.Block())

        def give_credits(sp):
            for x in compute:
                sp.sem_inc(x, 1)
            for x in by_dma:
                sp.sem_inc(x, 16)

        def hold(eng):
            eng.sem_inc(held, 1)

        def each_flagged(eng, head, unit):
            with eng.Fori(0, B) as b:
                flag = eng.value_load(flags[0:1, bass.ds(b, 1)], min_val=0, max_val=1)
                with eng.If(flag > 0):
                    for h in range(H):
                        head(b, h)
                        with eng.Fori(0, NT) as t:
                            unit(b, h, t, h * NT + t)
                    if eng is nc.sync:
                        eng.wait_ge(arrived, 3)
                        eng.sem_clear(arrived)
                        for x in compute + by_dma:
                            eng.sem_clear(x)
                        give_credits(eng)
                        eng.sem_inc(reset_done, 1)
                        eng.wait_ge(left, 3)
                        eng.sem_clear(reset_done)
                        eng.sem_clear(left)
                    else:
                        eng.sem_inc(arrived, 1)
                        eng.wait_ge(reset_done, 1)
                        eng.sem_inc(left, 1)

        @block.sync
        def _(sp):
            give_credits(sp)
            for k, a in enumerate((a_src, a_dst)):
                sp.dma_start(a_sb[:, k], spread(a, 0, P)).then_inc(consts_loaded, 16)
            for dst, src in ((bias_b, bias1), (gamma_b, gamma1), (beta_b, beta1)):
                sp.dma_start(dst[:, :, :], spread(src, 0, P)).then_inc(consts_loaded, 16)

            def head(b, h):
                sp.wait_ge(out_ready, 1 + h * NT)
                sp.dma_start(hh[:, :, :], xh_t[bass.ds(b * NT, NT), :, h, 1, :].rearrange("t p e -> p t e")
                             ).then_inc(hh_loaded, 16)
                sp.wait_ge(edT_ready, 1 + (h + 1) * NQ)
                sp.dma_start(ed_dram, edT[:, :]).then_inc(ed_written, 16)
                sp.wait_ge(ed_written, 16 + 16 * (h + 1))
                sp.dma_start(ed_b[:, :, :], spread(ed_dram, 0, P)).then_inc(ed_b_loaded, 16)
                sp.wait_ge(ed_b_loaded, 16 + 16 * (h + 1))
                hold(sp)

            def unit(b, h, t, u):
                sp.wait_ge(out_ready, 1 + u)
                sp.dma_start(adj_sb[:, :], adj_t[b * NT + t]).then_inc(adj_loaded, 16)
                sp.dma_start(xh[:, :, :], xh_t[b * NT + t, :, h]).then_inc(xh_loaded, 16)
                sp.wait_ge(out_ready, 1 + u + 1)
                sp.dma_start(out_t[b * NT + t, :, h, :], o[:, 5, :]).then_inc(out_written, 16)
                sp.wait_ge(out_written, 16 + 16 * (u + 1))
                hold(sp)

            each_flagged(sp, head, unit)

        @block.scalar
        def _(act):
            A = nc.scalar

            def head(b, h):
                for q in range(NQ):
                    act.wait_ge(ed_T_done, 1 + h * NQ + q + 1)
                    act.wait_ge(ed_b_loaded, 16 + 16 * h)
                    A.activation(edT[:, q * QT * P:(q + 1) * QT * P], ps_e[0:T, :], ACT.Copy).then_inc(edT_ready, 1)

            def unit(b, h, t, u):
                act.wait_ge(ed_b_loaded, 16 + 16 * (h + 1))
                for k in range(T):
                    if k >= 2:
                        act.wait_ge(s_used, 1 + u * T + k - 1)
                    else:
                        act.wait_ge(s_used, 1 + u * T)
                    A.activation(s[:, k % 2, :], ed_b[:, k, :], ACT.Identity, bias=es[:, bass.ds(t, 1), k]
                                 ).then_inc(s_ready, 1)
                act.wait_ge(w_ready, 1 + u + 1)
                act.wait_ge(T_done, 1 + 4 * u)
                A.activation(pr[:, :], w[:, :], ACT.Exp, bias=nmx[:, :], accum_out=den[:, :]).then_inc(exp_done, 1)
                for k in range(4):
                    act.wait_ge(T_done, 1 + 4 * u + k + 1)
                    act.wait_ge(mm_done, 1 + 4 * u + k)
                    A.activation(prT[:, :, :], ps_t[:, :, :], ACT.Copy).then_inc(prT_ready, 1)
                act.wait_ge(var_ready, 1 + u + 1)
                A.activation(sd[:, :], mv[:, 1:2], ACT.Sqrt, bias=eps[:, 1:2]).then_inc(sqrt_ready, 1)

            each_flagged(act, head, unit)

        @block.tensor
        def _(pe):
            M = nc.tensor

            def head(b, h):
                pe.wait_ge(ed_ready, 1 + h + 1)
                for q in range(NQ):
                    pe.wait_ge(edT_ready, 1 + h * NQ + q)
                    for k in range(QT):
                        last = M.transpose(ps_e[0:T, k * P:(k + 1) * P], ed[:, q * QT + k, :], ident[:, :])
                    last.then_inc(ed_T_done, 1)

            def unit(b, h, t, u):
                pe.wait_ge(exp_done, 1 + u + 1)
                pe.wait_ge(var_ready, 1 + u)
                for k in range(4):
                    pe.wait_ge(prT_ready, 1 + 4 * u + k)
                    for j in range(4):
                        last = M.transpose(ps_t[:, j, :], pr[:, (4 * k + j) * P:(4 * k + j + 1) * P], ident[:, :])
                    last.then_inc(T_done, 1)
                    pe.wait_ge(prT_ready, 1 + 4 * u + k + 1)
                    for j in range(4):
                        last = M.matmul(ps_o[:, 0:HO], prT[:, j, :], hh[:, 4 * k + j, :], start=(k + j == 0),
                                        stop=(k == 3 and j == 3))
                    last.then_inc(mm_done, 1)

            each_flagged(pe, head, unit)

        @block.vector
        def _(dve):
            V = nc.vector
            dve.wait_ge(consts_loaded, 16 * 5)

            c = Chain(dve, chain, hold)

            def head(b, h):
                dve.wait_ge(hh_loaded, 16 + 16 * (h + 1))
                c.start()
                for t in range(NT):
                    for k, dst in enumerate((es, ed)):
                        c.link(V.tensor_tensor(prod[:, :, :], a_sb[:, k, h], spread(hh[:, t, :], 1, T), ALU.mult))
                        if t == NT - 1 and k == 1:
                            V.tensor_reduce(dst[:, t, :], prod[:, :, :], AX.X, ALU.add).then_inc(ed_ready, 1)
                        else:
                            c.link(V.tensor_reduce(dst[:, t, :], prod[:, :, :], AX.X, ALU.add))

            def unit(b, h, t, u):
                dve.wait_ge(adj_loaded, 16 + 16 * (u + 1))
                c.start()
                for k in range(T):
                    dve.wait_ge(s_ready, 1 + u * T + k + 1)
                    V.scalar_tensor_tensor(z[:, :] if k else w[:, :], adj_sb[:, :], float(k + 1), s[:, k % 2, :],
                                           ALU.is_equal, ALU.mult).then_inc(s_used, 1)
                    if k:
                        dve.wait_ge(s_used, 1 + u * T + k + 1)
                        c.link(V.tensor_tensor(w[:, :], w[:, :], z[:, :], ALU.add))
                c.link(V.scalar_tensor_tensor(w[:, :], w[:, :], SLOPE, w[:, :], ALU.mult, ALU.max))
                c.link(V.tensor_scalar(z[:, :], adj_sb[:, :], 0.0, NEG, ALU.is_equal, ALU.mult))
                c.link(V.tensor_tensor(w[:, :], w[:, :], z[:, :], ALU.add))
                V.tensor_reduce(nmx[:, :], w[:, :], AX.X, ALU.max, negate=True).then_inc(w_ready, 1)
                dve.wait_ge(exp_done, 1 + u + 1)
                c.link(V.reciprocal(rden[:, :], den[:, :]))
                dve.wait_ge(mm_done, 1 + 4 * (u + 1))
                dve.wait_ge(xh_loaded, 16 + 16 * (u + 1))
                c.link(V.scalar_tensor_tensor(o[:, 0, :], ps_o[:, 0:HO], rden[:, :], bias_b[:, h, :], ALU.mult, ALU.add))
                c.link(V.scalar_tensor_tensor(o[:, 1, :], o[:, 0, :], 0.0, xh[:, 1, :], ALU.max, ALU.add))
                c.link(V.bn_stats(st[:, :], o[:, 1, :]))
                V.bn_aggr(mv[:, :], st[:, :]).then_inc(var_ready, 1)
                dve.wait_ge(sqrt_ready, 1 + u + 1)
                c.link(V.reciprocal(rs[:, :], sd[:, :]))
                c.link(V.tensor_scalar(o[:, 2, :], o[:, 1, :], mv[:, 0:1], rs[:, :], ALU.subtract, ALU.mult))
                c.link(V.tensor_tensor(o[:, 3, :], o[:, 2, :], gamma_b[:, h, :], ALU.mult))
                c.link(V.tensor_tensor(o[:, 4, :], o[:, 3, :], beta_b[:, h, :], ALU.add))
                dve.wait_ge(out_written, 16 + 16 * u)
                V.tensor_tensor(o[:, 5, :], o[:, 4, :], xh[:, 0, :], ALU.add).then_inc(out_ready, 1)

            each_flagged(dve, head, unit)


_INS = ["x", "adj", "L0_gnn_W", "L0_gnn_b", "L1_gnn_W", "L1_gnn_a_src", "L1_gnn_a_dst", "L1_gnn_bias",
        "L1_gnn_ln_gamma", "L1_gnn_ln_beta"]


def kernel(**inputs):
    import numpy as _np
    import concourse.bacc as _bacc
    from concourse import mybir as _mybir
    from concourse.bass_utils import run_bass_kernel_spmd as _run

    nc = _bacc.Bacc("TRN2", target_bir_lowering=False, num_devices=1)
    arrays, args = {}, []
    for name in _INS:
        a = _np.ascontiguousarray(inputs[name])
        arrays[f"in_{name}_dram"] = a
        args.append(nc.dram_tensor(f"in_{name}_dram", a.shape, _mybir.dt.from_np(a.dtype), kind="ExternalInput").ap())
    shape = inputs["x"].shape
    args.append(nc.dram_tensor("out_0_dram", shape, _mybir.dt.float32, kind="ExternalOutput").ap())
    gnn_two_layers(nc, *args)
    r = _run(nc, [arrays], core_ids=[0])
    return r.results[0]["out_0_dram"]
```
